# Optimizing a Trainium2 kernel written in Bass

```python
import numpy as np
import jax
import jax.numpy as jnp

def _softmax(x, axis=-1):
    return jax.nn.softmax(x, axis=axis)

def _gelu(x):
    return jax.nn.gelu(x, approximate=True)

def _silu(x):
    return jax.nn.silu(x)

def _sigmoid(x):
    return jax.nn.sigmoid(x)

def _layernorm(x, axis=-1, eps=1e-05):
    m = jnp.mean(x, axis=axis, keepdims=True)
    v = jnp.var(x, axis=axis, keepdims=True)
    return (x - m) / jnp.sqrt(v + eps)

def _scatter_add(tgt, idx, src, axis=0):
    return tgt.at[idx].add(src)

def _segment_sum(src, seg, n):
    return jax.ops.segment_sum(src, seg, n)
kernel_name = 'mk_sandwich_d2_jaxref_r8_e1bb50'

def setup_inputs(seed: int=0):
    np.random.seed(seed)
    _w = jnp.asarray

    def _L0_attn_setup():
        import jax, jax.numpy as jnp
        import numpy as np
        N, L, D_IN, H, HD, D_OUT = (4, 256, 128, 16, 64, 128)
        DIM = H * HD
        key = jax.random.key(seed)
        ks = jax.random.split(key, 5)
        s_in = 1.0 / np.sqrt(D_IN)
        s_d = 1.0 / np.sqrt(DIM)
        return {'data': jax.random.normal(ks[0], (N, L, D_IN), jnp.float32), 'W_qkv': jax.random.uniform(ks[1], (D_IN, 3 * DIM), jnp.float32, -s_in, s_in), 'b_qkv': jax.random.uniform(ks[2], (3 * DIM,), jnp.float32, -s_in, s_in), 'W_out': jax.random.uniform(ks[3], (DIM, D_OUT), jnp.float32, -s_d, s_d), 'b_out': jax.random.uniform(ks[4], (D_OUT,), jnp.float32, -s_d, s_d)}
    _L0_attn_in = _L0_attn_setup()

    def _L0_ffn_setup():
        import jax, jax.numpy as jnp
        import numpy as np
        B, S, D, H, M, E, K = (4, 256, 128, 256, 64, 8, 2)

        def _layernorm(x, g, b, eps=1e-05):
            mu = x.mean(-1, keepdims=True)
            var = ((x - mu) ** 2).mean(-1, keepdims=True)
            return (x - mu) * jax.lax.rsqrt(var + eps) * g + b

        def _forward(inputs_embeds, enc_W, enc_b, s2c_W, s2c_b, rW1, rb1, rW2, rb2, We1, be1, We2, be2, c2s_W, c2s_b, dec_W, dec_b, ln_g, ln_b):
            b, s, _ = inputs_embeds.shape
            spikes_enc = jax.nn.sigmoid(inputs_embeds @ enc_W + enc_b)
            flat = spikes_enc.reshape(b * s, H)
            cont = flat @ s2c_W + s2c_b
            logits = jnp.tanh(cont @ rW1 + rb1) @ rW2 + rb2
            probs = jax.nn.softmax(logits, axis=-1)
            topw, topi = jax.lax.top_k(probs, K)
            w = topw / topw.sum(-1, keepdims=True)
            gates = (jax.nn.one_hot(topi, E, dtype=cont.dtype) * w[..., None]).sum(1)
            h = jax.nn.relu(jnp.einsum('nm,emh->enh', cont, We1) + be1[:, None, :])
            expert_out = jnp.einsum('enh,ehm->enm', h, We2) + be2[:, None, :]
            output_flat = jnp.einsum('enm,ne->nm', expert_out, gates)
            spikes_moe = jax.nn.sigmoid(output_flat @ c2s_W + c2s_b).reshape(b, s, H)
            decoded = jax.nn.sigmoid(spikes_moe @ dec_W + dec_b)
            return _layernorm(decoded, ln_g, ln_b)
        key = jax.random.key(seed)
        ks = jax.random.split(key, 10)
        r = lambda k, shape: jax.random.normal(k, shape, dtype=jnp.float32) * 0.02
        return {'inputs_embeds': jax.random.normal(ks[0], (B, S, D), dtype=jnp.float32), 'enc_W': r(ks[1], (D, H)), 'enc_b': jnp.zeros((H,), jnp.float32), 's2c_W': r(ks[2], (H, M)), 's2c_b': jnp.zeros((M,), jnp.float32), 'rW1': r(ks[3], (M, 64)), 'rb1': jnp.zeros((64,), jnp.float32), 'rW2': r(ks[4], (64, E)), 'rb2': jnp.zeros((E,), jnp.float32), 'We1': r(ks[5], (E, M, H // 2)), 'be1': jnp.zeros((E, H // 2), jnp.float32), 'We2': r(ks[6], (E, H // 2, M)), 'be2': jnp.zeros((E, M), jnp.float32), 'c2s_W': r(ks[7], (M, H)), 'c2s_b': jnp.zeros((H,), jnp.float32), 'dec_W': r(ks[8], (H, D)), 'dec_b': jnp.zeros((D,), jnp.float32), 'ln_g': jnp.ones((D,), jnp.float32), 'ln_b': jnp.zeros((D,), jnp.float32)}
    _L0_ffn_in = _L0_ffn_setup()

    def _L1_attn_setup():
        import jax, jax.numpy as jnp
        import numpy as np
        B, N, D, H = (2, 256, 128, 8)
        DH = D // H
        key = jax.random.key(seed)
        k0, k1, k2 = jax.random.split(key, 3)
        s = 1.0 / np.sqrt(D).astype(np.float32)
        return {'x': jax.random.normal(k0, (B, N, D), dtype=jnp.float32), 'w_qkv': jax.random.normal(k1, (3 * D, D), dtype=jnp.float32) * s, 'b_qkv': jnp.zeros((3 * D,), dtype=jnp.float32), 'w_o': jax.random.normal(k2, (D, D), dtype=jnp.float32) * s, 'b_o': jnp.zeros((D,), dtype=jnp.float32)}
    _L1_attn_in = _L1_attn_setup()

    def _L1_ffn_setup():
        import jax, jax.numpy as jnp
        import numpy as np
        B, T, D, H, E, K = (2, 512, 128, 512, 8, 2)
        key = jax.random.key(seed)
        ks = jax.random.split(key, 5)
        scale = 0.02
        x = jax.random.normal(ks[0], (B, T, D), dtype=jnp.float32)
        Wr = jax.random.normal(ks[1], (D, E), dtype=jnp.float32) * scale
        W1 = jax.random.normal(ks[2], (E, D, H), dtype=jnp.float32) * scale
        b1 = jnp.zeros((E, H), dtype=jnp.float32)
        W2 = jax.random.normal(ks[3], (E, H, D), dtype=jnp.float32) * scale
        b2 = jnp.zeros((E, D), dtype=jnp.float32)
        return {'x': x, 'Wr': Wr, 'W1': W1, 'b1': b1, 'W2': W2, 'b2': b2}
    _L1_ffn_in = _L1_ffn_setup()
    _d = {'L0_attn_data': _L0_attn_in['data'], 'L0_attn_W_qkv': _L0_attn_in['W_qkv'], 'L0_attn_b_qkv': _L0_attn_in['b_qkv'], 'L0_attn_W_out': _L0_attn_in['W_out'], 'L0_attn_b_out': _L0_attn_in['b_out'], 'L0_ffn_enc_W': _L0_ffn_in['enc_W'], 'L0_ffn_enc_b': _L0_ffn_in['enc_b'], 'L0_ffn_s2c_W': _L0_ffn_in['s2c_W'], 'L0_ffn_s2c_b': _L0_ffn_in['s2c_b'], 'L0_ffn_rW1': _L0_ffn_in['rW1'], 'L0_ffn_rb1': _L0_ffn_in['rb1'], 'L0_ffn_rW2': _L0_ffn_in['rW2'], 'L0_ffn_rb2': _L0_ffn_in['rb2'], 'L0_ffn_We1': _L0_ffn_in['We1'], 'L0_ffn_be1': _L0_ffn_in['be1'], 'L0_ffn_We2': _L0_ffn_in['We2'], 'L0_ffn_be2': _L0_ffn_in['be2'], 'L0_ffn_c2s_W': _L0_ffn_in['c2s_W'], 'L0_ffn_c2s_b': _L0_ffn_in['c2s_b'], 'L0_ffn_dec_W': _L0_ffn_in['dec_W'], 'L0_ffn_dec_b': _L0_ffn_in['dec_b'], 'L0_ffn_ln_g': _L0_ffn_in['ln_g'], 'L0_ffn_ln_b': _L0_ffn_in['ln_b'], 'L1_attn_w_qkv': _L1_attn_in['w_qkv'], 'L1_attn_b_qkv': _L1_attn_in['b_qkv'], 'L1_attn_w_o': _L1_attn_in['w_o'], 'L1_attn_b_o': _L1_attn_in['b_o'], 'L1_ffn_Wr': _L1_ffn_in['Wr'], 'L1_ffn_W1': _L1_ffn_in['W1'], 'L1_ffn_b1': _L1_ffn_in['b1'], 'L1_ffn_W2': _L1_ffn_in['W2'], 'L1_ffn_b2': _L1_ffn_in['b2']}
    _x0 = _d['L0_attn_data']
    _d['L0_attn_data'] = jax.random.normal(jax.random.fold_in(jax.random.key(seed), 1), (2, 1024, 128), dtype=_x0.dtype)
    del _x0
    return _d

def reference(L0_attn_data, L0_attn_W_qkv, L0_attn_b_qkv, L0_attn_W_out, L0_attn_b_out, L0_ffn_enc_W, L0_ffn_enc_b, L0_ffn_s2c_W, L0_ffn_s2c_b, L0_ffn_rW1, L0_ffn_rb1, L0_ffn_rW2, L0_ffn_rb2, L0_ffn_We1, L0_ffn_be1, L0_ffn_We2, L0_ffn_be2, L0_ffn_c2s_W, L0_ffn_c2s_b, L0_ffn_dec_W, L0_ffn_dec_b, L0_ffn_ln_g, L0_ffn_ln_b, L1_attn_w_qkv, L1_attn_b_qkv, L1_attn_w_o, L1_attn_b_o, L1_ffn_Wr, L1_ffn_W1, L1_ffn_b1, L1_ffn_W2, L1_ffn_b2):

    def _L0_attn_ref(data, W_qkv, b_qkv, W_out, b_out):
        import jax, jax.numpy as jnp
        import numpy as np
        N, L, D_IN, H, HD, D_OUT = (4, 256, 128, 16, 64, 128)
        DIM = H * HD
        n, l = (data.shape[0], data.shape[1])
        qkv = data @ W_qkv + b_qkv
        q = qkv[:, :, :DIM].reshape(n, l, H, HD)
        k = qkv[:, :, DIM:2 * DIM].reshape(n, l, H, HD)
        v = qkv[:, :, 2 * DIM:].reshape(n, l, H, HD)
        scores = jnp.einsum('nqhd,nkhd->nhqk', q, k)
        attention = jax.nn.softmax(scores / jnp.sqrt(jnp.float32(HD)), axis=3)
        out = jnp.einsum('nhql,nlhd->nqhd', attention, v).reshape(n, l, DIM)
        return out @ W_out + b_out

    def _L0_ffn_ref(inputs_embeds, enc_W, enc_b, s2c_W, s2c_b, rW1, rb1, rW2, rb2, We1, be1, We2, be2, c2s_W, c2s_b, dec_W, dec_b, ln_g, ln_b):
        import jax, jax.numpy as jnp
        import numpy as np
        B, S, D, H, M, E, K = (4, 256, 128, 256, 64, 8, 2)

        def _layernorm(x, g, b, eps=1e-05):
            mu = x.mean(-1, keepdims=True)
            var = ((x - mu) ** 2).mean(-1, keepdims=True)
            return (x - mu) * jax.lax.rsqrt(var + eps) * g + b

        def _forward(inputs_embeds, enc_W, enc_b, s2c_W, s2c_b, rW1, rb1, rW2, rb2, We1, be1, We2, be2, c2s_W, c2s_b, dec_W, dec_b, ln_g, ln_b):
            b, s, _ = inputs_embeds.shape
            spikes_enc = jax.nn.sigmoid(inputs_embeds @ enc_W + enc_b)
            flat = spikes_enc.reshape(b * s, H)
            cont = flat @ s2c_W + s2c_b
            logits = jnp.tanh(cont @ rW1 + rb1) @ rW2 + rb2
            probs = jax.nn.softmax(logits, axis=-1)
            topw, topi = jax.lax.top_k(probs, K)
            w = topw / topw.sum(-1, keepdims=True)
            gates = (jax.nn.one_hot(topi, E, dtype=cont.dtype) * w[..., None]).sum(1)
            h = jax.nn.relu(jnp.einsum('nm,emh->enh', cont, We1) + be1[:, None, :])
            expert_out = jnp.einsum('enh,ehm->enm', h, We2) + be2[:, None, :]
            output_flat = jnp.einsum('enm,ne->nm', expert_out, gates)
            spikes_moe = jax.nn.sigmoid(output_flat @ c2s_W + c2s_b).reshape(b, s, H)
            decoded = jax.nn.sigmoid(spikes_moe @ dec_W + dec_b)
            return _layernorm(decoded, ln_g, ln_b)
        return _forward(inputs_embeds, enc_W, enc_b, s2c_W, s2c_b, rW1, rb1, rW2, rb2, We1, be1, We2, be2, c2s_W, c2s_b, dec_W, dec_b, ln_g, ln_b)

    def _L1_attn_ref(x, w_qkv, b_qkv, w_o, b_o):
        import jax, jax.numpy as jnp
        import numpy as np
        B, N, D, H = (2, 256, 128, 8)
        DH = D // H
        b, n, d = x.shape
        h = H
        dh = d // h
        qkv = x @ w_qkv.T + b_qkv
        qkv = qkv.reshape(b, n, 3, dh, h)
        qkv = jnp.transpose(qkv, (2, 0, 4, 1, 3))
        q, k, v = (qkv[0], qkv[1], qkv[2])
        attn = jnp.einsum('bhik,bhjk->bhij', q, k)
        out = jnp.einsum('bhik,bhkj->bhij', attn, v)
        out = jnp.transpose(out, (0, 2, 1, 3)).reshape(b, n, d)
        return out @ w_o.T + b_o

    def _L1_ffn_ref(x, Wr, W1, b1, W2, b2):
        import jax, jax.numpy as jnp
        import numpy as np
        B, T, D, H, E, K = (2, 512, 128, 512, 8, 2)
        logits = jnp.einsum('btd,de->bte', x, Wr)
        probs = jax.nn.softmax(logits, axis=-1)
        w, idx = jax.lax.top_k(probs, K)
        w = w / jnp.sum(w, axis=-1, keepdims=True)
        dispatch = jnp.sum(jax.nn.one_hot(idx, E, dtype=x.dtype) * w[..., None], axis=-2)
        h = jax.nn.gelu(jnp.einsum('btd,edh->ebth', x, W1) + b1[:, None, None, :], approximate=False)
        y = jnp.einsum('ebth,ehd->ebtd', h, W2) + b2[:, None, None, :]
        out = jnp.einsum('ebtd,bte->btd', y, dispatch)
        return out
    x = L0_attn_data
    x = x + _layernorm(_L0_attn_ref(_layernorm(x, axis=-1), L0_attn_W_qkv, L0_attn_b_qkv, L0_attn_W_out, L0_attn_b_out), axis=-1)
    x = x + _layernorm(_L0_ffn_ref(_layernorm(x, axis=-1), L0_ffn_enc_W, L0_ffn_enc_b, L0_ffn_s2c_W, L0_ffn_s2c_b, L0_ffn_rW1, L0_ffn_rb1, L0_ffn_rW2, L0_ffn_rb2, L0_ffn_We1, L0_ffn_be1, L0_ffn_We2, L0_ffn_be2, L0_ffn_c2s_W, L0_ffn_c2s_b, L0_ffn_dec_W, L0_ffn_dec_b, L0_ffn_ln_g, L0_ffn_ln_b), axis=-1)
    x = x + _layernorm(_L1_attn_ref(_layernorm(x, axis=-1), L1_attn_w_qkv, L1_attn_b_qkv, L1_attn_w_o, L1_attn_b_o), axis=-1)
    x = x + _layernorm(_L1_ffn_ref(_layernorm(x, axis=-1), L1_ffn_Wr, L1_ffn_W1, L1_ffn_b1, L1_ffn_W2, L1_ffn_b2), axis=-1)
    return x

_drawn_inputs = setup_inputs


def setup_inputs(seed=0):
    import zlib

    import numpy as np

    out = dict(_drawn_inputs(seed))
    spreads = {'L0_ffn_enc_b': (0.0, 0.8),
     'L0_ffn_s2c_b': (0.0, 0.8),
     'L0_ffn_rb1': (0.0, 0.8),
     'L0_ffn_rb2': (0.0, 0.1),
     'L0_ffn_be1': (0.0, 0.8),
     'L0_ffn_be2': (0.0, 0.37),
     'L0_ffn_c2s_b': (0.0, 0.1),
     'L0_ffn_dec_b': (0.0, 0.1),
     'L0_ffn_ln_g': (1.0, 0.2),
     'L0_ffn_ln_b': (0.0, 0.1),
     'L1_attn_b_qkv': (0.0, 0.1),
     'L1_attn_b_o': (0.0, 0.8),
     'L1_ffn_b1': (0.0, 0.1),
     'L1_ffn_b2': (0.0, 0.1)}
    factors = {'L0_ffn_enc_W': 8.0,
     'L0_ffn_s2c_W': 8.0,
     'L0_ffn_rW1': 8.0,
     'L0_ffn_rW2': 8.0,
     'L0_ffn_We1': 8.0,
     'L0_ffn_We2': 8.0,
     'L0_ffn_c2s_W': 3.754}
    for name, (base, spread) in spreads.items():
        noise = np.random.default_rng([zlib.crc32(name.encode()), seed]).standard_normal(out[name].shape)
        drawn = base * np.exp(spread * noise) if base else spread * noise
        out[name] = jnp.asarray(drawn.astype(out[name].dtype))
    for name, factor in factors.items():
        out[name] = (out[name] * factor).astype(out[name].dtype)
    return out
```

```python
from contextlib import ExitStack

import concourse.bass as bass
from concourse import mybir

F32 = mybir.dt.float32
F32R = mybir.dt.float32r
BF16 = mybir.dt.bfloat16
ALU = mybir.AluOpType
ACT = mybir.ActivationFunctionType
X = mybir.AxisListType.X

P = 128
EPS = 1e-5
BANK = 512
TILES = BANK // P
LEAST = -3.0e38

HEADS, HD = 16, 64
PAIRS = HEADS // 2
RING = 4
PREP_USES = 42
POST_USES = 4
STEP_USES = PREP_USES + POST_USES
PIECES = 8
MAXIMA = {3: range(0, 8), 4: range(8, 16), 5: range(16, 24), 6: range(24, 32)}


class Buffers:
    pass


def wait(eng, sem, value):
    if not (isinstance(value, int) and value <= 0):
        eng.wait_ge(sem, value)


class Chain:

    def __init__(self, eng, sem, before=0):
        self.eng, self.sem, self.before, self.n = eng, sem, before, 0

    def link(self, ins):
        ins.then_inc(self.sem, 1)
        self.n += 1
        self.eng.wait_ge(self.sem, self.before + self.n)


def embed(nc, m, s):
    with ExitStack() as ctx:
        stats = ctx.enter_context(nc.sbuf_tensor("em_stats", [P, TILES, 6], F32))
        mv = ctx.enter_context(nc.sbuf_tensor("em_mv", [P, 4, TILES, 2], F32))
        rstd = ctx.enter_context(nc.sbuf_tensor("em_rstd", [P, 4, TILES], F32))
        xn = ctx.enter_context(nc.sbuf_tensor("em_xn", [P, 4, TILES, P], F32))
        turned = [ctx.enter_context(nc.psum_tensor(f"em_turned{c}", [P, BANK], F32)) for c in range(4)]
        block = ctx.enter_context(nc.Block())

        @block.sync
        def _(sp):
            sp.dma_start(m.b_out[:, :], m.inputs["b_out_row"].unsqueeze(1)).then_inc(s["bias_loaded"], 16)
            for c in range(4):
                n, t0 = c // 2, (c % 2) * TILES
                sp.dma_start(m.x[:, c * TILES:(c + 1) * TILES, :],
                             m.inputs["data"][n].rearrange("(t p) d -> p t d", p=P)[:, t0:t0 + TILES, :]
                             ).then_inc(s["x_loaded"][c], 16)

        @block.gpsimd
        def _(pool):
            nc.gpsimd.memset(m.ident[:, :], 0.0).then_inc(s["ident0"], 1)
            nc.gpsimd.memset(m.ident_bf[:, :], 0.0).then_inc(s["ident0"], 1)
            pool.wait_ge(s["ident0"], 2)
            for d in (m.ident, m.ident_bf):
                nc.gpsimd.affine_select(out=d[:, :], in_=d[:, :], compare_op=ALU.not_equal, fill=1.0, base=0,
                                        pattern=[[-1, P]], channel_multiplier=1).then_inc(s["ident_ready"], 1)

        @block.vector
        def _(dve):
            nc.vector.memset(m.eps[:, :], EPS).then_inc(s["eps_ready"], 1)
            nc.vector.memset(m.ones[:, :], 1.0)
            ch = Chain(dve, s["em_dve"])
            for c in range(4):
                dve.wait_ge(s["x_loaded"][c], 16)
                for t in range(TILES):
                    last = nc.vector.bn_stats(stats[:, t, :], m.x[:, c * TILES + t, :])
                ch.link(last)
                for t in range(TILES):
                    last = nc.vector.bn_aggr(mv[:, c, t, :], stats[:, t, :])
                last.then_inc(s["em_var"], 1)
                dve.wait_ge(s["em_sqrt"], c + 1)
                ch.link(nc.vector.reciprocal(rstd[:, c, :], rstd[:, c, :]))
                for t in range(TILES):
                    last = nc.vector.tensor_scalar(xn[:, c, t, :], m.x[:, c * TILES + t, :], mv[:, c, t, 0:1],
                                                   rstd[:, c, t:t + 1], ALU.subtract, ALU.mult)
                last.then_inc(s["em_xn"], 1)
            for c in range(4):
                dve.wait_ge(s["em_hi"], c + 1)
                cols = slice(c * BANK, (c + 1) * BANK)
                nc.vector.tensor_tensor(m.xT_lo[:, cols], m.xT[:, cols], m.xT_hi[:, cols].bitcast(F32),
                                        ALU.subtract).then_inc(s["em_lo"], 1)

        @block.scalar
        def _(act):
            act.wait_ge(s["eps_ready"], 1)
            for c in range(4):
                act.wait_ge(s["em_var"], c + 1)
                nc.scalar.activation(rstd[:, c, :], mv[:, c, :, 1], ACT.Sqrt,
                                     bias=m.eps[:, 0:1]).then_inc(s["em_sqrt"], 1)
            for c in range(4):
                act.wait_ge(s["em_turned"], c + 1)
                cols = slice(c * BANK, (c + 1) * BANK)
                nc.scalar.copy(m.xT[:, cols], turned[c][:, :])
                nc.scalar.copy(m.xT_hi[:, cols], turned[c][:, :]).then_inc(s["em_hi"], 1)

        @block.tensor
        def _(pe):
            pe.wait_ge(s["ident_ready"], 2)
            for c in range(4):
                pe.wait_ge(s["em_xn"], c + 1)
                for t in range(TILES):
                    last = nc.tensor.transpose(turned[c][:, t * P:(t + 1) * P], xn[:, c, t, :], m.ident[:, :])
                last.then_inc(s["em_turned"], 1)


def attention(nc, m, s):
    with ExitStack() as ctx:
        def sb(name, shape, dt=F32):
            return ctx.enter_context(nc.sbuf_tensor(name, shape, dt))

        w_raw = sb("w_raw", [P, 2, P])
        w_hi = sb("w_hi", [P, 2, P], F32R)
        w_lo = sb("w_lo", [P, 2, P], F32R)
        w_v = sb("w_v", [P, P])
        w_out = sb("w_out", [P, P])
        b_qk = sb("b_qk", [P, 2])
        b_v = sb("b_v", [P, P])
        q_both = [[sb(f"q_both{b}{h}", [P, 1024], F32R) for h in range(2)] for b in range(2)]
        q_shift = [[sb(f"q_shift{b}{h}", [P, 1024], F32R) for h in range(2)] for b in range(2)]
        k_hi = [[sb(f"k_hi{b}{h}", [P, 1024], F32R) for h in range(2)] for b in range(2)]
        k_lo = [[sb(f"k_lo{b}{h}", [P, 1024], F32R) for h in range(2)] for b in range(2)]
        v = [sb(f"v{b}", [P, 8, P]) for b in range(2)]
        probs = [sb(f"probs{h}", [P, RING, 1024]) for h in range(2)]
        key_sum = [[sb(f"key_sum{b}{h}", [P, 1024]) for h in range(2)] for b in range(2)]
        maxima = sb("maxima", [P, 2, 8, 2])
        neg_max = sb("neg_max", [P, 2, 8], BF16)
        raw_out = sb("raw_out", [P, 1024])
        row_sum = sb("row_sum", [P, 1024])
        sum_cols = sb("sum_cols", [P, 2, 8])
        inv_cols = sb("inv_cols", [P, 2, 8])
        inv_sum = sb("inv_sum", [P, 1024])
        inv_dram = nc.dram_tensor("inv_sums", [2, 2, 1024], F32, kind="Internal").ap()
        heads_out = sb("heads_out", [P, 1024])

        scores = [ctx.enter_context(nc.psum_tensor(f"scores{h}", [P, 1024], F32)) for h in range(2)]
        pv = ctx.enter_context(nc.psum_tensor("pv", [P, 1024], F32))
        shared = [ctx.enter_context(nc.psum_tensor(f"shared{b}", [P, BANK], F32)) for b in range(2)]

        HALF = [slice(0, HD), slice(HD, P)]
        OTHER = [HALF[1], HALF[0]]
        SHIFT_ROW = [HD, 0]
        C = [slice(0, BANK), slice(BANK, 2 * BANK)]

        def order_of_uses(prev, nxt):
            order = []
            if nxt:
                order += [("q", 0), ("q", 1), ("k", 0), ("k", 1), ("v", 0), ("v", 1)]
            if prev:
                order += [("sum", 0), ("sum", 1)]
            if nxt:
                order += [("max", i) for slot in (3, 4, 5) for i in MAXIMA[slot]] + [("row0", 0), ("row0", 1)]
                order += [("max", i) for i in MAXIMA[6]]
            if prev:
                order += [("proj", 0), ("proj", 1)]
            if nxt:
                order += [("row1", 0), ("row1", 1)]
            return {name: k for k, name in enumerate(order)}

        class Uses:

            def __init__(self, before, prev=True, nxt=True):
                self.before, self.at = before, order_of_uses(prev, nxt)

            def bank(self, *name):
                return self.at[name] % 2

            def earlier(self, *name):
                return self.before + self.at[name] // 2

        PREP, POST = PREP_USES // 2, POST_USES // 2
        prologue = Uses(0, prev=False)

        def uses_in(p, n, first=False, last=False):
            if first:
                return Uses(PREP, prev=False)
            return Uses(2 * PREP + (p * 2 + n - 1) * (PREP + POST), nxt=not last)

        epilogue = Uses(2 * PREP + (2 * PAIRS - 2) * (PREP + POST) + POST, nxt=False)

        W = m.inputs["W_qkv"].rearrange("d (c n) -> d c n", c=3)
        B = m.inputs["b_qkv"].rearrange("(c n) -> n c", c=3)

        block = ctx.enter_context(nc.Block())

        @block.sync
        def _(sp):
            def load_pair(p):
                cols = bass.ts(p, P)
                sp.dma_start(w_raw[:, :, :], W[:, 0:2, cols]).then_inc(s["pair_loaded"], 16)
                sp.dma_start(w_v[:, :], W[:, 2, cols]).then_inc(s["pair_loaded"], 16)
                sp.dma_start(b_qk[:, :], B[cols, 0:2]).then_inc(s["pair_loaded"], 16)
                sp.dma_start(b_v[:, :], m.inputs["b_qkv"][bass.ds(p * P + 2 * HEADS * HD, P)].partition_broadcast(P)
                             ).then_inc(s["pair_loaded"], 16)

            def next_pair(p, first=False):
                u = uses_in(p, 0, first=first)
                sp.wait_ge(s["shared_free"][u.bank("v", 1)], u.earlier("v", 1) + 1)
                load_pair(p + 1)

            def out_weights(p, first=False):
                if not first:
                    u = uses_in(p, 0)
                    sp.wait_ge(s["shared_free"][u.bank("proj", 1)], u.earlier("proj", 1) + 1)
                sp.dma_start(w_out[:, :], m.inputs["W_out"][bass.ts(p, P), :]).then_inc(s["w_out_loaded"], 16)

            def invert(p, n, u):
                st = p * 2 + n
                for c in range(2):
                    sp.wait_ge(s["shared_free"][u.bank("sum", c)], u.earlier("sum", c) + 1)
                for h in range(2):
                    sp.dma_start(sum_cols[:, h, :], row_sum[h * HD:h * HD + 1, :].rearrange("o (p j) -> o p j", j=8)
                                 ).then_inc(s["sum_cols_ready"], 16)
                sp.wait_ge(s["inverted"], st + 1)
                sp.dma_start(inv_dram[n].rearrange("h (p j) -> p h j", j=8), inv_cols[:, :, :]
                             ).then_inc(s["inv_stored"], 16)
                sp.wait_ge(s["inv_stored"], st * 16 + 16)
                wait(sp, s["normalised"], st)
                for h in range(2):
                    sp.dma_start(inv_sum[HALF[h], :], inv_dram[n, h].partition_broadcast(HD)
                                 ).then_inc(s["inv_sum_ready"], 16)

            load_pair(0)
            out_weights(0, first=True)
            next_pair(0, first=True)
            invert(0, 0, uses_in(0, 1))
            with sp.Fori(1, PAIRS - 1) as p:
                next_pair(p)
                invert(p - 1, 1, uses_in(p, 0))
                out_weights(p)
                invert(p, 0, uses_in(p, 1))
            invert(PAIRS - 2, 1, uses_in(PAIRS - 1, 0))
            out_weights(PAIRS - 1)
            invert(PAIRS - 1, 0, uses_in(PAIRS - 1, 1, last=True))
            invert(PAIRS - 1, 1, epilogue)

        @block.tensor
        def _(pe):
            def take(u, *name):
                wait(pe, s["shared_free"][u.bank(*name)], u.earlier(*name))
                return shared[u.bank(*name)]

            def read(u, *name):
                pe.wait_ge(s["shared_free"][u.bank(*name)], u.earlier(*name) + 1)

            def project_qk(u, what, c, p, n):
                j = "qk".index(what)
                pe.wait_ge(s["w_split"], p + 1)
                out = take(u, what, c)
                cols = slice(n * 1024 + c * BANK, n * 1024 + (c + 1) * BANK)
                nc.tensor.matmul(out[:, :], w_hi[:, j, :], m.xT_hi[:, cols], start=True, stop=False)
                nc.tensor.matmul(out[:, :], w_hi[:, j, :], m.xT_lo[:, cols], start=False, stop=False)
                nc.tensor.matmul(out[:, :], w_lo[:, j, :], m.xT_hi[:, cols], start=False, stop=True
                                 ).then_inc(s["shared_full"][u.bank(what, c)], 1)

            def project_v(u, j, n):
                out = take(u, "v", j)
                for t in range(TILES):
                    tok = n * 1024 + (j * TILES + t) * P
                    last = nc.tensor.matmul(out[:, t * P:(t + 1) * P], m.xT[:, tok:tok + P], w_v[:, :],
                                            start=True, stop=True)
                last.then_inc(s["shared_full"][u.bank("v", j)], 1)

            def find_maxima(u, slot, place, n):
                if slot not in MAXIMA:
                    return
                if slot == 3 and place == 0:
                    for c in range(2):
                        read(u, "k", c)
                i = MAXIMA[slot][place]
                h, qt, kc = i // 16, i % 16 // 2, i % 2
                out = take(u, "max", i)
                nc.tensor.matmul(out[:, :], q_both[n][h][:, qt * P:(qt + 1) * P], k_hi[n][h][:, C[kc]],
                                 start=True, stop=True).then_inc(s["shared_full"][u.bank("max", i)], 1)

            def shift_row(u, h, p, n):
                pe.wait_ge(s["neg_max_ready"], (p * 2 + n) * 2 + h + 1)
                r = SHIFT_ROW[h]
                for c in range(2):
                    out = take(u, f"row{h}", c)
                    for t in range(TILES):
                        j = c * TILES + t
                        last = nc.tensor.matmul(out[r:r + 1, t * P:(t + 1) * P], neg_max[:, h, j:j + 1],
                                                m.ident_bf[:, :], start=True, stop=True)
                    last.then_inc(s["shared_full"][u.bank(f"row{h}", c)], 1)

            def score(p, n, kt, h, prepared, between):
                if kt == 0:
                    for c in range(2):
                        read(prepared, f"row{h}", c)
                wait(pe, s["exp_done"][h], (p * 2 + n) * 8 + kt)
                for part, (w, q, start) in enumerate(((k_hi, q_both, True), (k_lo, q_shift, False))):
                    for c in range(2):
                        last = nc.tensor.matmul(scores[h][:, C[c]], w[n][h][:, kt * P:(kt + 1) * P],
                                                q[n][h][:, C[c]], start=start, stop=not start)
                    if part == 1:
                        last.then_inc(s["scores_ready"][h], 1)
                    between(h * 2 + part)

            def weigh(p, n, kt, between):
                for h in range(2):
                    pe.wait_ge(s["exp_done"][h], (p * 2 + n) * 8 + kt + 1)
                if kt == 0:
                    wait(pe, s["raw_out_ready"], p * 2 + n)
                for c in range(2):
                    for h in range(2):
                        last = nc.tensor.matmul(pv[HALF[h], C[c]], v[n][:, kt, HALF[h]],
                                                probs[h][:, kt % RING, C[c]], start=kt == 0, stop=kt == 7)
                    if c == 1:
                        last.then_inc(s["weighed"], 1)
                    between(4 + 2 * c)
                    between(5 + 2 * c)

            def sum_rows(u, p, n):
                for h in range(2):
                    pe.wait_ge(s["keys_added"][h], (p * 2 + n + 1) * 7)
                for c in range(2):
                    out = take(u, "sum", c)
                    for h in range(2):
                        last = nc.tensor.matmul(out[HALF[h], :], m.ones[:, HALF[h]], key_sum[n][h][:, C[c]],
                                                start=True, stop=True)
                    last.then_inc(s["shared_full"][u.bank("sum", c)], 1)

            def project_out(u, p, n):
                pe.wait_ge(s["w_out_loaded"], p * 16 + 16)
                pe.wait_ge(s["normalised"], p * 2 + n + 1)
                for c in range(2):
                    out = take(u, "proj", c)
                    nc.tensor.matmul(out[:, :], w_out[:, :], heads_out[:, C[c]], start=True, stop=True
                                     ).then_inc(s["shared_full"][u.bank("proj", c)], 1)

            def step(p, n, prepared, first=False, last=False):
                u = uses_in(p, n, first, last)
                before, after = (p - 1 + n, 1 - n), (p + n, 1 - n)
                for kt in range(8):
                    def between(place):
                        if not last:
                            find_maxima(u, kt, place, after[1])

                    if kt == 6 and not last:
                        shift_row(u, 0, *after)
                    score(p, n, kt, 0, prepared, between)
                    if kt < 2 and not last:
                        project_qk(u, "qk"[kt], 0, *after)
                    if kt == 2 and not last:
                        project_v(u, 0, after[1])
                    score(p, n, kt, 1, prepared, between)
                    if kt == 2 and not last:
                        project_v(u, 1, after[1])
                    if kt > 0:
                        weigh(p, n, kt - 1, between)
                    elif not first:
                        weigh(*before, 7, between)
                    if kt < 2 and not last:
                        project_qk(u, "qk"[kt], 1, *after)
                    if kt == 2 and not first:
                        sum_rows(u, *before)
                    if kt == 7 and not first:
                        project_out(u, *before)
                    if kt == 7 and not last:
                        shift_row(u, 1, *after)
                return u

            pe.wait_ge(s["filled"], 1)
            for what in "qk":
                for c in range(2):
                    project_qk(prologue, what, c, 0, 0)
            for j in range(2):
                project_v(prologue, j, 0)
            for slot in MAXIMA:
                if slot == 6:
                    shift_row(prologue, 0, 0, 0)
                for place in range(PIECES):
                    find_maxima(prologue, slot, place, 0)
            shift_row(prologue, 1, 0, 0)
            u = step(0, 0, prologue, first=True)
            step(0, 1, u)
            with pe.Fori(1, PAIRS - 1) as p:
                u = step(p, 0, uses_in(p - 1, 1))
                step(p, 1, u)
            u = step(PAIRS - 1, 0, uses_in(PAIRS - 2, 1))
            step(PAIRS - 1, 1, u, last=True)
            weigh(PAIRS - 1, 1, 7, lambda place: None)
            sum_rows(epilogue, PAIRS - 1, 1)
            project_out(epilogue, PAIRS - 1, 1)

        @block.scalar
        def _(act):
            def got(u, *name):
                act.wait_ge(s["shared_full"][u.bank(*name)], u.earlier(*name) + 1)
                return shared[u.bank(*name)]

            def leading(u, what, n):
                j = "qk".index(what)
                if what == "q":
                    places = [(q_both[n][0], 0, 0), (q_shift[n][0], 0, 0), (q_both[n][1], 1, 1), (q_shift[n][1], 1, 1)]
                else:
                    places = [(k_hi[n][0], 0, 0), (k_hi[n][0], 1, 0), (k_hi[n][1], 0, 1), (k_hi[n][1], 1, 1)]
                for c in range(2):
                    ps = got(u, what, c)
                    for to, half, h in places:
                        last = nc.scalar.activation(to[HALF[half], C[c]], ps[HALF[h], :], ACT.Identity,
                                                    bias=b_qk[HALF[h], j:j + 1])
                    last.then_inc(s["leading_ready"], 1)

            def shift_rows(u, h, n):
                r = SHIFT_ROW[h]
                for c in range(2):
                    ps = got(u, f"row{h}", c)
                    nc.scalar.copy(q_shift[n][h][r:r + 1, C[c]], ps[r:r + 1, :]
                                   ).then_inc(s["shared_free"][u.bank(f"row{h}", c)], 1)

            def fetch_sums(u, p, n):
                wait(act, s["sum_cols_ready"], (p * 2 + n) * 32)
                for c in range(2):
                    ps = got(u, "sum", c)
                    nc.scalar.copy(row_sum[:, C[c]], ps[:, :]).then_inc(s["shared_free"][u.bank("sum", c)], 1)

            def exponentials(p, n, kt, first):
                st = p * 2 + n
                for h in range(2):
                    act.wait_ge(s["scores_ready"][h], st * 8 + kt + 1)
                    if kt >= RING or not first:
                        act.wait_ge(s["weighed"], st * 8 + kt - RING + 1)
                        act.wait_ge(s["keys_added"][h], st * 7 + (max(kt - RING, 1) if kt >= RING else kt + RING - 7))
                    nc.scalar.activation(probs[h][:, kt % RING, :], scores[h][:, :], ACT.Exp,
                                         scale=HD ** -0.5).then_inc(s["exp_done"][h], 1)

            def fetch_out(p, n):
                st = p * 2 + n
                act.wait_ge(s["weighed"], st * 8 + 8)
                wait(act, s["normalised"], st)
                nc.scalar.copy(raw_out[:, :], pv[:, :]).then_inc(s["raw_out_ready"], 1)

            def step(p, n, first=False, last=False):
                u = uses_in(p, n, first, last)
                for kt in range(8):
                    if kt == 6 and not last:
                        shift_rows(u, 0, 1 - n)
                    exponentials(p, n, kt, first)
                    if kt == 0 and not first:
                        fetch_out(p - 1 + n, 1 - n)
                    if kt == 2 and not first:
                        fetch_sums(u, p - 1 + n, 1 - n)
                    if last:
                        continue
                    if kt == 0:
                        leading(u, "q", 1 - n)
                    if kt == 1:
                        leading(u, "k", 1 - n)
                    if kt == 7:
                        shift_rows(u, 1, 1 - n)

            act.wait_ge(s["filled"], 1)
            leading(prologue, "q", 0)
            leading(prologue, "k", 0)
            shift_rows(prologue, 0, 0)
            shift_rows(prologue, 1, 0)
            step(0, 0, first=True)
            step(0, 1)
            with act.Fori(1, PAIRS - 1) as p:
                step(p, 0)
                step(p, 1)
            step(PAIRS - 1, 0)
            step(PAIRS - 1, 1, last=True)
            fetch_out(PAIRS - 1, 1)
            fetch_sums(epilogue, PAIRS - 1, 1)

        @block.vector
        def _(dve):
            def got(u, *name):
                dve.wait_ge(s["shared_full"][u.bank(*name)], u.earlier(*name) + 1)
                return shared[u.bank(*name)]

            def done(u, *name):
                dve.wait_ge(s["shared_free"][u.bank(*name)], u.earlier(*name) + 1)

            def remainders(u, what, p, n):
                j = "qk".index(what)
                for c in range(2):
                    ps = got(u, what, c)
                    dve.wait_ge(s["leading_ready"], (p * 2 + n) * 4 + 2 * j + c + 1)
                    for h in range(2):
                        lead = (q_both if what == "q" else k_hi)[n][h][HALF[h], C[c]]
                        to = q_both[n][h][OTHER[h], C[c]] if what == "q" else k_lo[n][h][HALF[h], C[c]]
                        last = nc.vector.scalar_tensor_tensor(out=to, in0=ps[HALF[h], :], scalar=b_qk[HALF[h], j:j + 1],
                                                              in1=lead.bitcast(F32), op0=ALU.add, op1=ALU.subtract)
                    last.then_inc(s["shared_free"][u.bank(what, c)], 1)

            def values(u, n):
                bias = b_v[:, :].unsqueeze(1).broadcast_to([P, TILES, P])
                for j in range(2):
                    ps = got(u, "v", j)
                    nc.vector.tensor_tensor(v[n][:, j * TILES:(j + 1) * TILES, :],
                                            ps[:, :].rearrange("p (t d) -> p t d", t=TILES), bias, ALU.add
                                            ).then_inc(s["shared_free"][u.bank("v", j)], 1)

            def find_maxima(u, slot):
                for i in MAXIMA[slot]:
                    h, qt, kc = i // 16, i % 16 // 2, i % 2
                    ps = got(u, "max", i)
                    nc.vector.tensor_reduce(maxima[:, h, qt, kc:kc + 1], ps[:, :], X, ALU.max
                                            ).then_inc(s["shared_free"][u.bank("max", i)], 1)
                    if i % 16 == 15:
                        done(u, "max", i - 1)
                        done(u, "max", i)
                        nc.vector.tensor_reduce(neg_max[:, h, :], maxima[:, h, :, :], X, ALU.max, negate=True
                                                ).then_inc(s["neg_max_ready"], 1)

            def invert(p, n):
                st = p * 2 + n
                dve.wait_ge(s["sum_cols_ready"], st * 32 + 32)
                wait(dve, s["inv_stored"], st * 16)
                nc.vector.reciprocal(inv_cols[:, :, :], sum_cols[:, :, :]).then_inc(s["inverted"], 1)

            def normalise(p, n):
                st = p * 2 + n
                dve.wait_ge(s["inv_sum_ready"], st * 32 + 32)
                dve.wait_ge(s["raw_out_ready"], st + 1)
                nc.vector.tensor_tensor(heads_out[:, :], raw_out[:, :], inv_sum[:, :], ALU.mult
                                        ).then_inc(s["normalised"], 1)

            def add_projection(u, n):
                for c in range(2):
                    ps = got(u, "proj", c)
                    y = m.yT[:, n * 1024 + c * BANK:n * 1024 + (c + 1) * BANK]
                    nc.vector.tensor_tensor(y, ps[:, :], y, ALU.add).then_inc(s["shared_free"][u.bank("proj", c)], 1)

            def split_weights(p):
                dve.wait_ge(s["pair_loaded"], p * 64 + 64)
                nc.vector.tensor_copy(w_hi[:, :, :], w_raw[:, :, :]).then_inc(s["w_hi_ready"], 1)
                dve.wait_ge(s["w_hi_ready"], p + 1)
                nc.vector.tensor_tensor(w_lo[:, :, :], w_raw[:, :, :], w_hi[:, :, :].bitcast(F32), ALU.subtract
                                        ).then_inc(s["w_split"], 1)

            def step(p, n, first=False, last=False):
                u = uses_in(p, n, first, last)
                before, after = (p - 1 + n, 1 - n), (p + n, 1 - n)
                for kt in range(8):
                    if kt == 4 and not first:
                        invert(*before)
                    if kt in MAXIMA and not last:
                        find_maxima(u, kt)
                    if kt == 6 and not first:
                        normalise(*before)
                    if kt == 7 and not first:
                        add_projection(u, before[1])
                    if last:
                        continue
                    if kt == 0:
                        remainders(u, "q", *after)
                    if kt == 1:
                        remainders(u, "k", *after)
                    if kt == 2:
                        values(u, after[1])
                    if kt == 7 and n == 0 and not (isinstance(p, int) and p == PAIRS - 1):
                        split_weights(p + 1)

            split_weights(0)
            dve.wait_ge(s["bias_loaded"], 16)
            nc.vector.memset(m.yT[:, :], 0.0).then_inc(s["yT_clear"], 1)
            dve.wait_ge(s["yT_clear"], 1)
            nc.vector.tensor_scalar(m.yT[:, :], m.yT[:, :], m.b_out[:, 0:1], None, ALU.add)
            remainders(prologue, "q", 0, 0)
            remainders(prologue, "k", 0, 0)
            values(prologue, 0)
            for slot in MAXIMA:
                find_maxima(prologue, slot)
            step(0, 0, first=True)
            step(0, 1)
            with dve.Fori(1, PAIRS - 1) as p:
                step(p, 0)
                step(p, 1)
            step(PAIRS - 1, 0)
            step(PAIRS - 1, 1, last=True)
            invert(PAIRS - 1, 1)
            normalise(PAIRS - 1, 1)
            add_projection(epilogue, 1)

        @block.gpsimd
        def _(pool):
            for b in range(2):
                nc.gpsimd.memset(q_shift[b][0][OTHER[0], :].bitcast(F32), 0.0)
                nc.gpsimd.memset(q_shift[b][1][OTHER[1], :].bitcast(F32), 0.0)
                nc.gpsimd.memset(k_lo[b][0][OTHER[0], :].bitcast(F32), 0.0)
                last = nc.gpsimd.memset(k_lo[b][1][OTHER[1], :].bitcast(F32), 0.0)
            last.then_inc(s["cleared"], 1)
            pool.wait_ge(s["cleared"], 1)
            for b in range(2):
                for h in range(2):
                    r = SHIFT_ROW[h]
                    last = nc.gpsimd.memset(k_lo[b][h][r:r + 1, :].bitcast(F32), 1.0)
            last.then_inc(s["filled"], 1)

            def step(p, n, first=False):
                st = p * 2 + n
                for kt in range(1, 8):
                    for h in range(2):
                        pool.wait_ge(s["exp_done"][h], st * 8 + kt + 1)
                        if kt == 1:
                            if not (first or (isinstance(p, int) and p == 0)):
                                pool.wait_ge(s["normalised"], st - 1)
                            a = probs[h][:, 0, :]
                        else:
                            pool.wait_ge(s["keys_added"][h], st * 7 + kt - 1)
                            a = key_sum[n][h][:, :]
                        nc.gpsimd.tensor_tensor(key_sum[n][h][:, :], a, probs[h][:, kt % RING, :], ALU.add
                                                ).then_inc(s["keys_added"][h], 1)

            step(0, 0, first=True)
            step(0, 1)
            with pool.Fori(1, PAIRS) as p:
                step(p, 0)
                step(p, 1)


class Norms:

    def __init__(self, nc, chain, carrier, var_ready, root_ready, eps, stats, mv, rstd, i, each):
        self.nc, self.chain, self.var_ready, self.root_ready, self.eps = nc, chain, var_ready, root_ready, eps
        self.carrier = carrier
        self.stats, self.mv, self.rstd, self.done = stats, mv, rstd, i * each

    def norm(self, src, out):
        nc, dve = self.nc, self.chain.eng
        nc.vector.memset(self.carrier[:, :], 0.0)
        for t in range(TILES):
            last = nc.vector.bn_stats(self.stats[:, t, :], src[:, t, :])
        self.chain.link(last)
        nc.vector.memset(self.carrier[:, :], 0.0)
        for t in range(TILES):
            last = nc.vector.bn_aggr(self.mv[:, t, :], self.stats[:, t, :])
        last.then_inc(self.var_ready, 1)
        self.done = self.done + 1
        dve.wait_ge(self.root_ready, self.done)
        self.chain.link(nc.vector.reciprocal(self.rstd[:, :], self.rstd[:, :]))
        for t in range(TILES):
            last = nc.vector.tensor_scalar(out[:, t, :], src[:, t, :], self.mv[:, t, 0:1], self.rstd[:, t:t + 1],
                                           ALU.subtract, ALU.mult)
        return last

    def root(self, act):
        self.done = self.done + 1
        act.wait_ge(self.var_ready, self.done)
        self.nc.scalar.activation(self.rstd[:, :], self.mv[:, :, 1], ACT.Sqrt, bias=self.eps[:, 0:1]
                                  ).then_inc(self.root_ready, 1)


EXPERTS = 8
GATE_LINKS = 14


def pick_two(nc, ch, t, logits, bias, rank, weights_wanted, weights_ready, value):
    dve = ch.eng
    shape = [P, TILES, EXPERTS]

    def wide(a):
        return a[:, :].unsqueeze(2).broadcast_to(shape)

    ranks = rank[:, :].unsqueeze(1).broadcast_to(shape)
    if bias is None:
        ch.link(nc.vector.tensor_copy(t.logit[:, :, :], logits))
    else:
        ch.link(nc.vector.tensor_tensor(t.logit[:, :, :], logits, bias[:, :].unsqueeze(1).broadcast_to(shape), ALU.add))

    def choose(values, best, chosen):
        ch.link(nc.vector.tensor_reduce(best[:, :], values, X, ALU.max))
        ch.link(nc.vector.tensor_tensor(t.score[:, :, :], values, wide(best), ALU.is_equal))
        ch.link(nc.vector.tensor_tensor(t.score[:, :, :], t.score[:, :, :], ranks, ALU.mult))
        ch.link(nc.vector.tensor_reduce(t.first[:, :], t.score[:, :, :], X, ALU.max))
        ch.link(nc.vector.tensor_tensor(chosen[:, :, :], t.score[:, :, :], wide(t.first), ALU.is_equal))

    choose(t.logit[:, :, :], t.best1, t.chosen1)
    ch.link(nc.vector.scalar_tensor_tensor(out=t.rest[:, :, :], in0=t.chosen1[:, :, :], scalar=LEAST,
                                           in1=t.logit[:, :, :], op0=ALU.mult, op1=ALU.add))
    choose(t.rest[:, :, :], t.best2, t.chosen2)
    nc.vector.tensor_tensor(t.gap[:, :], t.best1[:, :], t.best2[:, :], ALU.subtract).then_inc(weights_wanted, 1)
    dve.wait_ge(weights_ready, value)
    ch.link(nc.vector.tensor_tensor(t.chosen1[:, :, :], t.chosen1[:, :, :], wide(t.weight1), ALU.mult))
    ch.link(nc.vector.tensor_tensor(t.chosen2[:, :, :], t.chosen2[:, :, :], wide(t.weight2), ALU.mult))
    return nc.vector.tensor_tensor(t.gates[:, :, :], t.chosen1[:, :, :], t.chosen2[:, :, :], ALU.add)


def weigh_two(nc, act, t, weights_wanted, weights_ready, value):
    act.wait_ge(weights_wanted, value)
    nc.scalar.activation(t.weight1[:, :], t.gap[:, :], ACT.Sigmoid)
    nc.scalar.activation(t.weight2[:, :], t.gap[:, :], ACT.Sigmoid, scale=-1.0).then_inc(weights_ready, 1)


def gating_buffers(sb, name):
    g = Buffers()
    g.logit, g.score, g.rest, g.chosen1, g.chosen2, g.gates = (
        sb(f"{name}_{what}", [P, TILES, EXPERTS]) for what in ("logit", "score", "rest", "chosen1", "chosen2", "gates"))
    g.best1, g.best2, g.first, g.gap, g.weight1, g.weight2 = (
        sb(f"{name}_{what}", [P, TILES]) for what in ("best1", "best2", "first", "gap", "weight1", "weight2"))
    return g


M0, H0 = 64, 256
NORMS0 = 5
LINKS0 = NORMS0 * 2 + GATE_LINKS + (EXPERTS - 2) + 7


def ffn0(nc, m, s):
    with ExitStack() as ctx:
        def sb(name, shape, dt=F32):
            return ctx.enter_context(nc.sbuf_tensor(name, shape, dt))

        enc_raw, enc_hi, enc_lo = sb("enc_raw", [P, H0]), sb("enc_hi", [P, H0], F32R), sb("enc_lo", [P, H0], F32R)
        s2c = sb("s2c", [P, 2, M0])
        r1_raw, r1_hi, r1_lo = sb("r1_raw", [P, M0]), sb("r1_hi", [P, M0], F32R), sb("r1_lo", [P, M0], F32R)
        e1_raw = sb("e1_raw", [P, EXPERTS, P])
        e1_hi, e1_lo = sb("e1_hi", [P, EXPERTS, P], F32R), sb("e1_lo", [P, EXPERTS, P], F32R)
        r2 = sb("r2", [M0, EXPERTS])
        e2 = sb("e2", [P, EXPERTS, M0])
        e2_bias = sb("e2_bias", [EXPERTS, M0])
        c2s = sb("c2s", [M0, H0])
        dec = sb("dec", [P, 2, P])
        enc_b, c2s_b = sb("enc_b", [P, 2]), sb("c2s_b", [P, 2])
        s2c_b, r1_b = sb("s2c_b", [M0, 1]), sb("r1_b", [M0, 1])
        e1_b = sb("e1_b", [P, EXPERTS])
        r2_b = sb("r2_b", [P, EXPERTS])
        dec_b, ln_g, ln_b = sb("dec_b", [P, P]), sb("ln_g", [P, P]), sb("ln_b", [P, P])
        qkv_raw, qkv_T = sb("qkv_raw", [P, 3, P]), sb("qkv_T", [P, 3, P])
        q_b, kv_b = sb("q_b", [P, 1]), sb("kv_b", [P, 2 * P])

        yT = sb("yT_chunk", [P, BANK])
        post = sb("post", [P, TILES, P])
        xn = sb("xn", [P, TILES, P])
        xT_hi, xT_lo = sb("xT_hi_chunk", [P, BANK], F32R), sb("xT_lo_chunk", [P, BANK], F32R)
        spikes = sb("spikes", [P, 2, BANK])
        cont = sb("cont", [P, BANK], F32R)
        router = sb("router", [M0, BANK])
        hidden = [sb(f"hidden{b}", [P, BANK]) for b in range(2)]
        part = sb("part", [P, TILES, M0])
        mixed = sb("mixed", [P, TILES, M0])
        gates_T = sb("gates_T", [EXPERTS, BANK])
        moe = sb("moe", [M0, BANK])
        decoded = sb("decoded", [P, TILES, P])
        xT2 = sb("xT2", [P, BANK])
        stats, mv, rstd = sb("stats0", [P, TILES, 6]), sb("mv0", [P, TILES, 2]), sb("rstd0", [P, TILES])
        g = gating_buffers(sb, "g0")

        def pb(name, shape):
            return ctx.enter_context(nc.psum_tensor(name, shape, F32))

        turned = pb("turned", [P, BANK])
        wide = pb("wide", [P, 2, BANK])
        narrow = pb("narrow", [P, BANK])
        small = pb("small", [P, BANK])
        hid = [pb(f"hid{b}", [P, BANK]) for b in range(2)]
        eout = pb("eout", [P, BANK])
        turned_t = turned[:, :].rearrange("p (t d) -> p t d", t=TILES)
        eout_t = eout[:, 0:TILES * M0].rearrange("p (t d) -> p t d", t=TILES)
        logits = small[:, 0:TILES * EXPERTS].rearrange("p (t e) -> p t e", t=TILES)

        block = ctx.enter_context(nc.Block())
        CHUNKS = 4

        @block.sync
        def _(sp):
            def load(dst, src):
                sp.dma_start(dst, src).then_inc(s["f0_loaded"], 16)

            load(enc_raw[:, :], m.inputs["enc_W"])
            load(s2c[:, :, :], m.inputs["s2c_W"].rearrange("(c p) n -> p c n", p=P))
            for half in range(2):
                rows = slice(half * M0, (half + 1) * M0)
                load(r1_raw[rows, :], m.inputs["rW1"])
                load(e1_raw[rows, :, :], m.inputs["We1"].rearrange("e m h -> m e h"))
            load(r2[:, :], m.inputs["rW2"])
            load(e2[:, :, :], m.inputs["We2"].rearrange("e h m -> h e m"))
            load(e2_bias[:, :], m.inputs["be2"])
            load(c2s[:, :], m.inputs["c2s_W"])
            load(dec[:, :, :], m.inputs["dec_W"].rearrange("(c p) n -> p c n", p=P))
            load(qkv_raw[:, :, :], m.inputs["w_qkv1"].rearrange("(c p) d -> p c d", p=P))
            load(enc_b[:, :], m.inputs["enc_b"].rearrange("(c p) -> p c", p=P))
            load(c2s_b[:, :], m.inputs["c2s_b"].rearrange("(c p) -> p c", p=P))
            load(s2c_b[:, :], m.inputs["s2c_b"].unsqueeze(1))
            load(r1_b[:, :], m.inputs["rb1"].unsqueeze(1))
            load(e1_b[:, :], m.inputs["be1"].rearrange("e p -> p e"))
            load(r2_b[:, :], m.inputs["rb2"].partition_broadcast(P))
            load(dec_b[:, :], m.inputs["dec_b"].partition_broadcast(P))
            load(ln_g[:, :], m.inputs["ln_g"].partition_broadcast(P))
            load(ln_b[:, :], m.inputs["ln_b"].partition_broadcast(P))
            load(q_b[:, :], m.inputs["b_qkv1"][0:P].unsqueeze(1))
            load(kv_b[:, :], m.inputs["b_qkv1"][P:3 * P].partition_broadcast(P))
        F0_LOADS = 23

        @block.gpsimd
        def _(pool):
            nc.gpsimd.memset(e1_lo[M0:P, :, :].bitcast(F32), 0.0)
            nc.gpsimd.memset(r1_lo[M0:P, :].bitcast(F32), 0.0).then_inc(s["f0_zeros"], 1)

        @block.tensor
        def _(pe):
            pe.wait_ge(s["f0_loaded"], 16 * F0_LOADS)
            for c in range(3):
                last = nc.tensor.transpose(turned[:, c * P:(c + 1) * P], qkv_raw[:, c, :], m.ident[:, :])
            last.then_inc(s["qkv_turned"], 1)
            pe.wait_ge(s["f0_zeros"], 1)
            pe.wait_ge(s["f0_split"], 1)
            pe.wait_ge(s["qkv_T_ready"], 1)
            with pe.Fori(0, CHUNKS) as i:
                now = i + 1

                def expert_hidden(e):
                    b = e % 2
                    wait_count = i * EXPERTS + (e - 1)
                    if e >= 2:
                        pe.wait_ge(s["f0_hidden"], wait_count)
                    nc.tensor.matmul(hid[b][:, :], e1_hi[:, e, :], cont[:, :], start=True, stop=False)
                    nc.tensor.matmul(hid[b][:, :], e1_lo[:, e, :], cont[:, :], start=False, stop=True
                                     ).then_inc(s["f0_hidden_sum"], 1)

                def expert_out(e):
                    pe.wait_ge(s["f0_hidden"], i * EXPERTS + (e + 1))
                    if e > 0:
                        pe.wait_ge(s["f0_part"], i * EXPERTS + e)
                    for t in range(TILES):
                        last = nc.tensor.matmul(eout_t[:, t, :], hidden[e % 2][:, t * P:(t + 1) * P], e2[:, e, :],
                                                start=True, stop=True)
                    last.then_inc(s["f0_eout"], 1)

                pe.wait_ge(s["f0_yT"], now)
                for t in range(TILES):
                    last = nc.tensor.transpose(turned_t[:, t, :], yT[:, t * P:(t + 1) * P], m.ident[:, :])
                last.then_inc(s["f0_y_turned"], 1)
                pe.wait_ge(s["f0_xn"], now)
                for t in range(TILES):
                    last = nc.tensor.transpose(turned_t[:, t, :], xn[:, t, :], m.ident[:, :])
                last.then_inc(s["f0_x_turned"], 1)
                pe.wait_ge(s["f0_xT_lo"], now)
                for c in range(2):
                    cols = slice(c * P, (c + 1) * P)
                    nc.tensor.matmul(wide[:, c, :], enc_hi[:, cols], xT_hi[:, :], start=True, stop=False)
                    nc.tensor.matmul(wide[:, c, :], enc_hi[:, cols], xT_lo[:, :], start=False, stop=False)
                    nc.tensor.matmul(wide[:, c, :], enc_lo[:, cols], xT_hi[:, :], start=False, stop=True
                                     ).then_inc(s["f0_enc"], 1)
                for c in range(2):
                    pe.wait_ge(s["f0_spikes"], i * 2 + (c + 1))
                    last = nc.tensor.matmul(narrow[0:M0, :], s2c[:, c, :], spikes[:, c, :], start=c == 0, stop=c == 1)
                last.then_inc(s["f0_cont"], 1)
                pe.wait_ge(s["f0_cont_lo"], now)
                nc.tensor.matmul(narrow[0:M0, :], r1_hi[:, :], cont[:, :], start=True, stop=False)
                nc.tensor.matmul(narrow[0:M0, :], r1_lo[:, :], cont[:, :], start=False, stop=True
                                 ).then_inc(s["f0_router"], 1)
                expert_hidden(0)
                expert_hidden(1)
                pe.wait_ge(s["f0_tanh"], now)
                for t in range(TILES):
                    last = nc.tensor.matmul(logits[:, t, :], router[:, t * P:(t + 1) * P], r2[:, :],
                                            start=True, stop=True)
                last.then_inc(s["f0_logits"], 1)
                for e in range(EXPERTS):
                    expert_out(e)
                    if e + 2 < EXPERTS:
                        expert_hidden(e + 2)
                pe.wait_ge(s["f0_gates"], now)
                for t in range(TILES):
                    last = nc.tensor.transpose(small[0:EXPERTS, t * P:(t + 1) * P], g.gates[:, t, :], m.ident[:, :])
                last.then_inc(s["f0_gates_turned"], 1)
                pe.wait_ge(s["f0_gates_T"], now)
                nc.tensor.matmul(narrow[0:M0, :], e2_bias[:, :], gates_T[:, :], start=True, stop=False,
                                 skip_group_check=True)
                pe.wait_ge(s["f0_mixed"], now)
                for t in range(TILES):
                    last = nc.tensor.matmul(narrow[0:M0, t * P:(t + 1) * P], mixed[:, t, :], m.ident[:, :],
                                            start=False, stop=t == TILES - 1, skip_group_check=True)
                last.then_inc(s["f0_moe_sum"], 1)
                pe.wait_ge(s["f0_moe"], now)
                for c in range(2):
                    nc.tensor.matmul(wide[:, c, :], c2s[:, c * P:(c + 1) * P], moe[:, :], start=True, stop=True
                                     ).then_inc(s["f0_enc2"], 1)
                pe.wait_ge(s["f0_spikes2"], i * 2 + 2)
                for t in range(TILES):
                    for c in range(2):
                        last = nc.tensor.matmul(turned_t[:, t, :], spikes[:, c, t * P:(t + 1) * P], dec[:, c, :],
                                                start=c == 0, stop=c == 1)
                last.then_inc(s["f0_dec"], 1)
                pe.wait_ge(s["f0_xn2"], now)
                for t in range(TILES):
                    last = nc.tensor.transpose(turned_t[:, t, :], xn[:, t, :], m.ident[:, :])
                last.then_inc(s["f0_x2_turned"], 1)
                pe.wait_ge(s["f0_xT2"], now)
                nc.tensor.matmul(wide[:, 0, :], qkv_T[:, 0, :], xT2[:, :], start=True, stop=True).then_inc(s["f0_q"], 1)
                for t in range(TILES):
                    last = nc.tensor.matmul(hid[t // 2][:, (t % 2) * 256:(t % 2) * 256 + 256],
                                            xT2[:, t * P:(t + 1) * P],
                                            qkv_T[:, 1:3, :].rearrange("p c d -> p (c d)"), start=True, stop=True)
                    if t % 2:
                        last.then_inc(s["f0_kv"], 1)

        @block.scalar
        def _(act):
            act.wait_ge(s["qkv_turned"], 1)
            nc.scalar.copy(qkv_T[:, :, :], turned[:, 0:3 * P].rearrange("p (c d) -> p c d", c=3)
                           ).then_inc(s["qkv_T_ready"], 1)
            with act.Fori(0, CHUNKS) as i:
                now = i + 1
                norms = Norms(nc, None, m.carrier, s["f0_var"], s["f0_root"], m.eps, stats, mv, rstd, i, NORMS0)
                nc.scalar.copy(yT[:, :], m.yT[:, bass.ts(i, BANK)]).then_inc(s["f0_yT"], 1)
                norms.root(act)
                norms.root(act)
                act.wait_ge(s["f0_x_turned"], now)
                nc.scalar.copy(xT_hi[:, :], turned[:, :]).then_inc(s["f0_xT_hi"], 1)
                for c in range(2):
                    act.wait_ge(s["f0_enc"], i * 2 + (c + 1))
                    nc.scalar.activation(spikes[:, c, :], wide[:, c, :], ACT.Sigmoid, bias=enc_b[:, c:c + 1]
                                         ).then_inc(s["f0_spikes"], 1)
                act.wait_ge(s["f0_cont"], now)
                nc.scalar.activation(cont[0:M0, :], narrow[0:M0, :], ACT.Identity, bias=s2c_b[:, 0:1]
                                     ).then_inc(s["f0_cont_hi"], 1)
                act.wait_ge(s["f0_router"], now)
                nc.scalar.activation(router[:, :], narrow[0:M0, :], ACT.Tanh, bias=r1_b[:, 0:1]).then_inc(s["f0_tanh"], 1)

                def expert(e):
                    act.wait_ge(s["f0_hidden_sum"], i * EXPERTS + (e + 1))
                    if e >= 2:
                        act.wait_ge(s["f0_eout"], i * EXPERTS + (e - 1))
                    nc.scalar.activation(hidden[e % 2][:, :], hid[e % 2][:, :], ACT.Relu, bias=e1_b[:, e:e + 1]
                                         ).then_inc(s["f0_hidden"], 1)

                expert(0)
                expert(1)
                weigh_two(nc, act, g, s["f0_gap"], s["f0_weights"], now)
                for e in range(2, EXPERTS):
                    expert(e)
                act.wait_ge(s["f0_gates_turned"], now)
                nc.scalar.copy(gates_T[:, :], small[0:EXPERTS, :]).then_inc(s["f0_gates_T"], 1)
                act.wait_ge(s["f0_moe_sum"], now)
                nc.scalar.copy(moe[:, :], narrow[0:M0, :]).then_inc(s["f0_moe"], 1)
                for c in range(2):
                    act.wait_ge(s["f0_enc2"], i * 2 + (c + 1))
                    nc.scalar.activation(spikes[:, c, :], wide[:, c, :], ACT.Sigmoid, bias=c2s_b[:, c:c + 1]
                                         ).then_inc(s["f0_spikes2"], 1)
                act.wait_ge(s["f0_dec_sum"], now)
                nc.scalar.activation(decoded[:, :, :], decoded[:, :, :], ACT.Sigmoid).then_inc(s["f0_decoded"], 1)
                norms.root(act)
                norms.root(act)
                norms.root(act)
                act.wait_ge(s["f0_x2_turned"], now)
                nc.scalar.copy(xT2[:, :], turned[:, :]).then_inc(s["f0_xT2"], 1)
                act.wait_ge(s["f0_q"], now)
                nc.scalar.activation(m.qT[:, bass.ts(i, BANK)], wide[:, 0, :], ACT.Identity, bias=q_b[:, 0:1]
                                     ).then_inc(s["f0_qT"], 1)

        @block.vector
        def _(dve):
            dve.wait_ge(s["f0_loaded"], 16 * F0_LOADS)
            nc.vector.tensor_copy(enc_hi[:, :], enc_raw[:, :])
            nc.vector.tensor_copy(r1_hi[:, :], r1_raw[:, :])
            nc.vector.tensor_copy(e1_hi[:, :, :], e1_raw[:, :, :]).then_inc(s["f0_w_hi"], 1)
            for e in range(EXPERTS):
                nc.vector.memset(m.rank[:, e:e + 1], float(EXPERTS - e))
            dve.wait_ge(s["f0_w_hi"], 1)
            nc.vector.tensor_tensor(enc_lo[:, :], enc_raw[:, :], enc_hi[:, :].bitcast(F32), ALU.subtract)
            nc.vector.tensor_tensor(r1_lo[0:M0, :], r1_raw[0:M0, :], r1_hi[0:M0, :].bitcast(F32), ALU.subtract)
            nc.vector.tensor_tensor(e1_lo[0:M0, :, :], e1_raw[0:M0, :, :], e1_hi[0:M0, :, :].bitcast(F32), ALU.subtract
                                    ).then_inc(s["f0_split"], 1)
            dve.wait_ge(s["f0_split"], 1)
            with dve.Fori(0, CHUNKS) as i:
                now = i + 1
                ch = Chain(dve, s["f0_dve"], i * LINKS0)
                norms = Norms(nc, ch, m.carrier, s["f0_var"], s["f0_root"], m.eps, stats, mv, rstd, i, NORMS0)
                x = m.x[:, bass.ts(i, TILES), :]
                dve.wait_ge(s["f0_y_turned"], now)
                ch.link(norms.norm(turned_t, post))
                ch.link(nc.vector.tensor_tensor(x, x, post[:, :, :], ALU.add))
                norms.norm(x, xn).then_inc(s["f0_xn"], 1)
                dve.wait_ge(s["f0_x_turned"], now)
                dve.wait_ge(s["f0_xT_hi"], now)
                nc.vector.tensor_tensor(xT_lo[:, :], turned[:, :], xT_hi[:, :].bitcast(F32), ALU.subtract
                                        ).then_inc(s["f0_xT_lo"], 1)
                dve.wait_ge(s["f0_cont_hi"], now)
                nc.vector.scalar_tensor_tensor(out=cont[M0:P, :], in0=narrow[0:M0, :], scalar=s2c_b[:, 0:1],
                                               in1=cont[0:M0, :].bitcast(F32), op0=ALU.add, op1=ALU.subtract
                                               ).then_inc(s["f0_cont_lo"], 1)
                dve.wait_ge(s["f0_logits"], now)
                pick_two(nc, ch, g, logits, r2_b, m.rank, s["f0_gap"], s["f0_weights"], now).then_inc(s["f0_gates"], 1)
                dve.wait_ge(s["f0_gates"], now)
                for e in range(EXPERTS):
                    gate = g.gates[:, :, e:e + 1].broadcast_to([P, TILES, M0])
                    dve.wait_ge(s["f0_eout"], i * EXPERTS + (e + 1))
                    to = part if e else mixed
                    nc.vector.tensor_tensor(to[:, :, :], eout_t, gate, ALU.mult).then_inc(s["f0_part"], 1)
                    if e:
                        dve.wait_ge(s["f0_part"], i * EXPERTS + (e + 1))
                        ins = nc.vector.tensor_tensor(mixed[:, :, :], mixed[:, :, :], part[:, :, :], ALU.add)
                        if e < EXPERTS - 1:
                            ch.link(ins)
                        else:
                            ins.then_inc(s["f0_mixed"], 1)
                dve.wait_ge(s["f0_dec"], now)
                nc.vector.tensor_tensor(decoded[:, :, :], turned_t,
                                        dec_b[:, :].unsqueeze(1).broadcast_to([P, TILES, P]), ALU.add
                                        ).then_inc(s["f0_dec_sum"], 1)
                dve.wait_ge(s["f0_decoded"], now)
                ch.link(norms.norm(decoded, post))
                ch.link(nc.vector.tensor_tensor(post[:, :, :], post[:, :, :],
                                                ln_g[:, :].unsqueeze(1).broadcast_to([P, TILES, P]), ALU.mult))
                ch.link(nc.vector.tensor_tensor(post[:, :, :], post[:, :, :],
                                                ln_b[:, :].unsqueeze(1).broadcast_to([P, TILES, P]), ALU.add))
                ch.link(norms.norm(post, decoded))
                ch.link(nc.vector.tensor_tensor(x, x, decoded[:, :, :], ALU.add))
                norms.norm(x, xn).then_inc(s["f0_xn2"], 1)
                assert ch.n == LINKS0, ch.n
                for c in range(2):
                    dve.wait_ge(s["f0_kv"], i * 2 + (c + 1))
                    nc.vector.tensor_tensor(m.kv[:, bass.ds(i * 4 + 2 * c, 2), :],
                                            hid[c][:, :].rearrange("p (t d) -> p t d", t=2),
                                            kv_b[:, :].unsqueeze(1).broadcast_to([P, 2, 2 * P]), ALU.add
                                            ).then_inc(s["f0_kv_read"], 1)


D1 = P
DH1 = 16
HEADS1 = 8


def linear_attention(nc, m, s):
    with ExitStack() as ctx:
        w_raw = ctx.enter_context(nc.sbuf_tensor("wo_raw", [P, P], F32))
        w_ordered = ctx.enter_context(nc.sbuf_tensor("wo_ordered", [P, P], F32))
        w_T = ctx.enter_context(nc.sbuf_tensor("wo_T", [P, P], F32))
        same_head = ctx.enter_context(nc.sbuf_tensor("same_head", [P, HEADS1], F32))
        vk = ctx.enter_context(nc.sbuf_tensor("vk", [P, 2, P], F32))
        turned = ctx.enter_context(nc.psum_tensor("wo_turned", [P, P], F32))
        vk_sum = [ctx.enter_context(nc.psum_tensor(f"vk_sum{b}", [P, P], F32)) for b in range(2)]
        mix = [ctx.enter_context(nc.psum_tensor(f"mix{b}", [P, P], F32)) for b in range(2)]
        block = ctx.enter_context(nc.Block())

        @block.sync
        def _(sp):
            sp.dma_start(w_raw[:, :], m.inputs["w_o1"]).then_inc(s["wo_loaded"], 16)

        @block.tensor
        def _(pe):
            for b in range(2):
                for t in range(8):
                    kv = m.kv[:, b * 8 + t, :]
                    last = nc.tensor.matmul(vk_sum[b][:, :], kv[:, P:2 * P], kv[:, 0:P], start=t == 0, stop=t == 7)
                last.then_inc(s["vk_summed"], 1)
            pe.wait_ge(s["wo_ordered"], 1)
            nc.tensor.transpose(turned[:, :], w_ordered[:, :], m.ident[:, :]).then_inc(s["wo_turned"], 1)
            pe.wait_ge(s["wo_ready"], 1)
            for b in range(2):
                pe.wait_ge(s["vk_masked"], b + 1)
                nc.tensor.matmul(mix[b][:, :], vk[:, b, :], w_T[:, :], start=True, stop=True).then_inc(s["mixed1"], 1)

        @block.scalar
        def _(act):
            act.wait_ge(s["wo_turned"], 1)
            nc.scalar.copy(w_T[:, :], turned[:, :]).then_inc(s["wo_ready"], 1)

        @block.vector
        def _(dve):
            dve.wait_ge(s["wo_loaded"], 16)
            nc.vector.tensor_copy(w_ordered[:, :].rearrange("p (d h) -> p d h", h=HEADS1),
                                  w_raw[:, :].rearrange("p (h d) -> p d h", h=HEADS1)).then_inc(s["wo_ordered"], 1)
            nc.vector.tensor_reduce(same_head[:, :], m.ident[:, :].rearrange("p (d h) -> p h d", h=HEADS1), X, ALU.add
                                    ).then_inc(s["same_head"], 1)
            dve.wait_ge(s["same_head"], 1)
            for b in range(2):
                dve.wait_ge(s["vk_summed"], b + 1)
                nc.vector.tensor_tensor(vk[:, b, :].rearrange("p (d h) -> p d h", h=HEADS1),
                                        vk_sum[b][:, :].rearrange("p (d h) -> p d h", h=HEADS1),
                                        same_head[:, :].unsqueeze(1).broadcast_to([P, DH1, HEADS1]), ALU.mult
                                        ).then_inc(s["vk_masked"], 1)
            for b in range(2):
                dve.wait_ge(s["mixed1"], b + 1)
                for c in range(2):
                    last = nc.vector.tensor_copy(m.mix[:, b * 2 + c, :], mix[b][:, :])
            last.then_inc(s["mix_ready"], 1)


H1 = 512
HC = H1 // P
NORMS1 = 3
LINKS1 = NORMS1 * 2 + GATE_LINKS + (EXPERTS - 1) + 5


def ffn1(nc, m, s):
    with ExitStack() as ctx:
        def sb(name, shape, dt=F32):
            return ctx.enter_context(nc.sbuf_tensor(name, shape, dt))

        w1_raw = sb("w1_raw", [P, EXPERTS, H1])
        w1_hi, w1_lo = sb("w1_hi", [P, EXPERTS, H1], F32R), sb("w1_lo", [P, EXPERTS, H1], F32R)
        w2 = sb("w2", [P, EXPERTS, HC, P])
        b1 = sb("b1", [P, EXPERTS, HC])
        b2 = sb("b2", [EXPERTS, P])
        wr = sb("wr", [P, EXPERTS])
        bo = sb("bo", [P, P])
        qT = sb("qT_chunk", [P, BANK])
        post = sb("post1", [P, TILES, P])
        xn = sb("xn1", [P, TILES, P])
        xT = sb("xT1", [P, BANK])
        xT_hi, xT_lo = sb("xT_hi1", [P, BANK], F32R), sb("xT_lo1", [P, BANK], F32R)
        hidden = [sb(f"hidden1_{b}", [P, BANK]) for b in range(HC)]
        part = sb("part1", [P, TILES, P])
        mixed = sb("mixed1", [P, TILES, P])
        gates_T = sb("gates_T1", [EXPERTS, BANK])
        stats, mv, rstd = sb("stats1", [P, TILES, 6]), sb("mv1", [P, TILES, 2]), sb("rstd1", [P, TILES])
        g = gating_buffers(sb, "g1")

        def pb(name, shape):
            return ctx.enter_context(nc.psum_tensor(name, shape, F32))

        turned = pb("turned1", [P, BANK])
        small = pb("small1", [P, BANK])
        hid = [pb(f"hid1_{b}", [P, BANK]) for b in range(4)]
        eout = [pb(f"eout1_{b}", [P, BANK]) for b in range(2)]
        turned_t = turned[:, :].rearrange("p (t d) -> p t d", t=TILES)
        eout_t = [e[:, :].rearrange("p (t d) -> p t d", t=TILES) for e in eout]
        logits = small[:, 0:TILES * EXPERTS].rearrange("p (t e) -> p t e", t=TILES)
        CHUNKS = 4
        block = ctx.enter_context(nc.Block())

        @block.sync
        def _(sp):
            for e in range(EXPERTS):
                sp.dma_start(w1_raw[:, e, :], m.inputs["W1"][e]).then_inc(s["w1_loaded"][e], 16)
                sp.dma_start(w2[:, e, :, :], m.inputs["W2"][e].rearrange("(c p) d -> p c d", p=P)).then_inc(s["w1_loaded"][e], 16)
            sp.dma_start(b1[:, :, :], m.inputs["b1"].rearrange("e (c p) -> p e c", p=P)).then_inc(s["f1_loaded"], 16)
            with sp.Fori(0, CHUNKS) as i:
                sp.wait_ge(s["f1_x_out"], i + 1)
                sp.dma_start(m.out_tiles[:, bass.ts(i, TILES), :], m.x[:, bass.ts(i, TILES), :]).then_inc(s["stored"], 16)
            sp.wait_ge(s["stored"], 16 * CHUNKS)

        @block.gpsimd
        def _(pool):
            for dst, src in ((bo[:, :], m.inputs["b_o1"].partition_broadcast(P)), (wr[:, :], m.inputs["Wr"]), (b2[:, :], m.inputs["b2"])):
                pool.dma_start(dst, src).then_inc(s["f1_small_loaded"], 16)
            pool.wait_ge(s["f1_small_loaded"], 48)

        @block.tensor
        def _(pe):
            pe.wait_ge(s["f1_small_loaded"], 48)
            pe.wait_ge(s["f1_loaded"], 16)
            with pe.Fori(0, CHUNKS) as i:
                now = i + 1
                pe.wait_ge(s["f1_qT"], now)
                for t in range(TILES):
                    last = nc.tensor.matmul(turned_t[:, t, :], qT[:, t * P:(t + 1) * P],
                                            m.mix[:, bass.ds(i, 1), :].rearrange("p a d -> p (a d)"),
                                            start=True, stop=True)
                last.then_inc(s["f1_attended"], 1)
                pe.wait_ge(s["f1_xn"], now)
                for t in range(TILES):
                    last = nc.tensor.transpose(turned_t[:, t, :], xn[:, t, :], m.ident[:, :])
                last.then_inc(s["f1_x_turned"], 1)
                pe.wait_ge(s["f1_xT_lo"], now)
                for t in range(TILES):
                    last = nc.tensor.matmul(logits[:, t, :], xT[:, t * P:(t + 1) * P], wr[:, :], start=True, stop=True)
                last.then_inc(s["f1_logits"], 1)

                def expert_hidden(e, c):
                    k = e * HC + c
                    if k >= 4:
                        pe.wait_ge(s["f1_hidden"], i * (EXPERTS * HC) + (k - 3))
                    cols = slice(c * P, (c + 1) * P)
                    nc.tensor.matmul(hid[c][:, :], w1_hi[:, e, cols], xT_hi[:, :], start=True, stop=False)
                    nc.tensor.matmul(hid[c][:, :], w1_hi[:, e, cols], xT_lo[:, :], start=False, stop=False)
                    nc.tensor.matmul(hid[c][:, :], w1_lo[:, e, cols], xT_hi[:, :], start=False, stop=True
                                     ).then_inc(s["f1_hidden_sum"], 1)

                def expert_out(e, c):
                    pe.wait_ge(s["f1_hidden"], i * (EXPERTS * HC) + (e * HC + c + 1))
                    if c == 0 and e >= 2:
                        pe.wait_ge(s["f1_part"], i * EXPERTS + (e - 1))
                    for t in range(TILES):
                        last = nc.tensor.matmul(eout_t[e % 2][:, t, :], hidden[c][:, t * P:(t + 1) * P], w2[:, e, c, :],
                                                start=c == 0 and t == 0, stop=c == HC - 1, skip_group_check=True)
                    last.then_inc(s["f1_eout"], 1)

                for e in range(EXPERTS):
                    pe.wait_ge(s["w1_split"], e + 1)
                    for c in range(HC):
                        expert_hidden(e, c)
                        if e > 0 or c > 1:
                            k = e * HC + c - 2
                            expert_out(k // HC, k % HC)
                for k in (EXPERTS * HC - 2, EXPERTS * HC - 1):
                    expert_out(k // HC, k % HC)
                pe.wait_ge(s["f1_gates"], now)
                for t in range(TILES):
                    last = nc.tensor.transpose(small[0:EXPERTS, t * P:(t + 1) * P], g.gates[:, t, :], m.ident[:, :])
                last.then_inc(s["f1_gates_turned"], 1)
                pe.wait_ge(s["f1_gates_T"], now)
                for t in range(TILES):
                    last = nc.tensor.matmul(turned_t[:, t, :], gates_T[:, t * P:(t + 1) * P], b2[:, :],
                                            start=True, stop=True)
                last.then_inc(s["f1_bias"], 1)

        @block.scalar
        def _(act):
            with act.Fori(0, CHUNKS) as i:
                now = i + 1
                norms = Norms(nc, None, m.carrier, s["f1_var"], s["f1_root"], m.eps, stats, mv, rstd, i, NORMS1)
                nc.scalar.copy(qT[:, :], m.qT[:, bass.ts(i, BANK)]).then_inc(s["f1_qT"], 1)
                norms.root(act)
                norms.root(act)
                act.wait_ge(s["f1_x_turned"], now)
                nc.scalar.copy(xT[:, :], turned[:, :])
                nc.scalar.copy(xT_hi[:, :], turned[:, :]).then_inc(s["f1_xT_hi"], 1)
                weigh_two(nc, act, g, s["f1_gap"], s["f1_weights"], now)
                for e in range(EXPERTS):
                    for c in range(HC):
                        k = e * HC + c
                        act.wait_ge(s["f1_hidden_sum"], i * (EXPERTS * HC) + (k + 1))
                        if k >= HC:
                            act.wait_ge(s["f1_eout"], i * (EXPERTS * HC) + (k - HC + 1))
                        nc.scalar.activation(hidden[c][:, :], hid[c][:, :], ACT.Gelu, bias=b1[:, e, c:c + 1]
                                             ).then_inc(s["f1_hidden"], 1)
                act.wait_ge(s["f1_gates_turned"], now)
                nc.scalar.copy(gates_T[:, :], small[0:EXPERTS, :]).then_inc(s["f1_gates_T"], 1)
                norms.root(act)

        @block.vector
        def _(dve):
            for e in range(EXPERTS):
                dve.wait_ge(s["w1_loaded"][e], 32)
                nc.vector.tensor_copy(w1_hi[:, e, :], w1_raw[:, e, :]).then_inc(s["w1_hi_ready"], 1)
                dve.wait_ge(s["w1_hi_ready"], e + 1)
                nc.vector.tensor_tensor(w1_lo[:, e, :], w1_raw[:, e, :], w1_hi[:, e, :].bitcast(F32), ALU.subtract
                                        ).then_inc(s["w1_split"], 1)
            with dve.Fori(0, CHUNKS) as i:
                now = i + 1
                ch = Chain(dve, s["f1_dve"], i * LINKS1)
                norms = Norms(nc, ch, m.carrier, s["f1_var"], s["f1_root"], m.eps, stats, mv, rstd, i, NORMS1)
                x = m.x[:, bass.ts(i, TILES), :]
                dve.wait_ge(s["f1_attended"], now)
                ch.link(nc.vector.tensor_tensor(post[:, :, :], turned_t,
                                                bo[:, :].unsqueeze(1).broadcast_to([P, TILES, P]), ALU.add))
                ch.link(norms.norm(post, xn))
                ch.link(nc.vector.tensor_tensor(x, x, xn[:, :, :], ALU.add))
                norms.norm(x, xn).then_inc(s["f1_xn"], 1)
                dve.wait_ge(s["f1_x_turned"], now)
                dve.wait_ge(s["f1_xT_hi"], now)
                nc.vector.tensor_tensor(xT_lo[:, :], turned[:, :], xT_hi[:, :].bitcast(F32), ALU.subtract
                                        ).then_inc(s["f1_xT_lo"], 1)
                dve.wait_ge(s["f1_logits"], now)
                pick_two(nc, ch, g, logits, None, m.rank, s["f1_gap"], s["f1_weights"], now).then_inc(s["f1_gates"], 1)
                dve.wait_ge(s["f1_gates"], now)
                for e in range(EXPERTS):
                    gate = g.gates[:, :, e:e + 1].broadcast_to([P, TILES, P])
                    dve.wait_ge(s["f1_eout"], i * (EXPERTS * HC) + (e + 1) * HC)
                    to = part if e else mixed
                    nc.vector.tensor_tensor(to[:, :, :], eout_t[e % 2], gate, ALU.mult).then_inc(s["f1_part"], 1)
                    if e:
                        dve.wait_ge(s["f1_part"], i * EXPERTS + (e + 1))
                        ch.link(nc.vector.tensor_tensor(mixed[:, :, :], mixed[:, :, :], part[:, :, :], ALU.add))
                dve.wait_ge(s["f1_bias"], now)
                ch.link(nc.vector.tensor_tensor(mixed[:, :, :], turned_t, mixed[:, :, :], ALU.add))
                ch.link(norms.norm(mixed, post))
                nc.vector.tensor_tensor(x, x, post[:, :, :], ALU.add).then_inc(s["f1_x_out"], 1)
                dve.wait_ge(s["f1_x_out"], now)
                assert ch.n == LINKS1, ch.n


INPUTS = ["L0_attn_data", "L0_attn_W_qkv", "L0_attn_b_qkv", "L0_attn_W_out", "L0_attn_b_out",
          "L0_ffn_enc_W", "L0_ffn_enc_b", "L0_ffn_s2c_W", "L0_ffn_s2c_b", "L0_ffn_rW1", "L0_ffn_rb1", "L0_ffn_rW2",
          "L0_ffn_rb2", "L0_ffn_We1", "L0_ffn_be1", "L0_ffn_We2", "L0_ffn_be2", "L0_ffn_c2s_W", "L0_ffn_c2s_b",
          "L0_ffn_dec_W", "L0_ffn_dec_b", "L0_ffn_ln_g", "L0_ffn_ln_b",
          "L1_attn_w_qkv", "L1_attn_b_qkv", "L1_attn_w_o", "L1_attn_b_o",
          "L1_ffn_Wr", "L1_ffn_W1", "L1_ffn_b1", "L1_ffn_W2", "L1_ffn_b2"]
SHORT = ["data", "W_qkv", "b_qkv", "W_out", "b_out_row", "enc_W", "enc_b", "s2c_W", "s2c_b", "rW1", "rb1", "rW2", "rb2",
         "We1", "be1", "We2", "be2", "c2s_W", "c2s_b", "dec_W", "dec_b", "ln_g", "ln_b",
         "w_qkv1", "b_qkv1", "w_o1", "b_o1", "Wr", "W1", "b1", "W2", "b2"]


SEMAPHORES = """
bias_loaded cleared em_dve em_hi em_lo em_sqrt em_turned em_var em_xn eps_ready f0_cont f0_cont_hi f0_cont_lo
f0_dec f0_dec_sum f0_decoded f0_dve f0_enc f0_enc2 f0_eout f0_gap f0_gates f0_gates_T f0_gates_turned
f0_hidden f0_hidden_sum f0_kv f0_kv_read f0_loaded f0_logits f0_mixed f0_moe f0_moe_sum f0_part f0_q f0_qT
f0_root f0_router f0_spikes f0_spikes2 f0_split f0_tanh f0_var f0_w_hi f0_weights f0_x2_turned f0_xT2 f0_xT_hi
f0_xT_lo f0_x_turned f0_xn f0_xn2 f0_yT f0_y_turned f0_zeros f1_attended f1_bias f1_dve f1_eout f1_gap
f1_gates f1_gates_T f1_gates_turned f1_hidden f1_hidden_sum f1_loaded f1_logits f1_part f1_qT f1_root
f1_small_loaded f1_var f1_weights f1_xT_hi f1_xT_lo f1_x_out f1_x_turned f1_xn filled ident0 ident_ready
inv_stored inv_sum_ready inverted leading_ready mix_ready mixed1 neg_max_ready normalised pair_loaded
qkv_T_ready qkv_turned raw_out_ready same_head stored sum_cols_ready vk_masked vk_summed w1_hi_ready w1_split
w_hi_ready w_out_loaded w_split weighed wo_loaded wo_ordered wo_ready wo_turned yT_clear
""".split()
SEMAPHORE_LISTS = {'x_loaded': 4, 'shared_free': 2, 'shared_full': 2, 'exp_done': 2, 'scores_ready': 2, 'keys_added': 2, 'w1_loaded': 8}


def build(nc, inputs, out):
    m = Buffers()
    m.inputs = inputs
    m.out_tiles = out.rearrange("n (t p) d -> p (n t) d", p=P)
    with ExitStack() as ctx:
        def sb(name, shape, dt=F32):
            return ctx.enter_context(nc.sbuf_tensor(name, shape, dt))

        ctx.enter_context(nc.allow_non_contiguous_dma(reason="biases as columns"))
        s = {name: ctx.enter_context(nc.semaphore(name)) for name in SEMAPHORES}
        for name, count in SEMAPHORE_LISTS.items():
            s[name] = [ctx.enter_context(nc.semaphore(f"{name}{i}")) for i in range(count)]
        m.x = sb("x", [P, 16, P])
        m.xT = sb("xT", [P, 2048])
        m.xT_hi = sb("xT_hi", [P, 2048], F32R)
        m.xT_lo = sb("xT_lo", [P, 2048], F32R)
        m.yT = sb("yT", [P, 2048])
        m.kv = sb("kv", [P, 16, 2 * P])
        m.mix = sb("mix", [P, 4, P])
        m.qT = m.xT
        m.ident, m.ident_bf = sb("ident", [P, P]), sb("ident_bf", [P, P], BF16)
        m.ones, m.eps, m.rank = sb("ones", [P, P]), sb("eps", [P, 1]), sb("rank", [P, EXPERTS])
        m.b_out, m.carrier = sb("b_out", [P, 1]), sb("carrier", [P, 1])
        embed(nc, m, s)
        attention(nc, m, s)
        ffn0(nc, m, s)
        linear_attention(nc, m, s)
        ffn1(nc, m, s)


def kernel(**inputs):
    import numpy as _np
    import concourse.bacc as _bacc
    from concourse.bass_utils import run_bass_kernel_spmd as _run

    nc = _bacc.Bacc("TRN2", target_bir_lowering=False, num_devices=1)
    arrays, args = {}, {}
    for name, short in zip(INPUTS, SHORT):
        a = _np.ascontiguousarray(inputs[name])
        arrays[f"in_{name}_dram"] = a
        args[short] = nc.dram_tensor(f"in_{name}_dram", a.shape, mybir.dt.from_np(a.dtype), kind="ExternalInput").ap()
    out = nc.dram_tensor("out_dram", (2, 1024, P), F32, kind="ExternalOutput").ap()
    build(nc, args, out)
    r = _run(nc, [arrays], core_ids=[0])
    return r.results[0]["out_dram"]
```

```python
from contextlib import ExitStack

import concourse.bass as bass
from concourse import mybir

F32 = mybir.dt.float32
F32R = mybir.dt.float32r
BF16 = mybir.dt.bfloat16
ALU = mybir.AluOpType
ACT = mybir.ActivationFunctionType
X = mybir.AxisListType.X

P = 128
EPS = 1e-5
BANK = 512
TILES = BANK // P
LEAST = -3.0e38

HEADS, HD = 16, 64
PAIRS = HEADS // 2
RING = 4
PREP_USES = 42
POST_USES = 4
STEP_USES = PREP_USES + POST_USES
PIECES = 8
MAXIMA = {3: range(0, 8), 4: range(8, 16), 5: range(16, 24), 6: range(24, 32)}


class Buffers:
    pass


def wait(eng, sem, value):
    if not (isinstance(value, int) and value <= 0):
        eng.wait_ge(sem, value)


class Chain:

    def __init__(self, eng, sem, before=0):
        self.eng, self.sem, self.before, self.n = eng, sem, before, 0

    def link(self, ins):
        ins.then_inc(self.sem, 1)
        self.n += 1
        self.eng.wait_ge(self.sem, self.before + self.n)


def embed(nc, m, s):
    with ExitStack() as ctx:
        stats = ctx.enter_context(nc.sbuf_tensor("em_stats", [P, TILES, 6], F32))
        mv = ctx.enter_context(nc.sbuf_tensor("em_mv", [P, 4, TILES, 2], F32))
        rstd = ctx.enter_context(nc.sbuf_tensor("em_rstd", [P, 4, TILES], F32))
        xn = ctx.enter_context(nc.sbuf_tensor("em_xn", [P, 4, TILES, P], F32))
        turned = [ctx.enter_context(nc.psum_tensor(f"em_turned{c}", [P, BANK], F32)) for c in range(4)]
        block = ctx.enter_context(nc.Block())

        @block.sync
        def _(sp):
            sp.dma_start(m.b_out[:, :], m.inputs["b_out_row"].unsqueeze(1)).then_inc(s["bias_loaded"], 16)
            for c in range(4):
                n, t0 = c // 2, (c % 2) * TILES
                sp.dma_start(m.x[:, c * TILES:(c + 1) * TILES, :],
                             m.inputs["data"][n].rearrange("(t p) d -> p t d", p=P)[:, t0:t0 + TILES, :]
                             ).then_inc(s["x_loaded"][c], 16)

        @block.gpsimd
        def _(pool):
            nc.gpsimd.memset(m.ident[:, :], 0.0).then_inc(s["ident0"], 1)
            nc.gpsimd.memset(m.ident_bf[:, :], 0.0).then_inc(s["ident0"], 1)
            pool.wait_ge(s["ident0"], 2)
            for d in (m.ident, m.ident_bf):
                nc.gpsimd.affine_select(out=d[:, :], in_=d[:, :], compare_op=ALU.not_equal, fill=1.0, base=0,
                                        pattern=[[-1, P]], channel_multiplier=1).then_inc(s["ident_ready"], 1)

        @block.vector
        def _(dve):
            nc.vector.memset(m.eps[:, :], EPS).then_inc(s["eps_ready"], 1)
            nc.vector.memset(m.ones[:, :], 1.0)
            ch = Chain(dve, s["em_dve"])
            for c in range(4):
                dve.wait_ge(s["x_loaded"][c], 16)
                for t in range(TILES):
                    last = nc.vector.bn_stats(stats[:, t, :], m.x[:, c * TILES + t, :])
                ch.link(last)
                for t in range(TILES):
                    last = nc.vector.bn_aggr(mv[:, c, t, :], stats[:, t, :])
                last.then_inc(s["em_var"], 1)
                dve.wait_ge(s["em_sqrt"], c + 1)
                ch.link(nc.vector.reciprocal(rstd[:, c, :], rstd[:, c, :]))
                for t in range(TILES):
                    last = nc.vector.tensor_scalar(xn[:, c, t, :], m.x[:, c * TILES + t, :], mv[:, c, t, 0:1],
                                                   rstd[:, c, t:t + 1], ALU.subtract, ALU.mult)
                last.then_inc(s["em_xn"], 1)
            for c in range(4):
                dve.wait_ge(s["em_hi"], c + 1)
                cols = slice(c * BANK, (c + 1) * BANK)
                nc.vector.tensor_tensor(m.xT_lo[:, cols], m.xT[:, cols], m.xT_hi[:, cols].bitcast(F32),
                                        ALU.subtract).then_inc(s["em_lo"], 1)

        @block.scalar
        def _(act):
            act.wait_ge(s["eps_ready"], 1)
            for c in range(4):
                act.wait_ge(s["em_var"], c + 1)
                nc.scalar.activation(rstd[:, c, :], mv[:, c, :, 1], ACT.Sqrt,
                                     bias=m.eps[:, 0:1]).then_inc(s["em_sqrt"], 1)
            for c in range(4):
                act.wait_ge(s["em_turned"], c + 1)
                cols = slice(c * BANK, (c + 1) * BANK)
                nc.scalar.copy(m.xT[:, cols], turned[c][:, :])
                nc.scalar.copy(m.xT_hi[:, cols], turned[c][:, :]).then_inc(s["em_hi"], 1)

        @block.tensor
        def _(pe):
            pe.wait_ge(s["ident_ready"], 2)
            for c in range(4):
                pe.wait_ge(s["em_xn"], c + 1)
                for t in range(TILES):
                    last = nc.tensor.transpose(turned[c][:, t * P:(t + 1) * P], xn[:, c, t, :], m.ident[:, :])
                last.then_inc(s["em_turned"], 1)


def attention(nc, m, s):
    with ExitStack() as ctx:
        def sb(name, shape, dt=F32):
            return ctx.enter_context(nc.sbuf_tensor(name, shape, dt))

        w_raw = sb("w_raw", [P, 2, P])
        w_hi = sb("w_hi", [P, 2, P], F32R)
        w_lo = sb("w_lo", [P, 2, P], F32R)
        w_v = sb("w_v", [P, P])
        w_out = sb("w_out", [P, P])
        b_qk = sb("b_qk", [P, 2])
        b_v = sb("b_v", [P, P])
        q_both = [[sb(f"q_both{b}{h}", [P, 1024], F32R) for h in range(2)] for b in range(2)]
        q_shift = [[sb(f"q_shift{b}{h}", [P, 1024], F32R) for h in range(2)] for b in range(2)]
        k_hi = [[sb(f"k_hi{b}{h}", [P, 1024], F32R) for h in range(2)] for b in range(2)]
        k_lo = [[sb(f"k_lo{b}{h}", [P, 1024], F32R) for h in range(2)] for b in range(2)]
        v = [sb(f"v{b}", [P, 8, P]) for b in range(2)]
        probs = [sb(f"probs{h}", [P, RING, 1024]) for h in range(2)]
        key_sum = [[sb(f"key_sum{b}{h}", [P, 1024]) for h in range(2)] for b in range(2)]
        maxima = sb("maxima", [P, 2, 8, 2])
        neg_max = sb("neg_max", [P, 2, 8], BF16)
        raw_out = sb("raw_out", [P, 1024])
        row_sum = sb("row_sum", [P, 1024])
        sum_cols = sb("sum_cols", [P, 2, 8])
        inv_cols = sb("inv_cols", [P, 2, 8])
        inv_sum = sb("inv_sum", [P, 1024])
        inv_dram = nc.dram_tensor("inv_sums", [2, 2, 1024], F32, kind="Internal").ap()
        heads_out = sb("heads_out", [P, 1024])

        scores = [ctx.enter_context(nc.psum_tensor(f"scores{h}", [P, 1024], F32)) for h in range(2)]
        pv = ctx.enter_context(nc.psum_tensor("pv", [P, 1024], F32))
        shared = [ctx.enter_context(nc.psum_tensor(f"shared{b}", [P, BANK], F32)) for b in range(2)]

        HALF = [slice(0, HD), slice(HD, P)]
        OTHER = [HALF[1], HALF[0]]
        SHIFT_ROW = [HD, 0]
        C = [slice(0, BANK), slice(BANK, 2 * BANK)]

        def order_of_uses(prev, nxt):
            order = []
            if nxt:
                order += [("q", 0), ("q", 1), ("k", 0), ("k", 1), ("v", 0), ("v", 1)]
            if prev:
                order += [("sum", 0), ("sum", 1)]
            if nxt:
                order += [("max", i) for i in range(32)] + [(f"row{h}", c) for h in range(2) for c in range(2)]
            if prev:
                order += [("proj", 0), ("proj", 1)]
            return {name: k for k, name in enumerate(order)}

        class Uses:

            def __init__(self, before, prev=True, nxt=True):
                self.before, self.at = before, order_of_uses(prev, nxt)

            def bank(self, *name):
                return self.at[name] % 2

            def earlier(self, *name):
                return self.before + self.at[name] // 2

        PREP, POST = PREP_USES // 2, POST_USES // 2
        prologue = Uses(0, prev=False)

        def uses_in(p, n, first=False, last=False):
            if first:
                return Uses(PREP, prev=False)
            return Uses(2 * PREP + (p * 2 + n - 1) * (PREP + POST), nxt=not last)

        epilogue = Uses(2 * PREP + (2 * PAIRS - 2) * (PREP + POST) + POST, nxt=False)

        W = m.inputs["W_qkv"].rearrange("d (c n) -> d c n", c=3)
        B = m.inputs["b_qkv"].rearrange("(c n) -> n c", c=3)

        block = ctx.enter_context(nc.Block())

        @block.sync
        def _(sp):
            def load_pair(p):
                cols = bass.ts(p, P)
                sp.dma_start(w_raw[:, :, :], W[:, 0:2, cols]).then_inc(s["pair_loaded"], 16)
                sp.dma_start(w_v[:, :], W[:, 2, cols]).then_inc(s["pair_loaded"], 16)
                sp.dma_start(b_qk[:, :], B[cols, 0:2]).then_inc(s["pair_loaded"], 16)
                sp.dma_start(b_v[:, :], m.inputs["b_qkv"][bass.ds(p * P + 2 * HEADS * HD, P)].partition_broadcast(P)
                             ).then_inc(s["pair_loaded"], 16)

            def next_pair(p, first=False):
                u = uses_in(p, 0, first=first)
                sp.wait_ge(s["shared_free"][u.bank("v", 1)], u.earlier("v", 1) + 1)
                load_pair(p + 1)

            def out_weights(p, first=False):
                if not first:
                    u = uses_in(p, 0)
                    sp.wait_ge(s["shared_free"][u.bank("proj", 1)], u.earlier("proj", 1) + 1)
                sp.dma_start(w_out[:, :], m.inputs["W_out"][bass.ts(p, P), :]).then_inc(s["w_out_loaded"], 16)

            def invert(p, n, u):
                st = p * 2 + n
                for c in range(2):
                    sp.wait_ge(s["shared_free"][u.bank("sum", c)], u.earlier("sum", c) + 1)
                for h in range(2):
                    sp.dma_start(sum_cols[:, h, :], row_sum[h * HD:h * HD + 1, :].rearrange("o (p j) -> o p j", j=8)
                                 ).then_inc(s["sum_cols_ready"], 16)
                sp.wait_ge(s["inverted"], st + 1)
                sp.dma_start(inv_dram[n].rearrange("h (p j) -> p h j", j=8), inv_cols[:, :, :]
                             ).then_inc(s["inv_stored"], 16)
                sp.wait_ge(s["inv_stored"], st * 16 + 16)
                wait(sp, s["normalised"], st)
                for h in range(2):
                    sp.dma_start(inv_sum[HALF[h], :], inv_dram[n, h].partition_broadcast(HD)
                                 ).then_inc(s["inv_sum_ready"], 16)

            def copy_leading(p, n):
                st = p * 2 + n
                for j, (what, to) in enumerate(((q_both, q_shift), (k_hi, k_hi))):
                    sp.wait_ge(s["leading_ready"], st * 4 + 2 * j + 2)
                    for h in range(2):
                        sp.dma_start(to[n][h][(HALF, OTHER)[j][h], :].bitcast(F32), what[n][h][HALF[h], :].bitcast(F32)
                                     ).then_inc(s["leading_copied"], 16)

            def step(p, n, first=False, last=False):
                if not last:
                    copy_leading(p + n, 1 - n)
                if n == 0 and not (isinstance(p, int) and p == PAIRS - 1):
                    next_pair(p, first)
                if not first:
                    invert(p - 1 + n, 1 - n, uses_in(p, n, last=last))
                if n == 0 and not first:
                    out_weights(p)

            load_pair(0)
            out_weights(0, first=True)
            copy_leading(0, 0)
            step(0, 0, first=True)
            step(0, 1)
            with sp.Fori(1, PAIRS - 1) as p:
                step(p, 0)
                step(p, 1)
            step(PAIRS - 1, 0)
            step(PAIRS - 1, 1, last=True)
            invert(PAIRS - 1, 1, epilogue)

        @block.tensor
        def _(pe):
            def take(u, *name):
                wait(pe, s["shared_free"][u.bank(*name)], u.earlier(*name))
                return shared[u.bank(*name)]

            def read(u, *name):
                pe.wait_ge(s["shared_free"][u.bank(*name)], u.earlier(*name) + 1)

            def project_qk(u, what, c, p, n):
                j = "qk".index(what)
                pe.wait_ge(s["w_split"], p + 1)
                out = take(u, what, c)
                cols = slice(n * 1024 + c * BANK, n * 1024 + (c + 1) * BANK)
                nc.tensor.matmul(out[:, :], w_hi[:, j, :], m.xT_hi[:, cols], start=True, stop=False)
                nc.tensor.matmul(out[:, :], w_hi[:, j, :], m.xT_lo[:, cols], start=False, stop=False)
                nc.tensor.matmul(out[:, :], w_lo[:, j, :], m.xT_hi[:, cols], start=False, stop=True
                                 ).then_inc(s["shared_full"][u.bank(what, c)], 1)

            def project_v(u, j, n):
                out = take(u, "v", j)
                for t in range(TILES):
                    tok = n * 1024 + (j * TILES + t) * P
                    last = nc.tensor.matmul(out[:, t * P:(t + 1) * P], m.xT[:, tok:tok + P], w_v[:, :],
                                            start=True, stop=True)
                last.then_inc(s["shared_full"][u.bank("v", j)], 1)

            def find_maxima(u, slot, place, p, n):
                if slot not in MAXIMA:
                    return
                if slot == 3 and place == 0:
                    for c in range(2):
                        read(u, "k", c)
                    pe.wait_ge(s["leading_copied"], (p * 2 + n + 1) * 64)
                i = MAXIMA[slot][place]
                h, qt, kc = i // 16, i % 16 // 2, i % 2
                out = take(u, "max", i)
                nc.tensor.matmul(out[:, :], q_both[n][h][:, qt * P:(qt + 1) * P], k_hi[n][h][:, C[kc]],
                                 start=True, stop=True).then_inc(s["shared_full"][u.bank("max", i)], 1)

            def shift_row(u, h, c, p, n):
                pe.wait_ge(s["neg_max_ready"], (p * 2 + n) * 2 + h + 1)
                r = SHIFT_ROW[h]
                out = take(u, f"row{h}", c)
                for t in range(TILES):
                    j = c * TILES + t
                    last = nc.tensor.matmul(out[r:r + 1, t * P:(t + 1) * P], neg_max[:, h, j:j + 1],
                                            m.ident_bf[:, :], start=True, stop=True)
                last.then_inc(s["shared_full"][u.bank(f"row{h}", c)], 1)

            def score(p, n, kt, h, prepared, between):
                if kt == 0:
                    for c in range(2):
                        read(prepared, f"row{h}", c)
                wait(pe, s["exp_done"][h], (p * 2 + n) * 8 + kt)
                for part, (w, q, start) in enumerate(((k_hi, q_both, True), (k_lo, q_shift, False))):
                    for c in range(2):
                        last = nc.tensor.matmul(scores[h][:, C[c]], w[n][h][:, kt * P:(kt + 1) * P],
                                                q[n][h][:, C[c]], start=start, stop=not start)
                    if part == 1:
                        last.then_inc(s["scores_ready"][h], 1)
                    between(h * 2 + part)

            def weigh(p, n, kt, between):
                for h in range(2):
                    pe.wait_ge(s["exp_done"][h], (p * 2 + n) * 8 + kt + 1)
                if kt == 0:
                    wait(pe, s["raw_out_ready"], p * 2 + n)
                for c in range(2):
                    for h in range(2):
                        last = nc.tensor.matmul(pv[HALF[h], C[c]], v[n][:, kt, HALF[h]],
                                                probs[h][:, kt % RING, C[c]], start=kt == 0, stop=kt == 7)
                    if c == 1:
                        last.then_inc(s["weighed"], 1)
                    between(4 + 2 * c)
                    between(5 + 2 * c)

            def sum_rows(u, p, n):
                for h in range(2):
                    pe.wait_ge(s["keys_added"][h], (p * 2 + n + 1) * 7)
                for c in range(2):
                    out = take(u, "sum", c)
                    for h in range(2):
                        last = nc.tensor.matmul(out[HALF[h], :], m.ones[:, HALF[h]], key_sum[n][h][:, C[c]],
                                                start=True, stop=True)
                    last.then_inc(s["shared_full"][u.bank("sum", c)], 1)

            def project_out(u, p, n):
                pe.wait_ge(s["w_out_loaded"], p * 16 + 16)
                pe.wait_ge(s["normalised"], p * 2 + n + 1)
                for c in range(2):
                    out = take(u, "proj", c)
                    nc.tensor.matmul(out[:, :], w_out[:, :], heads_out[:, C[c]], start=True, stop=True
                                     ).then_inc(s["shared_full"][u.bank("proj", c)], 1)

            def step(p, n, prepared, first=False, last=False):
                u = uses_in(p, n, first, last)
                before, after = (p - 1 + n, 1 - n), (p + n, 1 - n)
                for kt in range(8):
                    def between(place):
                        if not last:
                            find_maxima(u, kt, place, *after)
                        if not last and kt == 7 and place < 4:
                            shift_row(u, place // 2, place % 2, *after)

                    score(p, n, kt, 0, prepared, between)
                    if kt == 0 and not last:
                        project_qk(u, "q", 0, *after)
                    if kt == 2 and not last:
                        project_v(u, 0, after[1])
                    score(p, n, kt, 1, prepared, between)
                    if kt == 1 and not last:
                        project_qk(u, "k", 0, *after)
                    if kt == 2 and not last:
                        project_v(u, 1, after[1])
                    if kt > 0:
                        weigh(p, n, kt - 1, between)
                    elif not first:
                        weigh(*before, 7, between)
                    if kt < 2 and not last:
                        project_qk(u, "qk"[kt], 1, *after)
                    if kt == 2 and not first:
                        sum_rows(u, *before)
                    if kt == 7 and not first:
                        project_out(u, *before)
                return u

            pe.wait_ge(s["filled"], 1)
            for what in "qk":
                for c in range(2):
                    project_qk(prologue, what, c, 0, 0)
            for j in range(2):
                project_v(prologue, j, 0)
            for slot in MAXIMA:
                for place in range(PIECES):
                    find_maxima(prologue, slot, place, 0, 0)
            for h in range(2):
                for c in range(2):
                    shift_row(prologue, h, c, 0, 0)
            u = step(0, 0, prologue, first=True)
            step(0, 1, u)
            with pe.Fori(1, PAIRS - 1) as p:
                u = step(p, 0, uses_in(p - 1, 1))
                step(p, 1, u)
            u = step(PAIRS - 1, 0, uses_in(PAIRS - 2, 1))
            step(PAIRS - 1, 1, u, last=True)
            weigh(PAIRS - 1, 1, 7, lambda place: None)
            sum_rows(epilogue, PAIRS - 1, 1)
            project_out(epilogue, PAIRS - 1, 1)

        @block.scalar
        def _(act):
            def got(u, *name):
                act.wait_ge(s["shared_full"][u.bank(*name)], u.earlier(*name) + 1)
                return shared[u.bank(*name)]

            def leading(u, what, c, n):
                j = "qk".index(what)
                ps = got(u, what, c)
                for h in range(2):
                    to = (q_both if what == "q" else k_hi)[n][h]
                    last = nc.scalar.activation(to[HALF[h], C[c]], ps[HALF[h], :], ACT.Identity,
                                                bias=b_qk[HALF[h], j:j + 1])
                last.then_inc(s["leading_ready"], 1)

            def shift_rows(u, h, n):
                r = SHIFT_ROW[h]
                for c in range(2):
                    ps = got(u, f"row{h}", c)
                    nc.scalar.copy(q_shift[n][h][r:r + 1, C[c]], ps[r:r + 1, :]
                                   ).then_inc(s["shared_free"][u.bank(f"row{h}", c)], 1)

            def fetch_sums(u, p, n):
                wait(act, s["sum_cols_ready"], (p * 2 + n) * 32)
                for c in range(2):
                    ps = got(u, "sum", c)
                    nc.scalar.copy(row_sum[:, C[c]], ps[:, :]).then_inc(s["shared_free"][u.bank("sum", c)], 1)

            def exponentials(p, n, kt, first):
                st = p * 2 + n
                for h in range(2):
                    act.wait_ge(s["scores_ready"][h], st * 8 + kt + 1)
                    if kt >= RING or not first:
                        act.wait_ge(s["weighed"], st * 8 + kt - RING + 1)
                        act.wait_ge(s["keys_added"][h], st * 7 + (max(kt - RING, 1) if kt >= RING else kt + RING - 7))
                    nc.scalar.activation(probs[h][:, kt % RING, :], scores[h][:, :], ACT.Exp,
                                         scale=HD ** -0.5).then_inc(s["exp_done"][h], 1)

            def fetch_out(p, n):
                st = p * 2 + n
                act.wait_ge(s["weighed"], st * 8 + 8)
                wait(act, s["normalised"], st)
                nc.scalar.copy(raw_out[:, :], pv[:, :]).then_inc(s["raw_out_ready"], 1)

            def step(p, n, first=False, last=False):
                u = uses_in(p, n, first, last)
                for kt in range(8):
                    if kt == 7 and not last:
                        shift_rows(u, 0, 1 - n)
                    exponentials(p, n, kt, first)
                    if kt < 2 and not last:
                        leading(u, "qk"[kt], 0, 1 - n)
                    if kt == 0 and not first:
                        fetch_out(p - 1 + n, 1 - n)
                    if kt < 2 and not last:
                        leading(u, "qk"[kt], 1, 1 - n)
                    if kt == 2 and not first:
                        fetch_sums(u, p - 1 + n, 1 - n)
                    if kt == 7 and not last:
                        shift_rows(u, 1, 1 - n)

            act.wait_ge(s["filled"], 1)
            for what in "qk":
                for c in range(2):
                    leading(prologue, what, c, 0)
            shift_rows(prologue, 0, 0)
            shift_rows(prologue, 1, 0)
            step(0, 0, first=True)
            step(0, 1)
            with act.Fori(1, PAIRS - 1) as p:
                step(p, 0)
                step(p, 1)
            step(PAIRS - 1, 0)
            step(PAIRS - 1, 1, last=True)
            fetch_out(PAIRS - 1, 1)
            fetch_sums(epilogue, PAIRS - 1, 1)

        @block.vector
        def _(dve):
            def got(u, *name):
                dve.wait_ge(s["shared_full"][u.bank(*name)], u.earlier(*name) + 1)
                return shared[u.bank(*name)]

            def done(u, *name):
                dve.wait_ge(s["shared_free"][u.bank(*name)], u.earlier(*name) + 1)

            def remainders(u, what, p, n):
                j = "qk".index(what)
                for c in range(2):
                    ps = got(u, what, c)
                    dve.wait_ge(s["leading_ready"], (p * 2 + n) * 4 + 2 * j + c + 1)
                    for h in range(2):
                        lead = (q_both if what == "q" else k_hi)[n][h][HALF[h], C[c]]
                        to = q_both[n][h][OTHER[h], C[c]] if what == "q" else k_lo[n][h][HALF[h], C[c]]
                        last = nc.vector.scalar_tensor_tensor(out=to, in0=ps[HALF[h], :], scalar=b_qk[HALF[h], j:j + 1],
                                                              in1=lead.bitcast(F32), op0=ALU.add, op1=ALU.subtract)
                    last.then_inc(s["shared_free"][u.bank(what, c)], 1)

            def values(u, n):
                bias = b_v[:, :].unsqueeze(1).broadcast_to([P, TILES, P])
                for j in range(2):
                    ps = got(u, "v", j)
                    nc.vector.tensor_tensor(v[n][:, j * TILES:(j + 1) * TILES, :],
                                            ps[:, :].rearrange("p (t d) -> p t d", t=TILES), bias, ALU.add
                                            ).then_inc(s["shared_free"][u.bank("v", j)], 1)

            def find_maxima(u, slot):
                for i in MAXIMA[slot]:
                    h, qt, kc = i // 16, i % 16 // 2, i % 2
                    ps = got(u, "max", i)
                    nc.vector.tensor_reduce(maxima[:, h, qt, kc:kc + 1], ps[:, :], X, ALU.max
                                            ).then_inc(s["shared_free"][u.bank("max", i)], 1)
                    if i % 16 == 15:
                        done(u, "max", i - 1)
                        done(u, "max", i)
                        nc.vector.tensor_reduce(neg_max[:, h, :], maxima[:, h, :, :], X, ALU.max, negate=True
                                                ).then_inc(s["neg_max_ready"], 1)

            def invert(p, n):
                st = p * 2 + n
                dve.wait_ge(s["sum_cols_ready"], st * 32 + 32)
                wait(dve, s["inv_stored"], st * 16)
                nc.vector.reciprocal(inv_cols[:, :, :], sum_cols[:, :, :]).then_inc(s["inverted"], 1)

            def normalise(p, n):
                st = p * 2 + n
                dve.wait_ge(s["inv_sum_ready"], st * 32 + 32)
                dve.wait_ge(s["raw_out_ready"], st + 1)
                nc.vector.tensor_tensor(heads_out[:, :], raw_out[:, :], inv_sum[:, :], ALU.mult
                                        ).then_inc(s["normalised"], 1)

            def add_projection(u, n):
                for c in range(2):
                    ps = got(u, "proj", c)
                    y = m.yT[:, n * 1024 + c * BANK:n * 1024 + (c + 1) * BANK]
                    nc.vector.tensor_tensor(y, ps[:, :], y, ALU.add).then_inc(s["shared_free"][u.bank("proj", c)], 1)

            def split_weights(p):
                dve.wait_ge(s["pair_loaded"], p * 64 + 64)
                nc.vector.tensor_copy(w_hi[:, :, :], w_raw[:, :, :]).then_inc(s["w_hi_ready"], 1)
                dve.wait_ge(s["w_hi_ready"], p + 1)
                nc.vector.tensor_tensor(w_lo[:, :, :], w_raw[:, :, :], w_hi[:, :, :].bitcast(F32), ALU.subtract
                                        ).then_inc(s["w_split"], 1)

            def step(p, n, first=False, last=False):
                u = uses_in(p, n, first, last)
                before, after = (p - 1 + n, 1 - n), (p + n, 1 - n)
                for kt in range(8):
                    if kt == 4 and not first:
                        invert(*before)
                    if kt in MAXIMA and not last:
                        find_maxima(u, kt)
                    if kt == 7 and not first:
                        normalise(*before)
                        add_projection(u, before[1])
                    if last:
                        continue
                    if kt == 0:
                        remainders(u, "q", *after)
                    if kt == 1:
                        remainders(u, "k", *after)
                    if kt == 2:
                        values(u, after[1])
                    if kt == 7 and n == 0 and not (isinstance(p, int) and p == PAIRS - 1):
                        split_weights(p + 1)

            split_weights(0)
            dve.wait_ge(s["bias_loaded"], 16)
            nc.vector.memset(m.yT[:, :], 0.0).then_inc(s["yT_clear"], 1)
            dve.wait_ge(s["yT_clear"], 1)
            nc.vector.tensor_scalar(m.yT[:, :], m.yT[:, :], m.b_out[:, 0:1], None, ALU.add)
            remainders(prologue, "q", 0, 0)
            remainders(prologue, "k", 0, 0)
            values(prologue, 0)
            for slot in MAXIMA:
                find_maxima(prologue, slot)
            step(0, 0, first=True)
            step(0, 1)
            with dve.Fori(1, PAIRS - 1) as p:
                step(p, 0)
                step(p, 1)
            step(PAIRS - 1, 0)
            step(PAIRS - 1, 1, last=True)
            invert(PAIRS - 1, 1)
            normalise(PAIRS - 1, 1)
            add_projection(epilogue, 1)

        @block.gpsimd
        def _(pool):
            for b in range(2):
                nc.gpsimd.memset(q_shift[b][0][OTHER[0], :].bitcast(F32), 0.0)
                nc.gpsimd.memset(q_shift[b][1][OTHER[1], :].bitcast(F32), 0.0)
                nc.gpsimd.memset(k_lo[b][0][OTHER[0], :].bitcast(F32), 0.0)
                last = nc.gpsimd.memset(k_lo[b][1][OTHER[1], :].bitcast(F32), 0.0)
            last.then_inc(s["cleared"], 1)
            pool.wait_ge(s["cleared"], 1)
            for b in range(2):
                for h in range(2):
                    r = SHIFT_ROW[h]
                    last = nc.gpsimd.memset(k_lo[b][h][r:r + 1, :].bitcast(F32), 1.0)
            last.then_inc(s["filled"], 1)

            def step(p, n, first=False):
                st = p * 2 + n
                for kt in range(1, 8):
                    for h in range(2):
                        pool.wait_ge(s["exp_done"][h], st * 8 + kt + 1)
                        if kt == 1:
                            if not (first or (isinstance(p, int) and p == 0)):
                                pool.wait_ge(s["normalised"], st - 1)
                            a = probs[h][:, 0, :]
                        else:
                            pool.wait_ge(s["keys_added"][h], st * 7 + kt - 1)
                            a = key_sum[n][h][:, :]
                        nc.gpsimd.tensor_tensor(key_sum[n][h][:, :], a, probs[h][:, kt % RING, :], ALU.add
                                                ).then_inc(s["keys_added"][h], 1)

            step(0, 0, first=True)
            step(0, 1)
            with pool.Fori(1, PAIRS) as p:
                step(p, 0)
                step(p, 1)


class Norms:

    def __init__(self, nc, chain, carrier, var_ready, root_ready, eps, stats, mv, rstd, before):
        self.nc, self.chain, self.var_ready, self.root_ready, self.eps = nc, chain, var_ready, root_ready, eps
        self.carrier = carrier
        self.stats, self.mv, self.rstd, self.done = stats, mv, rstd, before

    def norm(self, src, out):
        nc, dve = self.nc, self.chain.eng
        nc.vector.memset(self.carrier[:, :], 0.0)
        for t, tile in enumerate(src):
            last = nc.vector.bn_stats(self.stats[:, t, :], tile)
        self.chain.link(last)
        nc.vector.memset(self.carrier[:, :], 0.0)
        for t in range(len(src)):
            last = nc.vector.bn_aggr(self.mv[:, t, :], self.stats[:, t, :])
        last.then_inc(self.var_ready, 1)
        self.done = self.done + 1
        dve.wait_ge(self.root_ready, self.done)
        self.chain.link(nc.vector.reciprocal(self.rstd[:, :], self.rstd[:, :]))
        made = []
        for t, tile in enumerate(src):
            made.append(nc.vector.tensor_scalar(out[:, t, :], tile, self.mv[:, t, 0:1], self.rstd[:, t:t + 1],
                                                ALU.subtract, ALU.mult))
        return made[TILES - 1::TILES]

    def root(self, act):
        self.done = self.done + 1
        act.wait_ge(self.var_ready, self.done)
        self.nc.scalar.activation(self.rstd[:, :], self.mv[:, :, 1], ACT.Sqrt, bias=self.eps[:, 0:1]
                                  ).then_inc(self.root_ready, 1)


EXPERTS = 8
GATE_LINKS = 14


def pick_two(nc, ch, t, logits, bias, rank, weights_wanted, weights_ready, value):
    dve = ch.eng
    shape = [P, t.tiles, EXPERTS]

    def wide(a):
        return a[:, :].unsqueeze(2).broadcast_to(shape)

    ranks = rank[:, :].unsqueeze(1).broadcast_to(shape)
    if bias is None:
        ch.link(nc.vector.tensor_copy(t.logit[:, :, :], logits))
    else:
        ch.link(nc.vector.tensor_tensor(t.logit[:, :, :], logits, bias[:, :].unsqueeze(1).broadcast_to(shape), ALU.add))

    def choose(values, best, chosen):
        ch.link(nc.vector.tensor_reduce(best[:, :], values, X, ALU.max))
        ch.link(nc.vector.tensor_tensor(t.score[:, :, :], values, wide(best), ALU.is_equal))
        ch.link(nc.vector.tensor_tensor(t.score[:, :, :], t.score[:, :, :], ranks, ALU.mult))
        ch.link(nc.vector.tensor_reduce(t.first[:, :], t.score[:, :, :], X, ALU.max))
        ch.link(nc.vector.tensor_tensor(chosen[:, :, :], t.score[:, :, :], wide(t.first), ALU.is_equal))

    choose(t.logit[:, :, :], t.best1, t.chosen1)
    ch.link(nc.vector.scalar_tensor_tensor(out=t.rest[:, :, :], in0=t.chosen1[:, :, :], scalar=LEAST,
                                           in1=t.logit[:, :, :], op0=ALU.mult, op1=ALU.add))
    choose(t.rest[:, :, :], t.best2, t.chosen2)
    nc.vector.tensor_tensor(t.gap[:, :], t.best1[:, :], t.best2[:, :], ALU.subtract).then_inc(weights_wanted, 1)
    dve.wait_ge(weights_ready, value)
    ch.link(nc.vector.tensor_tensor(t.chosen1[:, :, :], t.chosen1[:, :, :], wide(t.weight1), ALU.mult))
    ch.link(nc.vector.tensor_tensor(t.chosen2[:, :, :], t.chosen2[:, :, :], wide(t.weight2), ALU.mult))
    return nc.vector.tensor_tensor(t.gates[:, :, :], t.chosen1[:, :, :], t.chosen2[:, :, :], ALU.add)


def weigh_two(nc, act, t, weights_wanted, weights_ready, value):
    act.wait_ge(weights_wanted, value)
    nc.scalar.activation(t.weight1[:, :], t.gap[:, :], ACT.Sigmoid)
    nc.scalar.activation(t.weight2[:, :], t.gap[:, :], ACT.Sigmoid, scale=-1.0).then_inc(weights_ready, 1)


def tiles_of(a):
    return [a[:, t, :] for t in range(a.shape[1])]


def gating_buffers(sb, name, tiles):
    g = Buffers()
    g.tiles = tiles
    g.logit, g.score, g.rest, g.chosen1, g.chosen2, g.gates = (
        sb(f"{name}_{what}", [P, tiles, EXPERTS]) for what in ("logit", "score", "rest", "chosen1", "chosen2", "gates"))
    g.best1, g.best2, g.first, g.gap, g.weight1, g.weight2 = (
        sb(f"{name}_{what}", [P, tiles]) for what in ("best1", "best2", "first", "gap", "weight1", "weight2"))
    return g
M0, H0 = 64, 256
PAIR = 2 * BANK
NORMS0 = 5
LINKS0 = NORMS0 * 2 + GATE_LINKS + 2 * (EXPERTS - 1) + 5


def ffn0(nc, m, s):
    with ExitStack() as ctx:
        def sb(name, shape, dt=F32):
            return ctx.enter_context(nc.sbuf_tensor(name, shape, dt))

        enc_raw, enc_hi, enc_lo = sb("enc_raw", [P, H0]), sb("enc_hi", [P, H0], F32R), sb("enc_lo", [P, H0], F32R)
        s2c = sb("s2c", [P, 2, M0])
        r1_raw, r1_hi, r1_lo = sb("r1_raw", [P, M0]), sb("r1_hi", [P, M0], F32R), sb("r1_lo", [P, M0], F32R)
        e1_raw = sb("e1_raw", [P, EXPERTS, P])
        e1_hi, e1_lo = sb("e1_hi", [P, EXPERTS, P], F32R), sb("e1_lo", [P, EXPERTS, P], F32R)
        r2 = sb("r2", [M0, EXPERTS])
        e2 = sb("e2", [P, EXPERTS, M0])
        e2_bias = sb("e2_bias", [EXPERTS, M0])
        c2s = sb("c2s", [M0, H0])
        dec = sb("dec", [P, 2, P])
        enc_b, c2s_b = sb("enc_b", [P, 2]), sb("c2s_b", [P, 2])
        s2c_b, r1_b = sb("s2c_b", [M0, 1]), sb("r1_b", [M0, 1])
        e1_b = sb("e1_b", [P, EXPERTS])
        r2_b = sb("r2_b", [P, EXPERTS])
        dec_b, ln_g, ln_b = sb("dec_b", [P, P]), sb("ln_g", [P, P]), sb("ln_b", [P, P])
        qkv_raw, qkv_T = sb("qkv_raw", [P, 3, P]), sb("qkv_T", [P, 3, P])
        q_b, kv_b = sb("q_b", [P, 1]), sb("kv_b", [P, 2 * P])

        yT = sb("yT_pair", [P, PAIR])
        post = sb("post", [P, 2 * TILES, P])
        xn = sb("xn", [P, 2 * TILES, P])
        xT_hi, xT_lo = sb("xT_hi_pair", [P, PAIR], F32R), sb("xT_lo_pair", [P, PAIR], F32R)
        spikes = sb("spikes", [P, 2, PAIR])
        cont = sb("cont", [P, PAIR], F32R)
        router = sb("router", [M0, PAIR])
        mixed = sb("mixed0", [P, 2 * TILES, M0])
        gates_T = sb("gates_T", [EXPERTS, PAIR])
        moe = sb("moe", [M0, PAIR])
        decoded = sb("decoded", [P, 2 * TILES, P])
        xT2 = sb("xT2", [P, PAIR])
        stats, mv, rstd = sb("stats0", [P, 2 * TILES, 6]), sb("mv0", [P, 2 * TILES, 2]), sb("rstd0", [P, 2 * TILES])
        g = gating_buffers(sb, "g0", 2 * TILES)
        hidden = [sb(f"hidden0_{c}", [P, BANK]) for c in range(2)]
        part = [sb(f"part0_{c}", [P, TILES, M0]) for c in range(2)]

        def pb(name, shape):
            return ctx.enter_context(nc.psum_tensor(name, shape, F32))

        turned = [pb(f"turned0_{c}", [P, BANK]) for c in range(2)]
        narrow = [pb(f"narrow0_{c}", [P, BANK]) for c in range(2)]
        hid = [pb(f"hid0_{c}", [P, BANK]) for c in range(2)]
        eout = [pb(f"eout0_{c}", [P, BANK]) for c in range(2)]
        wide = [hid, eout]
        turned_t = [a[:, :].rearrange("p (t d) -> p t d", t=TILES) for a in turned]
        eout_t = [a[:, 0:TILES * M0].rearrange("p (t d) -> p t d", t=TILES) for a in eout]
        logits = turned[0][:, 0:2 * TILES * EXPERTS].rearrange("p (t e) -> p t e", t=2 * TILES)
        COLS = [slice(0, BANK), slice(BANK, PAIR)]
        ROWS = [slice(0, TILES), slice(TILES, 2 * TILES)]
        STEPS = 2 * EXPERTS
        LOADS = 23

        block = ctx.enter_context(nc.Block())

        @block.sync
        def _(sp):
            def load(dst, src):
                sp.dma_start(dst, src).then_inc(s["f0_loaded"], 16)

            load(enc_raw[:, :], m.inputs["enc_W"])
            load(s2c[:, :, :], m.inputs["s2c_W"].rearrange("(c p) n -> p c n", p=P))
            for half in range(2):
                rows = slice(half * M0, (half + 1) * M0)
                load(r1_raw[rows, :], m.inputs["rW1"])
                load(e1_raw[rows, :, :], m.inputs["We1"].rearrange("e m h -> m e h"))
            load(r2[:, :], m.inputs["rW2"])
            load(e2[:, :, :], m.inputs["We2"].rearrange("e h m -> h e m"))
            load(e2_bias[:, :], m.inputs["be2"])
            load(c2s[:, :], m.inputs["c2s_W"])
            load(dec[:, :, :], m.inputs["dec_W"].rearrange("(c p) n -> p c n", p=P))
            load(qkv_raw[:, :, :], m.inputs["w_qkv1"].rearrange("(c p) d -> p c d", p=P))
            load(enc_b[:, :], m.inputs["enc_b"].rearrange("(c p) -> p c", p=P))
            load(c2s_b[:, :], m.inputs["c2s_b"].rearrange("(c p) -> p c", p=P))
            load(s2c_b[:, :], m.inputs["s2c_b"].unsqueeze(1))
            load(r1_b[:, :], m.inputs["rb1"].unsqueeze(1))
            load(e1_b[:, :], m.inputs["be1"].rearrange("e p -> p e"))
            load(r2_b[:, :], m.inputs["rb2"].partition_broadcast(P))
            load(dec_b[:, :], m.inputs["dec_b"].partition_broadcast(P))
            load(ln_g[:, :], m.inputs["ln_g"].partition_broadcast(P))
            load(ln_b[:, :], m.inputs["ln_b"].partition_broadcast(P))
            load(q_b[:, :], m.inputs["b_qkv1"][0:P].unsqueeze(1))
            load(kv_b[:, :], m.inputs["b_qkv1"][P:3 * P].partition_broadcast(P))
            for e in range(EXPERTS):
                sp.dma_start(m.w1_raw[:, e, :], m.inputs["W1"][e]).then_inc(s["w1_loaded"], 16)
                sp.dma_start(m.w2[:, e, :, :], m.inputs["W2"][e].rearrange("(c p) d -> p c d", p=P)).then_inc(s["w1_loaded"], 16)

        @block.gpsimd
        def _(pool):
            nc.gpsimd.memset(e1_lo[M0:P, :, :].bitcast(F32), 0.0)
            nc.gpsimd.memset(r1_lo[M0:P, :].bitcast(F32), 0.0).then_inc(s["f0_zeros"], 1)

        @block.tensor
        def _(pe):
            pe.wait_ge(s["f0_loaded"], 16 * LOADS)
            for c in range(3):
                last = nc.tensor.transpose(turned[0][:, c * P:(c + 1) * P], qkv_raw[:, c, :], m.ident[:, :])
            last.then_inc(s["qkv_turned"], 1)
            pe.wait_ge(s["f0_zeros"], 1)
            pe.wait_ge(s["f0_split"], 1)
            pe.wait_ge(s["qkv_T_ready"], 1)
            with pe.Fori(0, 2) as i:
                def expert_hidden(k):
                    e, c = k // 2, k % 2
                    if e >= 1:
                        pe.wait_ge(s["f0_hidden"], i * STEPS + (k - 1))
                    nc.tensor.matmul(hid[c][:, :], e1_hi[:, e, :], cont[:, COLS[c]], start=True, stop=False)
                    nc.tensor.matmul(hid[c][:, :], e1_lo[:, e, :], cont[:, COLS[c]], start=False, stop=True
                                     ).then_inc(s["f0_hidden_sum"], 1)

                def expert_out(k):
                    e, c = k // 2, k % 2
                    pe.wait_ge(s["f0_hidden"], i * STEPS + (k + 1))
                    if e >= 1:
                        pe.wait_ge(s["f0_part"], i * STEPS + (k - 1))
                    for t in range(TILES):
                        last = nc.tensor.matmul(eout_t[c][:, t, :], hidden[c][:, t * P:(t + 1) * P], e2[:, e, :],
                                                start=True, stop=True)
                    last.then_inc(s["f0_eout"], 1)

                for c in range(2):
                    pe.wait_ge(s["f0_yT"], i * 2 + (c + 1))
                    for t in range(TILES):
                        last = nc.tensor.transpose(turned_t[c][:, t, :], yT[:, c * BANK + t * P:c * BANK + (t + 1) * P],
                                                   m.ident[:, :])
                    last.then_inc(s["f0_y_turned"], 1)
                for c in range(2):
                    pe.wait_ge(s["f0_xn"], i * 2 + (c + 1))
                    for t in range(TILES):
                        last = nc.tensor.transpose(turned_t[c][:, t, :], xn[:, c * TILES + t, :], m.ident[:, :])
                    last.then_inc(s["f0_x_turned"], 1)
                for c in range(2):
                    pe.wait_ge(s["f0_xT_lo"], i * 2 + (c + 1))
                    for j in range(2):
                        w, out = slice(j * P, (j + 1) * P), wide[c][j][:, :]
                        nc.tensor.matmul(out, enc_hi[:, w], xT_hi[:, COLS[c]], start=True, stop=False)
                        nc.tensor.matmul(out, enc_hi[:, w], xT_lo[:, COLS[c]], start=False, stop=False)
                        nc.tensor.matmul(out, enc_lo[:, w], xT_hi[:, COLS[c]], start=False, stop=True
                                         ).then_inc(s["f0_enc"], 1)
                for c in range(2):
                    for j in range(2):
                        pe.wait_ge(s["f0_spikes"], i * 4 + (2 * c + j + 1))
                        last = nc.tensor.matmul(narrow[c][0:M0, :], s2c[:, j, :], spikes[:, j, COLS[c]],
                                                start=j == 0, stop=j == 1)
                    last.then_inc(s["f0_cont"], 1)
                for c in range(2):
                    pe.wait_ge(s["f0_cont_lo"], i * 2 + (c + 1))
                    nc.tensor.matmul(narrow[c][0:M0, :], r1_hi[:, :], cont[:, COLS[c]], start=True, stop=False)
                    nc.tensor.matmul(narrow[c][0:M0, :], r1_lo[:, :], cont[:, COLS[c]], start=False, stop=True
                                     ).then_inc(s["f0_router"], 1)
                    expert_hidden(c)
                for c in range(2):
                    pe.wait_ge(s["f0_tanh"], i * 2 + (c + 1))
                    for t in range(TILES):
                        j = c * TILES + t
                        last = nc.tensor.matmul(logits[:, j, :], router[:, j * P:(j + 1) * P], r2[:, :],
                                                start=True, stop=True)
                last.then_inc(s["f0_logits"], 1)
                for k in range(STEPS):
                    expert_out(k)
                    if k + 2 < STEPS:
                        expert_hidden(k + 2)
                    if k in (6, 7):
                        if k == 6:
                            pe.wait_ge(s["f0_gates"], i + 1)
                        c = k - 6
                        for t in range(TILES):
                            last = nc.tensor.transpose(turned[c][0:EXPERTS, t * P:(t + 1) * P],
                                                       g.gates[:, c * TILES + t, :], m.ident[:, :])
                        last.then_inc(s["f0_gates_turned"], 1)
                    if k in (10, 11):
                        c = k - 10
                        pe.wait_ge(s["f0_gates_T"], i * 2 + (c + 1))
                        nc.tensor.matmul(narrow[c][0:M0, :], e2_bias[:, :], gates_T[:, COLS[c]], start=True,
                                         stop=False, skip_group_check=True)
                for c in range(2):
                    pe.wait_ge(s["f0_mixed"], i * 2 + (c + 1))
                    for t in range(TILES):
                        last = nc.tensor.matmul(narrow[c][0:M0, t * P:(t + 1) * P], mixed[:, c * TILES + t, :],
                                                m.ident[:, :], start=False, stop=t == TILES - 1,
                                                skip_group_check=True)
                    last.then_inc(s["f0_moe_sum"], 1)
                for c in range(2):
                    pe.wait_ge(s["f0_moe"], i * 2 + (c + 1))
                    for j in range(2):
                        nc.tensor.matmul(wide[c][j][:, :], c2s[:, j * P:(j + 1) * P], moe[:, COLS[c]],
                                         start=True, stop=True).then_inc(s["f0_enc2"], 1)
                for c in range(2):
                    pe.wait_ge(s["f0_spikes2"], i * 4 + (2 * c + 2))
                    for t in range(TILES):
                        tok = c * BANK + t * P
                        for j in range(2):
                            last = nc.tensor.matmul(turned_t[c][:, t, :], spikes[:, j, tok:tok + P], dec[:, j, :],
                                                    start=j == 0, stop=j == 1)
                    last.then_inc(s["f0_dec"], 1)
                for c in range(2):
                    pe.wait_ge(s["f0_xn2"], i * 2 + (c + 1))
                    for t in range(TILES):
                        last = nc.tensor.transpose(turned_t[c][:, t, :], xn[:, c * TILES + t, :], m.ident[:, :])
                    last.then_inc(s["f0_x2_turned"], 1)
                for c in range(2):
                    pe.wait_ge(s["f0_xT2"], i * 2 + (c + 1))
                    nc.tensor.matmul(narrow[c][:, :], qkv_T[:, 0, :], xT2[:, COLS[c]], start=True, stop=True
                                     ).then_inc(s["f0_q"], 1)
                    for t in range(TILES):
                        tok = c * BANK + t * P
                        last = nc.tensor.matmul(wide[c][t // 2][:, (t % 2) * 256:(t % 2) * 256 + 256],
                                                xT2[:, tok:tok + P],
                                                qkv_T[:, 1:3, :].rearrange("p c d -> p (c d)"), start=True, stop=True)
                        if t % 2:
                            last.then_inc(s["f0_kv"], 1)

        @block.scalar
        def _(act):
            act.wait_ge(s["qkv_turned"], 1)
            nc.scalar.copy(qkv_T[:, :, :], turned[0][:, 0:3 * P].rearrange("p (c d) -> p c d", c=3)
                           ).then_inc(s["qkv_T_ready"], 1)
            with act.Fori(0, 2) as i:
                norms = Norms(nc, None, m.carrier, s["f0_var"], s["f0_root"], m.eps, stats, mv, rstd, i * NORMS0)
                for c in range(2):
                    nc.scalar.copy(yT[:, COLS[c]], m.yT[:, bass.ds(i * PAIR + c * BANK, BANK)]).then_inc(s["f0_yT"], 1)
                norms.root(act)
                norms.root(act)
                for c in range(2):
                    act.wait_ge(s["f0_x_turned"], i * 2 + (c + 1))
                    nc.scalar.copy(xT_hi[:, COLS[c]], turned[c][:, :]).then_inc(s["f0_xT_hi"], 1)
                for c in range(2):
                    for j in range(2):
                        act.wait_ge(s["f0_enc"], i * 4 + (2 * c + j + 1))
                        nc.scalar.activation(spikes[:, j, COLS[c]], wide[c][j][:, :], ACT.Sigmoid,
                                             bias=enc_b[:, j:j + 1]).then_inc(s["f0_spikes"], 1)
                for c in range(2):
                    act.wait_ge(s["f0_cont"], i * 2 + (c + 1))
                    nc.scalar.activation(cont[0:M0, COLS[c]], narrow[c][0:M0, :], ACT.Identity, bias=s2c_b[:, 0:1]
                                         ).then_inc(s["f0_cont_hi"], 1)
                for c in range(2):
                    act.wait_ge(s["f0_router"], i * 2 + (c + 1))
                    nc.scalar.activation(router[:, COLS[c]], narrow[c][0:M0, :], ACT.Tanh, bias=r1_b[:, 0:1]
                                         ).then_inc(s["f0_tanh"], 1)
                for k in range(STEPS):
                    e, c = k // 2, k % 2
                    act.wait_ge(s["f0_hidden_sum"], i * STEPS + (k + 1))
                    if e >= 1:
                        act.wait_ge(s["f0_eout"], i * STEPS + (k - 1))
                    nc.scalar.activation(hidden[c][:, :], hid[c][:, :], ACT.Relu, bias=e1_b[:, e:e + 1]
                                         ).then_inc(s["f0_hidden"], 1)
                    if k == 1:
                        weigh_two(nc, act, g, s["f0_gap"], s["f0_weights"], i + 1)
                    if k in (8, 9):
                        c = k - 8
                        act.wait_ge(s["f0_gates_turned"], i * 2 + (c + 1))
                        nc.scalar.copy(gates_T[:, COLS[c]], turned[c][0:EXPERTS, :]).then_inc(s["f0_gates_T"], 1)
                for c in range(2):
                    act.wait_ge(s["f0_moe_sum"], i * 2 + (c + 1))
                    nc.scalar.copy(moe[:, COLS[c]], narrow[c][0:M0, :]).then_inc(s["f0_moe"], 1)
                for c in range(2):
                    for j in range(2):
                        act.wait_ge(s["f0_enc2"], i * 4 + (2 * c + j + 1))
                        nc.scalar.activation(spikes[:, j, COLS[c]], wide[c][j][:, :], ACT.Sigmoid,
                                             bias=c2s_b[:, j:j + 1]).then_inc(s["f0_spikes2"], 1)
                for c in range(2):
                    act.wait_ge(s["f0_dec_sum"], i * 2 + (c + 1))
                    nc.scalar.activation(decoded[:, ROWS[c], :], decoded[:, ROWS[c], :], ACT.Sigmoid
                                         ).then_inc(s["f0_decoded"], 1)
                norms.root(act)
                norms.root(act)
                norms.root(act)
                for c in range(2):
                    act.wait_ge(s["f0_x2_turned"], i * 2 + (c + 1))
                    nc.scalar.copy(xT2[:, COLS[c]], turned[c][:, :]).then_inc(s["f0_xT2"], 1)
                for c in range(2):
                    act.wait_ge(s["f0_q"], i * 2 + (c + 1))
                    nc.scalar.activation(m.qT[:, bass.ds(i * PAIR + c * BANK, BANK)], narrow[c][:, :], ACT.Identity,
                                         bias=q_b[:, 0:1]).then_inc(s["f0_qT"], 1)

        @block.vector
        def _(dve):
            dve.wait_ge(s["f0_loaded"], 16 * LOADS)
            nc.vector.tensor_copy(enc_hi[:, :], enc_raw[:, :])
            nc.vector.tensor_copy(r1_hi[:, :], r1_raw[:, :])
            nc.vector.tensor_copy(e1_hi[:, :, :], e1_raw[:, :, :]).then_inc(s["f0_w_hi"], 1)
            for e in range(EXPERTS):
                nc.vector.memset(m.rank[:, e:e + 1], float(EXPERTS - e))
            dve.wait_ge(s["f0_w_hi"], 1)
            nc.vector.tensor_tensor(enc_lo[:, :], enc_raw[:, :], enc_hi[:, :].bitcast(F32), ALU.subtract)
            nc.vector.tensor_tensor(r1_lo[0:M0, :], r1_raw[0:M0, :], r1_hi[0:M0, :].bitcast(F32), ALU.subtract)
            nc.vector.tensor_tensor(e1_lo[0:M0, :, :], e1_raw[0:M0, :, :], e1_hi[0:M0, :, :].bitcast(F32), ALU.subtract
                                    ).then_inc(s["f0_split"], 1)
            dve.wait_ge(s["f0_split"], 1)
            with dve.Fori(0, 2) as i:
                ch = Chain(dve, s["f0_dve"], i * LINKS0)
                norms = Norms(nc, ch, m.carrier, s["f0_var"], s["f0_root"], m.eps, stats, mv, rstd, i * NORMS0)
                x = m.x[:, bass.ts(i, 2 * TILES), :]
                x_tiles = [m.x[:, bass.ds(i * (2 * TILES) + t, 1), :].rearrange("p a d -> p (a d)")
                           for t in range(2 * TILES)]

                def over_rows(row):
                    return row[:, :].unsqueeze(1).broadcast_to([P, 2 * TILES, P])

                dve.wait_ge(s["f0_y_turned"], i * 2 + 2)
                ch.link(norms.norm([tile for c in range(2) for tile in tiles_of(turned_t[c])], post)[-1])
                ch.link(nc.vector.tensor_tensor(x, x, post[:, :, :], ALU.add))
                for last in norms.norm(x_tiles, xn):
                    last.then_inc(s["f0_xn"], 1)
                for c in range(2):
                    dve.wait_ge(s["f0_x_turned"], i * 2 + (c + 1))
                    dve.wait_ge(s["f0_xT_hi"], i * 2 + (c + 1))
                    nc.vector.tensor_tensor(xT_lo[:, COLS[c]], turned[c][:, :], xT_hi[:, COLS[c]].bitcast(F32),
                                            ALU.subtract).then_inc(s["f0_xT_lo"], 1)
                for c in range(2):
                    dve.wait_ge(s["f0_cont_hi"], i * 2 + (c + 1))
                    nc.vector.scalar_tensor_tensor(out=cont[M0:P, COLS[c]], in0=narrow[c][0:M0, :],
                                                   scalar=s2c_b[:, 0:1], in1=cont[0:M0, COLS[c]].bitcast(F32),
                                                   op0=ALU.add, op1=ALU.subtract).then_inc(s["f0_cont_lo"], 1)
                dve.wait_ge(s["f0_logits"], i + 1)
                pick_two(nc, ch, g, logits, r2_b, m.rank, s["f0_gap"], s["f0_weights"], i + 1).then_inc(s["f0_gates"], 1)
                dve.wait_ge(s["f0_gates"], i + 1)
                for k in range(STEPS):
                    e, c = k // 2, k % 2
                    gate = g.gates[:, ROWS[c], e:e + 1].broadcast_to([P, TILES, M0])
                    dve.wait_ge(s["f0_eout"], i * STEPS + (k + 1))
                    to = part[c][:, :, :] if e else mixed[:, ROWS[c], :]
                    nc.vector.tensor_tensor(to, eout_t[c], gate, ALU.mult).then_inc(s["f0_part"], 1)
                    if e:
                        dve.wait_ge(s["f0_part"], i * STEPS + (k + 1))
                        ins = nc.vector.tensor_tensor(mixed[:, ROWS[c], :], mixed[:, ROWS[c], :], part[c][:, :, :],
                                                      ALU.add)
                        if e < EXPERTS - 1:
                            ch.link(ins)
                        else:
                            ins.then_inc(s["f0_mixed"], 1)
                for c in range(2):
                    dve.wait_ge(s["f0_dec"], i * 2 + (c + 1))
                    nc.vector.tensor_tensor(decoded[:, ROWS[c], :], turned_t[c],
                                            dec_b[:, :].unsqueeze(1).broadcast_to([P, TILES, P]), ALU.add
                                            ).then_inc(s["f0_dec_sum"], 1)
                dve.wait_ge(s["f0_decoded"], i * 2 + 2)
                ch.link(norms.norm(tiles_of(decoded), post)[-1])
                ch.link(nc.vector.tensor_tensor(post[:, :, :], post[:, :, :], over_rows(ln_g), ALU.mult))
                ch.link(nc.vector.tensor_tensor(post[:, :, :], post[:, :, :], over_rows(ln_b), ALU.add))
                ch.link(norms.norm(tiles_of(post), decoded)[-1])
                ch.link(nc.vector.tensor_tensor(x, x, decoded[:, :, :], ALU.add))
                for last in norms.norm(x_tiles, xn):
                    last.then_inc(s["f0_xn2"], 1)
                assert ch.n == LINKS0, (ch.n, LINKS0)
                for c in range(2):
                    for j in range(2):
                        dve.wait_ge(s["f0_kv"], i * 4 + (2 * c + j + 1))
                        nc.vector.tensor_tensor(m.kv[:, bass.ds(i * (2 * TILES) + (4 * c + 2 * j), 2), :],
                                                wide[c][j][:, :].rearrange("p (t d) -> p t d", t=2),
                                                kv_b[:, :].unsqueeze(1).broadcast_to([P, 2, 2 * P]), ALU.add
                                                ).then_inc(s["f0_kv_read"], 1)


D1 = P
DH1 = 16
HEADS1 = 8


def linear_attention(nc, m, s):
    with ExitStack() as ctx:
        w_raw = ctx.enter_context(nc.sbuf_tensor("wo_raw", [P, P], F32))
        w_ordered = ctx.enter_context(nc.sbuf_tensor("wo_ordered", [P, P], F32))
        w_T = ctx.enter_context(nc.sbuf_tensor("wo_T", [P, P], F32))
        same_head = ctx.enter_context(nc.sbuf_tensor("same_head", [P, HEADS1], F32))
        vk = ctx.enter_context(nc.sbuf_tensor("vk", [P, 2, P], F32))
        turned = ctx.enter_context(nc.psum_tensor("wo_turned", [P, P], F32))
        vk_sum = [ctx.enter_context(nc.psum_tensor(f"vk_sum{b}", [P, P], F32)) for b in range(2)]
        mix = [ctx.enter_context(nc.psum_tensor(f"mix{b}", [P, P], F32)) for b in range(2)]
        block = ctx.enter_context(nc.Block())

        @block.sync
        def _(sp):
            sp.dma_start(w_raw[:, :], m.inputs["w_o1"]).then_inc(s["wo_loaded"], 16)

        @block.tensor
        def _(pe):
            for b in range(2):
                for t in range(8):
                    kv = m.kv[:, b * 8 + t, :]
                    last = nc.tensor.matmul(vk_sum[b][:, :], kv[:, P:2 * P], kv[:, 0:P], start=t == 0, stop=t == 7)
                last.then_inc(s["vk_summed"], 1)
            pe.wait_ge(s["wo_ordered"], 1)
            nc.tensor.transpose(turned[:, :], w_ordered[:, :], m.ident[:, :]).then_inc(s["wo_turned"], 1)
            pe.wait_ge(s["wo_ready"], 1)
            for b in range(2):
                pe.wait_ge(s["vk_masked"], b + 1)
                nc.tensor.matmul(mix[b][:, :], vk[:, b, :], w_T[:, :], start=True, stop=True).then_inc(s["mixed1"], 1)

        @block.scalar
        def _(act):
            act.wait_ge(s["wo_turned"], 1)
            nc.scalar.copy(w_T[:, :], turned[:, :]).then_inc(s["wo_ready"], 1)

        @block.vector
        def _(dve):
            dve.wait_ge(s["wo_loaded"], 16)
            nc.vector.tensor_copy(w_ordered[:, :].rearrange("p (d h) -> p d h", h=HEADS1),
                                  w_raw[:, :].rearrange("p (h d) -> p d h", h=HEADS1)).then_inc(s["wo_ordered"], 1)
            nc.vector.tensor_reduce(same_head[:, :], m.ident[:, :].rearrange("p (d h) -> p h d", h=HEADS1), X, ALU.add
                                    ).then_inc(s["same_head"], 1)
            dve.wait_ge(s["same_head"], 1)
            for b in range(2):
                dve.wait_ge(s["vk_summed"], b + 1)
                nc.vector.tensor_tensor(vk[:, b, :].rearrange("p (d h) -> p d h", h=HEADS1),
                                        vk_sum[b][:, :].rearrange("p (d h) -> p d h", h=HEADS1),
                                        same_head[:, :].unsqueeze(1).broadcast_to([P, DH1, HEADS1]), ALU.mult
                                        ).then_inc(s["vk_masked"], 1)
            for b in range(2):
                dve.wait_ge(s["mixed1"], b + 1)
                for c in range(2):
                    last = nc.vector.tensor_copy(m.mix[:, b * 2 + c, :], mix[b][:, :])
            last.then_inc(s["mix_ready"], 1)


H1 = 512
HC = H1 // P
NORMS1 = 2
FRONT_LINKS = NORMS1 * 2 + GATE_LINKS + 3
EXPERT_LINKS = EXPERTS
TAIL_LINKS = 3


def ffn1(nc, m, s):
    with ExitStack() as ctx:
        def sb(name, shape, dt=F32):
            return ctx.enter_context(nc.sbuf_tensor(name, shape, dt))

        w1_hi, w1_lo = sb("w1_hi", [P, EXPERTS, H1], F32R), sb("w1_lo", [P, EXPERTS, H1], F32R)
        b1 = sb("b1", [P, EXPERTS, HC])
        b2 = sb("b2", [EXPERTS, P])
        wr = sb("wr", [P, EXPERTS])
        bo = sb("bo", [P, P])
        qT = sb("qT_chunk", [P, BANK])
        post = sb("post1", [P, TILES, P])
        xn = sb("xn1", [P, TILES, P])
        xT = sb("xT1", [P, BANK])
        hidden = [sb(f"hidden1_{b}", [P, BANK]) for b in range(HC)]
        part = sb("part1", [P, TILES, P])
        mixed = sb("mixed1", [P, TILES, P])
        final = sb("final", [P, TILES, P])
        gates = sb("gates_in_use", [P, TILES, EXPERTS])
        gates_T = sb("gates_T1", [EXPERTS, BANK])
        stats, mv, rstd = sb("stats1", [P, TILES, 6]), sb("mv1", [P, TILES, 2]), sb("rstd1", [P, TILES])
        g = gating_buffers(sb, "g1", TILES)

        def pb(name, shape):
            return ctx.enter_context(nc.psum_tensor(name, shape, F32))

        turned = pb("turned1", [P, BANK])
        small = pb("small1", [P, BANK])
        hid = [pb(f"hid1_{b}", [P, BANK]) for b in range(4)]
        eout = [pb(f"eout1_{b}", [P, BANK]) for b in range(2)]
        turned_t = turned[:, :].rearrange("p (t d) -> p t d", t=TILES)
        eout_t = [e[:, :].rearrange("p (t d) -> p t d", t=TILES) for e in eout]
        logits = small[:, 0:TILES * EXPERTS].rearrange("p (t e) -> p t e", t=TILES)
        CHUNKS = 4
        STEPS = EXPERTS * HC
        block = ctx.enter_context(nc.Block())

        def chunk_cols(a, i):
            return a[:, bass.ts(i, BANK)]

        @block.sync
        def _(sp):
            sp.dma_start(b1[:, :, :], m.inputs["b1"].rearrange("e (c p) -> p e c", p=P)).then_inc(s["f1_loaded"], 16)
            with sp.Fori(0, CHUNKS) as i:
                sp.wait_ge(s["f1_x_out"], i + 1)
                sp.dma_start(m.out_tiles[:, bass.ts(i, TILES), :], m.x[:, bass.ts(i, TILES), :]).then_inc(s["stored"], 16)
            sp.wait_ge(s["stored"], 16 * CHUNKS)

        @block.gpsimd
        def _(pool):
            for dst, src in ((bo[:, :], m.inputs["b_o1"].partition_broadcast(P)), (wr[:, :], m.inputs["Wr"]), (b2[:, :], m.inputs["b2"])):
                pool.dma_start(dst, src).then_inc(s["f1_small_loaded"], 16)
            for e in range(EXPERTS):
                pool.wait_ge(s["w1_hi_ready"], e + 1)
                nc.gpsimd.tensor_tensor(w1_lo[:, e, :], m.w1_raw[:, e, :], w1_hi[:, e, :].bitcast(F32), ALU.subtract
                                        ).then_inc(s["w1_split"], 1)
            pool.wait_ge(s["f1_small_loaded"], 48)

        @block.tensor
        def _(pe):
            def attended(i):
                pe.wait_ge(s["f1_qT"], i + 1)
                for t in range(TILES):
                    last = nc.tensor.matmul(turned_t[:, t, :], qT[:, t * P:(t + 1) * P],
                                            m.mix[:, bass.ds(i, 1), :].rearrange("p a d -> p (a d)"),
                                            start=True, stop=True)
                last.then_inc(s["f1_attended"], 1)

            def turn_x(i):
                pe.wait_ge(s["f1_xn"], i + 1)
                for t in range(TILES):
                    last = nc.tensor.transpose(turned_t[:, t, :], xn[:, t, :], m.ident[:, :])
                last.then_inc(s["f1_x_turned"], 1)

            def route(i):
                pe.wait_ge(s["f1_xT_lo"], i + 1)
                for t in range(TILES):
                    last = nc.tensor.matmul(logits[:, t, :], xT[:, t * P:(t + 1) * P], wr[:, :], start=True, stop=True)
                last.then_inc(s["f1_logits"], 1)

            def turn_gates(i):
                pe.wait_ge(s["f1_gates"], i + 1)
                for t in range(TILES):
                    last = nc.tensor.transpose(small[0:EXPERTS, t * P:(t + 1) * P], g.gates[:, t, :], m.ident[:, :])
                last.then_inc(s["f1_gates_turned"], 1)

            def bias(i):
                pe.wait_ge(s["f1_gates_T"], i + 1)
                for t in range(TILES):
                    last = nc.tensor.matmul(turned_t[:, t, :], gates_T[:, t * P:(t + 1) * P], b2[:, :],
                                            start=True, stop=True)
                last.then_inc(s["f1_bias"], 1)

            def expert_hidden(i, k):
                e, c = k // HC, k % HC
                if k >= 4 or not (isinstance(i, int) and i == 0):
                    pe.wait_ge(s["f1_hidden"], i * STEPS + (k - 3))
                cols = slice(c * P, (c + 1) * P)
                nc.tensor.matmul(hid[c][:, :], w1_hi[:, e, cols], chunk_cols(m.xT_hi, i), start=True, stop=False)
                nc.tensor.matmul(hid[c][:, :], w1_hi[:, e, cols], chunk_cols(m.xT_lo, i), start=False, stop=False)
                nc.tensor.matmul(hid[c][:, :], w1_lo[:, e, cols], chunk_cols(m.xT_hi, i), start=False, stop=True
                                 ).then_inc(s["f1_hidden_sum"], 1)

            def expert_out(i, k):
                e, c = k // HC, k % HC
                pe.wait_ge(s["f1_hidden"], i * STEPS + (k + 1))
                if c == 0 and (e >= 2 or not (isinstance(i, int) and i == 0)):
                    pe.wait_ge(s["f1_part"], i * EXPERTS + (e - 1))
                for t in range(TILES):
                    last = nc.tensor.matmul(eout_t[e % 2][:, t, :], hidden[c][:, t * P:(t + 1) * P],
                                            m.w2[:, e, c, :], start=c == 0 and t == 0, stop=c == HC - 1,
                                            skip_group_check=True)
                last.then_inc(s["f1_eout"], 1)

            def experts(i, last=False):
                for k in range(STEPS):
                    e, c = k // HC, k % HC
                    if isinstance(i, int) and i == 0 and c == 0:
                        pe.wait_ge(s["w1_split"], e + 1)
                    if not last:
                        if (e, c) == (2, 0):
                            pe.wait_ge(s["f1_biased"], i + 1)
                            attended(i + 1)
                        if (e, c) == (5, 0):
                            turn_x(i + 1)
                        if (e, c) == (6, 0):
                            route(i + 1)
                    expert_hidden(i, k)
                    if k == 0:
                        turn_gates(i)
                    if k == 2:
                        bias(i)
                    if k >= 2:
                        expert_out(i, k - 2)
                for k in (STEPS - 2, STEPS - 1):
                    expert_out(i, k)

            pe.wait_ge(s["f1_small_loaded"], 48)
            attended(0)
            turn_x(0)
            route(0)
            experts(0)
            with pe.Fori(1, CHUNKS - 1) as i:
                experts(i)
            experts(CHUNKS - 1, last=True)

        @block.scalar
        def _(act):
            def norms_of(i):
                return Norms(nc, None, m.carrier, s["f1_var"], s["f1_root"], m.eps, stats, mv, rstd, i)

            def take_q(i):
                if not (isinstance(i, int) and i == 0):
                    act.wait_ge(s["f1_attended"], i)
                nc.scalar.copy(qT[:, :], chunk_cols(m.qT, i)).then_inc(s["f1_qT"], 1)

            def take_x(i):
                act.wait_ge(s["f1_x_turned"], i + 1)
                nc.scalar.copy(xT[:, :], turned[:, :])
                nc.scalar.copy(chunk_cols(m.xT_hi, i), turned[:, :]).then_inc(s["f1_xT_hi"], 1)

            def take_gates(i):
                act.wait_ge(s["f1_gates_turned"], i + 1)
                nc.scalar.copy(gates_T[:, :], small[0:EXPERTS, :]).then_inc(s["f1_gates_T"], 1)

            def experts(i, first=False, last=False):
                norms = norms_of(NORMS1 if first else i * (NORMS1 + 1) + (NORMS1 - 1))
                for k in range(STEPS):
                    e, c = k // HC, k % HC
                    act.wait_ge(s["f1_hidden_sum"], i * STEPS + (k + 1))
                    if k >= HC or not first:
                        act.wait_ge(s["f1_eout"], i * STEPS + (k - HC + 1))
                    nc.scalar.activation(hidden[c][:, :], hid[c][:, :], ACT.Gelu, bias=b1[:, e, c:c + 1]
                                         ).then_inc(s["f1_hidden"], 1)
                    if k == 0:
                        take_gates(i)
                    if k == 1 and not first:
                        norms.root(act)
                    if last:
                        continue
                    if (e, c) == (1, 3):
                        take_q(i + 1)
                    if (e, c) in ((2, 3), (3, 3)):
                        norms.root(act)
                    if (e, c) == (5, 0):
                        take_x(i + 1)
                    if (e, c) == (6, 3):
                        weigh_two(nc, act, g, s["f1_gap"], s["f1_weights"], i + 2)

            take_q(0)
            for e in range(EXPERTS):
                act.wait_ge(s["w1_loaded"], 32 * EXPERTS)
                nc.scalar.copy(w1_hi[:, e, :], m.w1_raw[:, e, :]).then_inc(s["w1_hi_ready"], 1)
            norms = norms_of(0)
            norms.root(act)
            norms.root(act)
            take_x(0)
            weigh_two(nc, act, g, s["f1_gap"], s["f1_weights"], 1)
            act.wait_ge(s["f1_loaded"], 16)
            experts(0, first=True)
            with act.Fori(1, CHUNKS - 1) as i:
                experts(i)
            experts(CHUNKS - 1, last=True)
            norms_of(CHUNKS * (NORMS1 + 1) - 1).root(act)

        @block.vector
        def _(dve):
            def norms_of(ch, before):
                return Norms(nc, ch, m.carrier, s["f1_var"], s["f1_root"], m.eps, stats, mv, rstd, before)

            def x_of(i):
                return m.x[:, bass.ts(i, TILES), :]

            def x_tiles(i):
                return [m.x[:, bass.ds(i * TILES + t, 1), :].rearrange("p a d -> p (a d)") for t in range(TILES)]

            def add_attention(i, ch, norms):
                dve.wait_ge(s["f1_attended"], i + 1)
                ch.link(nc.vector.tensor_tensor(post[:, :, :], turned_t,
                                                bo[:, :].unsqueeze(1).broadcast_to([P, TILES, P]), ALU.add))
                ch.link(norms.norm(tiles_of(post), xn)[-1])
                ch.link(nc.vector.tensor_tensor(x_of(i), x_of(i), xn[:, :, :], ALU.add))

            def normalise(i, norms):
                norms.norm(x_tiles(i), xn)[-1].then_inc(s["f1_xn"], 1)

            def split_x(i):
                dve.wait_ge(s["f1_x_turned"], i + 1)
                dve.wait_ge(s["f1_xT_hi"], i + 1)
                nc.vector.tensor_tensor(chunk_cols(m.xT_lo, i), turned[:, :], chunk_cols(m.xT_hi, i).bitcast(F32),
                                        ALU.subtract).then_inc(s["f1_xT_lo"], 1)

            def find_gates(i, ch):
                dve.wait_ge(s["f1_logits"], i + 1)
                pick_two(nc, ch, g, logits, None, m.rank, s["f1_gap"], s["f1_weights"], i + 1).then_inc(s["f1_gates"], 1)
                assert ch.n == FRONT_LINKS, (ch.n, FRONT_LINKS)

            def tail(i, before):
                ch = Chain(dve, s["f1_tail"], i * TAIL_LINKS)
                norms = norms_of(ch, before)
                ch.link(norms.norm(tiles_of(mixed), final)[-1])
                nc.vector.tensor_tensor(x_of(i), x_of(i), final[:, :, :], ALU.add).then_inc(s["f1_x_out"], 1)
                assert ch.n == TAIL_LINKS, (ch.n, TAIL_LINKS)

            def experts(i, first=False, last=False):
                norms_before = NORMS1 if first else i * (NORMS1 + 1) + (NORMS1 - 1)
                if not first:
                    tail(i - 1, norms_before)
                    norms_before = norms_before + 1
                ch = Chain(dve, s["f1_dve"], i * EXPERT_LINKS)
                dve.wait_ge(s["f1_gates"], i + 1)
                ch.link(nc.vector.tensor_copy(gates[:, :, :], g.gates[:, :, :]))
                front = None if last else Chain(dve, s["f1_front"], (i + 1) * FRONT_LINKS)
                norms = norms_of(front, norms_before)
                for e in range(EXPERTS):
                    gate = gates[:, :, e:e + 1].broadcast_to([P, TILES, P])
                    dve.wait_ge(s["f1_eout"], i * STEPS + (e + 1) * HC)
                    nc.vector.tensor_tensor(part[:, :, :], eout_t[e % 2], gate, ALU.mult).then_inc(s["f1_part"], 1)
                    dve.wait_ge(s["f1_part"], i * EXPERTS + (e + 1))
                    if e == 0:
                        dve.wait_ge(s["f1_bias"], i + 1)
                        nc.vector.tensor_tensor(mixed[:, :, :], turned_t, part[:, :, :], ALU.add
                                                ).then_inc(s["f1_biased"], 1)
                        dve.wait_ge(s["f1_biased"], i + 1)
                    else:
                        ch.link(nc.vector.tensor_tensor(mixed[:, :, :], mixed[:, :, :], part[:, :, :], ALU.add))
                    if last:
                        continue
                    if e == 1:
                        add_attention(i + 1, front, norms)
                    if e == 2:
                        normalise(i + 1, norms)
                    if e == 4:
                        split_x(i + 1)
                    if e == 5:
                        find_gates(i + 1, front)
                assert ch.n == EXPERT_LINKS, (ch.n, EXPERT_LINKS)

            dve.wait_ge(s["f1_small_loaded"], 48)
            front = Chain(dve, s["f1_front"])
            norms = norms_of(front, 0)
            add_attention(0, front, norms)
            normalise(0, norms)
            split_x(0)
            find_gates(0, front)
            experts(0, first=True)
            with dve.Fori(1, CHUNKS - 1) as i:
                experts(i)
            experts(CHUNKS - 1, last=True)
            tail(CHUNKS - 1, CHUNKS * (NORMS1 + 1) - 1)


INPUTS = ["L0_attn_data", "L0_attn_W_qkv", "L0_attn_b_qkv", "L0_attn_W_out", "L0_attn_b_out",
          "L0_ffn_enc_W", "L0_ffn_enc_b", "L0_ffn_s2c_W", "L0_ffn_s2c_b", "L0_ffn_rW1", "L0_ffn_rb1", "L0_ffn_rW2",
          "L0_ffn_rb2", "L0_ffn_We1", "L0_ffn_be1", "L0_ffn_We2", "L0_ffn_be2", "L0_ffn_c2s_W", "L0_ffn_c2s_b",
          "L0_ffn_dec_W", "L0_ffn_dec_b", "L0_ffn_ln_g", "L0_ffn_ln_b",
          "L1_attn_w_qkv", "L1_attn_b_qkv", "L1_attn_w_o", "L1_attn_b_o",
          "L1_ffn_Wr", "L1_ffn_W1", "L1_ffn_b1", "L1_ffn_W2", "L1_ffn_b2"]
SHORT = ["data", "W_qkv", "b_qkv", "W_out", "b_out_row", "enc_W", "enc_b", "s2c_W", "s2c_b", "rW1", "rb1", "rW2", "rb2",
         "We1", "be1", "We2", "be2", "c2s_W", "c2s_b", "dec_W", "dec_b", "ln_g", "ln_b",
         "w_qkv1", "b_qkv1", "w_o1", "b_o1", "Wr", "W1", "b1", "W2", "b2"]


SEMAPHORES = """
bias_loaded cleared em_dve em_hi em_lo em_sqrt em_turned em_var em_xn eps_ready f0_cont f0_cont_hi f0_cont_lo
f0_dec f0_dec_sum f0_decoded f0_dve f0_enc f0_enc2 f0_eout f0_gap f0_gates f0_gates_T f0_gates_turned
f0_hidden f0_hidden_sum f0_kv f0_kv_read f0_loaded f0_logits f0_mixed f0_moe f0_moe_sum f0_part f0_q f0_qT
f0_root f0_router f0_spikes f0_spikes2 f0_split f0_tanh f0_var f0_w_hi f0_weights f0_x2_turned f0_xT2 f0_xT_hi
f0_xT_lo f0_x_turned f0_xn f0_xn2 f0_yT f0_y_turned f0_zeros f1_attended f1_bias f1_biased f1_dve f1_eout
f1_front f1_gap f1_gates f1_gates_T f1_gates_turned f1_hidden f1_hidden_sum f1_loaded f1_logits f1_part f1_qT
f1_root f1_small_loaded f1_tail f1_var f1_weights f1_xT_hi f1_xT_lo f1_x_out f1_x_turned f1_xn filled ident0
ident_ready inv_stored inv_sum_ready inverted leading_copied leading_ready mix_ready mixed1 neg_max_ready
normalised pair_loaded qkv_T_ready qkv_turned raw_out_ready same_head stored sum_cols_ready vk_masked
vk_summed w1_hi_ready w1_loaded w1_split w_hi_ready w_out_loaded w_split weighed wo_loaded wo_ordered wo_ready
wo_turned yT_clear
""".split()
SEMAPHORE_LISTS = {'x_loaded': 4, 'shared_free': 2, 'shared_full': 2, 'exp_done': 2, 'scores_ready': 2, 'keys_added': 2}


def build(nc, inputs, out):
    m = Buffers()
    m.inputs = inputs
    m.out_tiles = out.rearrange("n (t p) d -> p (n t) d", p=P)
    with ExitStack() as ctx:
        def sb(name, shape, dt=F32):
            return ctx.enter_context(nc.sbuf_tensor(name, shape, dt))

        ctx.enter_context(nc.allow_non_contiguous_dma(reason="biases as columns"))
        s = {name: ctx.enter_context(nc.semaphore(name)) for name in SEMAPHORES}
        for name, count in SEMAPHORE_LISTS.items():
            s[name] = [ctx.enter_context(nc.semaphore(f"{name}{i}")) for i in range(count)]
        m.x = sb("x", [P, 16, P])
        m.xT = sb("xT", [P, 2048])
        m.xT_hi = sb("xT_hi", [P, 2048], F32R)
        m.xT_lo = sb("xT_lo", [P, 2048], F32R)
        m.yT = sb("yT", [P, 2048])
        m.kv = sb("kv", [P, 16, 2 * P])
        m.mix = sb("mix", [P, 4, P])
        m.qT = m.xT
        m.ident, m.ident_bf = sb("ident", [P, P]), sb("ident_bf", [P, P], BF16)
        m.ones, m.eps, m.rank = sb("ones", [P, P]), sb("eps", [P, 1]), sb("rank", [P, EXPERTS])
        m.b_out, m.carrier = sb("b_out", [P, 1]), sb("carrier", [P, 1])
        embed(nc, m, s)
        attention(nc, m, s)
        m.w1_raw = sb("w1_raw", [P, EXPERTS, H1])
        m.w2 = sb("w2", [P, EXPERTS, HC, P])
        ffn0(nc, m, s)
        linear_attention(nc, m, s)
        ffn1(nc, m, s)


def kernel(**inputs):
    import numpy as _np
    import concourse.bacc as _bacc
    from concourse.bass_utils import run_bass_kernel_spmd as _run

    nc = _bacc.Bacc("TRN2", target_bir_lowering=False, num_devices=1)
    arrays, args = {}, {}
    for name, short in zip(INPUTS, SHORT):
        a = _np.ascontiguousarray(inputs[name])
        arrays[f"in_{name}_dram"] = a
        args[short] = nc.dram_tensor(f"in_{name}_dram", a.shape, mybir.dt.from_np(a.dtype), kind="ExternalInput").ap()
    out = nc.dram_tensor("out_dram", (2, 1024, P), F32, kind="ExternalOutput").ap()
    build(nc, args, out)
    r = _run(nc, [arrays], core_ids=[0])
    return r.results[0]["out_dram"]
```

```python
from contextlib import ExitStack

import concourse.bass as bass
from concourse import mybir

F32 = mybir.dt.float32
F32R = mybir.dt.float32r
BF16 = mybir.dt.bfloat16
ALU = mybir.AluOpType
ACT = mybir.ActivationFunctionType
X = mybir.AxisListType.X

P = 128
EPS = 1e-5
BANK = 512
TILES = BANK // P
LEAST = -3.0e38

HEADS, HD = 16, 64
PAIRS = HEADS // 2
RING = 4
PREP_USES = 42
POST_USES = 3
STEP_USES = PREP_USES + POST_USES
MAXIMA = {3: range(0, 8), 4: range(8, 16), 5: range(16, 24), 6: range(24, 32)}


class Buffers:
    pass


def wait(eng, sem, value):
    if not (isinstance(value, int) and value <= 0):
        eng.wait_ge(sem, value)


class Chain:

    def __init__(self, eng, sem, before=0):
        self.eng, self.sem, self.before, self.n = eng, sem, before, 0

    def link(self, ins):
        ins.then_inc(self.sem, 1)
        self.n += 1
        self.eng.wait_ge(self.sem, self.before + self.n)


def load_pair(sp, m, s, p):
    w = m.inputs["W_qkv"].rearrange("d (c n) -> d c n", c=3)
    cols = bass.ts(p, P)
    sp.dma_start(m.w_raw[:, :, :], w[:, 0:2, cols]).then_inc(s["pair_loaded"], 16)
    sp.dma_start(m.w_v[:, :], w[:, 2, cols]).then_inc(s["pair_loaded"], 16)
    sp.dma_start(m.b_qk[:, :], m.inputs["b_qkv"].rearrange("(c n) -> n c", c=3)[cols, 0:2]).then_inc(s["pair_loaded"], 16)
    sp.dma_start(m.b_v[:, :], m.inputs["b_qkv"][bass.ds(p * P + 2 * HEADS * HD, P)].partition_broadcast(P)
                 ).then_inc(s["pair_loaded"], 16)


def embed(nc, m, s):
    with ExitStack() as ctx:
        stats = ctx.enter_context(nc.sbuf_tensor("em_stats", [P, TILES, 6], F32))
        mv = ctx.enter_context(nc.sbuf_tensor("em_mv", [P, 4, TILES, 2], F32))
        rstd = ctx.enter_context(nc.sbuf_tensor("em_rstd", [P, 4, TILES], F32))
        xn = ctx.enter_context(nc.sbuf_tensor("em_xn", [P, 4, TILES, P], F32))
        turned = [ctx.enter_context(nc.psum_tensor(f"em_turned{c}", [P, BANK], F32)) for c in range(4)]
        block = ctx.enter_context(nc.Block())

        @block.sync
        def _(sp):
            sp.dma_start(m.b_out[:, :], m.inputs["b_out_row"].unsqueeze(1)).then_inc(s["bias_loaded"], 16)
            for c in range(4):
                n, t0 = c // 2, (c % 2) * TILES
                sp.dma_start(m.x[:, c * TILES:(c + 1) * TILES, :],
                             m.inputs["data"][n].rearrange("(t p) d -> p t d", p=P)[:, t0:t0 + TILES, :]
                             ).then_inc(s["x_loaded"][c], 16)
            load_pair(sp, m, s, 0)

        @block.gpsimd
        def _(pool):
            nc.gpsimd.memset(m.ident[:, :], 0.0).then_inc(s["ident0"], 1)
            nc.gpsimd.memset(m.ident_bf[:, :], 0.0).then_inc(s["ident0"], 1)
            pool.wait_ge(s["ident0"], 2)
            for d in (m.ident, m.ident_bf):
                nc.gpsimd.affine_select(out=d[:, :], in_=d[:, :], compare_op=ALU.not_equal, fill=1.0, base=0,
                                        pattern=[[-1, P]], channel_multiplier=1).then_inc(s["ident_ready"], 1)

        @block.vector
        def _(dve):
            nc.vector.memset(m.eps[:, :], EPS).then_inc(s["eps_ready"], 1)
            nc.vector.memset(m.ones[:, :], 1.0)
            ch = Chain(dve, s["em_dve"])
            for c in range(4):
                dve.wait_ge(s["x_loaded"][c], 16)
                for t in range(TILES):
                    last = nc.vector.bn_stats(stats[:, t, :], m.x[:, c * TILES + t, :])
                ch.link(last)
                for t in range(TILES):
                    last = nc.vector.bn_aggr(mv[:, c, t, :], stats[:, t, :])
                last.then_inc(s["em_var"], 1)
                dve.wait_ge(s["em_sqrt"], c + 1)
                ch.link(nc.vector.reciprocal(rstd[:, c, :], rstd[:, c, :]))
                for t in range(TILES):
                    last = nc.vector.tensor_scalar(xn[:, c, t, :], m.x[:, c * TILES + t, :], mv[:, c, t, 0:1],
                                                   rstd[:, c, t:t + 1], ALU.subtract, ALU.mult)
                last.then_inc(s["em_xn"], 1)
            for c in range(4):
                dve.wait_ge(s["em_hi"], c + 1)
                cols = slice(c * BANK, (c + 1) * BANK)
                nc.vector.tensor_tensor(m.xT_lo[:, cols], m.xT[:, cols], m.xT_hi[:, cols].bitcast(F32),
                                        ALU.subtract)

        @block.scalar
        def _(act):
            act.wait_ge(s["eps_ready"], 1)
            def leading(c):
                act.wait_ge(s["em_turned"], c + 1)
                cols = slice(c * BANK, (c + 1) * BANK)
                nc.scalar.copy(m.xT[:, cols], turned[c][:, :])
                nc.scalar.copy(m.xT_hi[:, cols], turned[c][:, :]).then_inc(s["em_hi"], 1)

            for c in range(4):
                act.wait_ge(s["em_var"], c + 1)
                nc.scalar.activation(rstd[:, c, :], mv[:, c, :, 1], ACT.Sqrt,
                                     bias=m.eps[:, 0:1]).then_inc(s["em_sqrt"], 1)
                if c:
                    leading(c - 1)
            leading(3)

        @block.tensor
        def _(pe):
            pe.wait_ge(s["ident_ready"], 2)
            for c in range(4):
                pe.wait_ge(s["em_xn"], c + 1)
                for t in range(TILES):
                    last = nc.tensor.transpose(turned[c][:, t * P:(t + 1) * P], xn[:, c, t, :], m.ident[:, :])
                last.then_inc(s["em_turned"], 1)


def attention(nc, m, s):
    with ExitStack() as ctx:
        def sb(name, shape, dt=F32):
            return ctx.enter_context(nc.sbuf_tensor(name, shape, dt))

        w_raw, w_v, b_qk, b_v = m.w_raw, m.w_v, m.b_qk, m.b_v
        w_hi = sb("w_hi", [P, 2, P], F32R)
        w_lo = sb("w_lo", [P, 2, P], F32R)
        w_out = sb("w_out", [P, P])
        q_both = [[sb(f"q_both{b}{h}", [P, 1024], F32R) for h in range(2)] for b in range(2)]
        q_shift = [[sb(f"q_shift{b}{h}", [P, 1024], F32R) for h in range(2)] for b in range(2)]
        k_hi = [[sb(f"k_hi{b}{h}", [P, 1024], F32R) for h in range(2)] for b in range(2)]
        k_lo = [[sb(f"k_lo{b}{h}", [P, 1024], F32R) for h in range(2)] for b in range(2)]
        v = [sb(f"v{b}", [P, 8, P]) for b in range(2)]
        probs = [sb(f"probs{h}", [P, RING, 1024]) for h in range(2)]
        key_sum = [[sb(f"key_sum{b}{h}", [P, 1024]) for h in range(2)] for b in range(2)]
        maxima = sb("maxima", [P, 2, 8, 2])
        neg_max = sb("neg_max", [P, 2, 8], BF16)
        raw_out = sb("raw_out", [P, 1024])
        row_sum = sb("row_sum", [P, BANK])
        sum_cols = sb("sum_cols", [P, 2, 8])
        inv_cols = sb("inv_cols", [P, 2, 8])
        inv_sum = sb("inv_sum", [P, 1024])
        inv_dram = nc.dram_tensor("inv_sums", [2, 2, 1024], F32, kind="Internal").ap()
        heads_out = sb("heads_out", [P, 1024])

        scores = [ctx.enter_context(nc.psum_tensor(f"scores{h}", [P, 1024], F32)) for h in range(2)]
        pv = ctx.enter_context(nc.psum_tensor("pv", [P, 1024], F32))
        shared = [ctx.enter_context(nc.psum_tensor(f"shared{b}", [P, BANK], F32)) for b in range(2)]

        HALF = [slice(0, HD), slice(HD, P)]
        OTHER = [HALF[1], HALF[0]]
        QUARTER = [[slice(h * HD + c * 32, h * HD + c * 32 + 32) for c in range(2)] for h in range(2)]
        SHIFT_ROW = [HD, 0]
        C = [slice(0, BANK), slice(BANK, 2 * BANK)]

        def order_of_uses(prev, nxt, maxima, sums):
            order = []
            if nxt:
                order += [("q", 0), ("q", 1), ("k", 0), ("k", 1), ("v", 0), ("v", 1)]
            if prev:
                order += [("sum", c) for c in range(sums)]
            if nxt:
                order += [("max", i) for i in range(32 if maxima else 0)]
                order += [(f"row{h}", c) for h in range(2) for c in range(2)]
            if prev:
                order += [("proj", 0), ("proj", 1)]
            return {name: k for k, name in enumerate(order)}

        class Uses:

            def __init__(self, rounds, odd, prev=True, nxt=True, maxima=True, sums=1):
                self.rounds, self.odd, self.at = rounds, odd, order_of_uses(prev, nxt, maxima, sums)

            def bank(self, *name):
                return (self.odd + self.at[name]) % 2

            def earlier(self, *name):
                return self.rounds + (self.odd + self.at[name]) // 2

        FIRST = PREP_USES - 32
        prologue = Uses(0, 0, prev=False, maxima=False)

        def uses_in(p, n, first=False, last=False):
            if first:
                return Uses(FIRST // 2, FIRST % 2, prev=False)
            before = FIRST + PREP_USES + (n - 1) * STEP_USES
            return Uses(p * STEP_USES + before // 2, before % 2, nxt=not last)

        before_end = FIRST + PREP_USES + (2 * PAIRS - 2) * STEP_USES + POST_USES
        epilogue = Uses(before_end // 2, before_end % 2, nxt=False, sums=2)

        wide = [scores[0], scores[1], pv]

        block = ctx.enter_context(nc.Block())

        @block.sync
        def _(sp):
            def next_pair(p, first=False):
                u = uses_in(p, 0, first=first)
                sp.wait_ge(s["shared_free"][u.bank("v", 1)], u.earlier("v", 1) + 1)
                load_pair(sp, m, s, p + 1)

            def out_weights(p, first=False):
                if not first:
                    u = uses_in(p, 0)
                    sp.wait_ge(s["shared_free"][u.bank("proj", 1)], u.earlier("proj", 1) + 1)
                sp.dma_start(w_out[:, :], m.inputs["W_out"][bass.ts(p, P), :]).then_inc(s["w_out_loaded"], 16)

            def invert(p, n, u):
                st = p * 2 + n
                sp.wait_ge(s["shared_free"][u.bank("sum", 0)], u.earlier("sum", 0) + 1)
                for h in range(2):
                    for c in range(2):
                        row = QUARTER[h][c].start
                        sp.dma_start(sum_cols[HALF[c], h, :], row_sum[row:row + 1, :].rearrange("o (p j) -> o p j", j=8)
                                     ).then_inc(s["sum_cols_ready"], 16)
                sp.wait_ge(s["inverted"], st + 1)
                sp.dma_start(inv_dram[n].rearrange("h (p j) -> p h j", j=8), inv_cols[:, :, :]
                             ).then_inc(s["inv_stored"], 16)
                sp.wait_ge(s["inv_stored"], st * 16 + 16)
                wait(sp, s["normalised"], st)
                for h in range(2):
                    sp.dma_start(inv_sum[HALF[h], :], inv_dram[n, h].partition_broadcast(HD)
                                 ).then_inc(s["inv_sum_ready"], 16)

            def copy_leading(p, n):
                st = p * 2 + n
                for j, (what, to) in enumerate(((q_both, q_shift), (k_hi, k_hi))):
                    sp.wait_ge(s["leading_ready"], st * 4 + 2 * j + 2)
                    for h in range(2):
                        sp.dma_start(to[n][h][(HALF, OTHER)[j][h], :].bitcast(F32), what[n][h][HALF[h], :].bitcast(F32)
                                     ).then_inc(s["leading_copied"], 16)

            def step(p, n, first=False, last=False):
                if not last:
                    copy_leading(p + n, 1 - n)
                if n == 0 and not (isinstance(p, int) and p == PAIRS - 1):
                    next_pair(p, first)
                if not first:
                    invert(p - 1 + n, 1 - n, uses_in(p, n, last=last))
                if n == 0 and not first:
                    out_weights(p)

            out_weights(0, first=True)
            copy_leading(0, 0)
            step(0, 0, first=True)
            step(0, 1)
            load_ffn0_weights(sp, m, s)
            with sp.Fori(1, PAIRS - 1) as p:
                step(p, 0)
                step(p, 1)
            step(PAIRS - 1, 0)
            step(PAIRS - 1, 1, last=True)

        @block.tensor
        def _(pe):
            def take(u, *name):
                wait(pe, s["shared_free"][u.bank(*name)], u.earlier(*name))
                return shared[u.bank(*name)]

            def read(u, *name):
                pe.wait_ge(s["shared_free"][u.bank(*name)], u.earlier(*name) + 1)

            def project_qk(u, what, c, p, n):
                j = "qk".index(what)
                pe.wait_ge(s["w_split"], p + 1)
                out = take(u, what, c)
                cols = slice(n * 1024 + c * BANK, n * 1024 + (c + 1) * BANK)
                nc.tensor.matmul(out[:, :], w_hi[:, j, :], m.xT_hi[:, cols], start=True, stop=False)
                nc.tensor.matmul(out[:, :], w_hi[:, j, :], m.xT_lo[:, cols], start=False, stop=False)
                nc.tensor.matmul(out[:, :], w_lo[:, j, :], m.xT_hi[:, cols], start=False, stop=True
                                 ).then_inc(s["shared_full"][u.bank(what, c)], 1)

            def project_v(u, j, n):
                out = take(u, "v", j)
                for t in range(TILES):
                    tok = n * 1024 + (j * TILES + t) * P
                    last = nc.tensor.matmul(out[:, t * P:(t + 1) * P], m.xT[:, tok:tok + P], w_v[:, :],
                                            start=True, stop=True)
                last.then_inc(s["shared_full"][u.bank("v", j)], 1)

            def find_maxima(u, slot, place, p, n):
                if slot not in MAXIMA:
                    return
                if slot == 3 and place == 0:
                    for c in range(2):
                        read(u, "k", c)
                    pe.wait_ge(s["leading_copied"], (p * 2 + n + 1) * 64)
                i = MAXIMA[slot][place]
                h, qt, kc = i // 16, i % 16 // 2, i % 2
                out = take(u, "max", i)
                nc.tensor.matmul(out[:, :], q_both[n][h][:, qt * P:(qt + 1) * P], k_hi[n][h][:, C[kc]],
                                 start=True, stop=True).then_inc(s["shared_full"][u.bank("max", i)], 1)

            def shift_row(u, h, c, p, n):
                pe.wait_ge(s["neg_max_ready"], (p * 2 + n) * 2 + h + 1)
                r = SHIFT_ROW[h]
                out = take(u, f"row{h}", c)
                for t in range(TILES):
                    j = c * TILES + t
                    last = nc.tensor.matmul(out[r:r + 1, t * P:(t + 1) * P], neg_max[:, h, j:j + 1],
                                            m.ident_bf[:, :], start=True, stop=True)
                last.then_inc(s["shared_full"][u.bank(f"row{h}", c)], 1)

            def score(p, n, kt, h, prepared, between):
                if kt == 0:
                    for c in range(2):
                        read(prepared, f"row{h}", c)
                wait(pe, s["exp_done"][h], (p * 2 + n) * 8 + kt)
                for part, (w, q, start) in enumerate(((k_hi, q_both, True), (k_lo, q_shift, False))):
                    for c in range(2):
                        last = nc.tensor.matmul(scores[h][:, C[c]], w[n][h][:, kt * P:(kt + 1) * P],
                                                q[n][h][:, C[c]], start=start, stop=not start)
                    if part == 1:
                        last.then_inc(s["scores_ready"][h], 1)
                    between(h * 2 + part)

            def weigh(p, n, kt, between):
                for h in range(2):
                    pe.wait_ge(s["exp_done"][h], (p * 2 + n) * 8 + kt + 1)
                if kt == 0:
                    wait(pe, s["raw_out_ready"], p * 2 + n)
                for c in range(2):
                    for h in range(2):
                        last = nc.tensor.matmul(pv[HALF[h], C[c]], v[n][:, kt, HALF[h]],
                                                probs[h][:, kt % RING, C[c]], start=kt == 0, stop=kt == 7)
                    if c == 1:
                        last.then_inc(s["weighed"], 1)
                    between(4 + 2 * c)
                    between(5 + 2 * c)

            def sum_rows(u, p, n):
                for h in range(2):
                    pe.wait_ge(s["keys_added"][h], (p * 2 + n + 1) * 7)
                out = take(u, "sum", 0)
                for h in range(2):
                    for c in range(2):
                        last = nc.tensor.matmul(out[QUARTER[h][c], :], m.ones[:, QUARTER[h][c]],
                                                key_sum[n][h][:, C[c]], start=True, stop=True)
                last.then_inc(s["shared_full"][u.bank("sum", 0)], 1)

            def sum_rows_last(u, p, n):
                for h in range(2):
                    pe.wait_ge(s["keys_added"][h], (p * 2 + n + 1) * 7)
                for c in range(2):
                    out = take(u, "sum", c)
                    for h in range(2):
                        last = nc.tensor.matmul(out[HALF[h], :], m.ones[:, HALF[h]], key_sum[n][h][:, C[c]],
                                                start=True, stop=True)
                    last.then_inc(s["shared_full"][u.bank("sum", c)], 1)

            def project_out(u, p, n):
                pe.wait_ge(s["w_out_loaded"], p * 16 + 16)
                for c in range(2):
                    pe.wait_ge(s["normalised"], p * 2 + n + 1 + (c if u is epilogue else 0))
                    out = take(u, "proj", c)
                    nc.tensor.matmul(out[:, :], w_out[:, :], heads_out[:, C[c]], start=True, stop=True
                                     ).then_inc(s["shared_full"][u.bank("proj", c)], 1)

            def step(p, n, prepared, first=False, last=False):
                u = uses_in(p, n, first, last)
                before, after = (p - 1 + n, 1 - n), (p + n, 1 - n)
                for kt in range(8):
                    def between(place):
                        if not last:
                            find_maxima(u, kt, place, *after)
                        if not last and kt == 7 and place < 4:
                            shift_row(u, place // 2, place % 2, *after)

                    score(p, n, kt, 0, prepared, between)
                    if kt == 0 and not last:
                        project_qk(u, "q", 0, *after)
                    score(p, n, kt, 1, prepared, between)
                    if kt == 1 and not last:
                        project_qk(u, "k", 0, *after)
                    if kt == 2 and not last:
                        project_v(u, 0, after[1])
                    if kt > 0:
                        weigh(p, n, kt - 1, between)
                    elif not first:
                        weigh(*before, 7, between)
                    if kt < 2 and not last:
                        project_qk(u, "qk"[kt], 1, *after)
                    if kt == 2 and not last:
                        project_v(u, 1, after[1])
                    if kt == 2 and not first:
                        sum_rows(u, *before)
                    if kt == 7 and not first:
                        project_out(u, *before)
                return u

            for what in "qk":
                for c in range(2):
                    project_qk(prologue, what, c, 0, 0)
            for j in range(2):
                project_v(prologue, j, 0)
            read(prologue, "q", 0)
            read(prologue, "q", 1)
            pe.wait_ge(s["leading_copied"], 64)
            for i in range(16):
                h, qt = i // 8, i % 8
                wait(pe, s["wide_free"], i - 2)
                for c in range(2):
                    last = nc.tensor.matmul(wide[i % 3][:, C[c]], q_both[0][h][:, qt * P:(qt + 1) * P],
                                            k_hi[0][h][:, C[c]], start=True, stop=True)
                last.then_inc(s["wide_full"], 1)
            for h in range(2):
                for c in range(2):
                    shift_row(prologue, h, c, 0, 0)
            pe.wait_ge(s["filled"], 1)
            u = step(0, 0, prologue, first=True)
            step(0, 1, u)
            with pe.Fori(1, PAIRS - 1) as p:
                u = step(p, 0, uses_in(p - 1, 1))
                step(p, 1, u)
            u = step(PAIRS - 1, 0, uses_in(PAIRS - 2, 1))
            step(PAIRS - 1, 1, u, last=True)
            weigh(PAIRS - 1, 1, 7, lambda place: None)
            sum_rows_last(epilogue, PAIRS - 1, 1)
            project_out(epilogue, PAIRS - 1, 1)

        @block.scalar
        def _(act):
            def got(u, *name):
                act.wait_ge(s["shared_full"][u.bank(*name)], u.earlier(*name) + 1)
                return shared[u.bank(*name)]

            def leading(u, what, c, n):
                j = "qk".index(what)
                ps = got(u, what, c)
                for h in range(2):
                    to = (q_both if what == "q" else k_hi)[n][h]
                    last = nc.scalar.activation(to[HALF[h], C[c]], ps[HALF[h], :], ACT.Identity,
                                                bias=b_qk[HALF[h], j:j + 1])
                last.then_inc(s["leading_ready"], 1)

            def shift_rows(u, h, n):
                r = SHIFT_ROW[h]
                for c in range(2):
                    ps = got(u, f"row{h}", c)
                    nc.scalar.copy(q_shift[n][h][r:r + 1, C[c]], ps[r:r + 1, :]
                                   ).then_inc(s["shared_free"][u.bank(f"row{h}", c)], 1)

            def fetch_sums(u, p, n):
                wait(act, s["sum_cols_ready"], (p * 2 + n) * 64)
                ps = got(u, "sum", 0)
                nc.scalar.copy(row_sum[:, :], ps[:, :]).then_inc(s["shared_free"][u.bank("sum", 0)], 1)

            def exponentials(p, n, kt, first):
                st = p * 2 + n
                for h in range(2):
                    act.wait_ge(s["scores_ready"][h], st * 8 + kt + 1)
                    if kt >= RING or not first:
                        act.wait_ge(s["weighed"], st * 8 + kt - RING + 1)
                        act.wait_ge(s["keys_added"][h], st * 7 + (max(kt - RING, 1) if kt >= RING else kt + RING - 7))
                    nc.scalar.activation(probs[h][:, kt % RING, :], scores[h][:, :], ACT.Exp,
                                         scale=HD ** -0.5).then_inc(s["exp_done"][h], 1)

            def fetch_out(p, n):
                st = p * 2 + n
                act.wait_ge(s["weighed"], st * 8 + 8)
                wait(act, s["normalised"], st)
                nc.scalar.copy(raw_out[:, :], pv[:, :]).then_inc(s["raw_out_ready"], 1)

            def step(p, n, first=False, last=False):
                u = uses_in(p, n, first, last)
                for kt in range(8):
                    if kt == 7 and not last:
                        shift_rows(u, 0, 1 - n)
                    exponentials(p, n, kt, first)
                    if kt < 2 and not last:
                        leading(u, "qk"[kt], 0, 1 - n)
                    if kt == 0 and not first:
                        fetch_out(p - 1 + n, 1 - n)
                    if kt < 2 and not last:
                        leading(u, "qk"[kt], 1, 1 - n)
                    if kt == 2 and not first:
                        fetch_sums(u, p - 1 + n, 1 - n)
                    if kt == 7 and not last:
                        shift_rows(u, 1, 1 - n)

            for what in "qk":
                for c in range(2):
                    leading(prologue, what, c, 0)
            act.wait_ge(s["filled"], 1)
            shift_rows(prologue, 0, 0)
            shift_rows(prologue, 1, 0)
            step(0, 0, first=True)
            step(0, 1)
            with act.Fori(1, PAIRS - 1) as p:
                step(p, 0)
                step(p, 1)
            step(PAIRS - 1, 0)
            step(PAIRS - 1, 1, last=True)
            fetch_out(PAIRS - 1, 1)

        @block.vector
        def _(dve):
            def got(u, *name):
                dve.wait_ge(s["shared_full"][u.bank(*name)], u.earlier(*name) + 1)
                return shared[u.bank(*name)]

            def done(u, *name):
                dve.wait_ge(s["shared_free"][u.bank(*name)], u.earlier(*name) + 1)

            def remainders(u, what, p, n):
                j = "qk".index(what)
                for c in range(2):
                    ps = got(u, what, c)
                    dve.wait_ge(s["leading_ready"], (p * 2 + n) * 4 + 2 * j + c + 1)
                    for h in range(2):
                        lead = (q_both if what == "q" else k_hi)[n][h][HALF[h], C[c]]
                        to = q_both[n][h][OTHER[h], C[c]] if what == "q" else k_lo[n][h][HALF[h], C[c]]
                        last = nc.vector.scalar_tensor_tensor(out=to, in0=ps[HALF[h], :], scalar=b_qk[HALF[h], j:j + 1],
                                                              in1=lead.bitcast(F32), op0=ALU.add, op1=ALU.subtract)
                    last.then_inc(s["shared_free"][u.bank(what, c)], 1)

            def values(u, n):
                bias = b_v[:, :].unsqueeze(1).broadcast_to([P, TILES, P])
                for j in range(2):
                    ps = got(u, "v", j)
                    nc.vector.tensor_tensor(v[n][:, j * TILES:(j + 1) * TILES, :],
                                            ps[:, :].rearrange("p (t d) -> p t d", t=TILES), bias, ALU.add
                                            ).then_inc(s["shared_free"][u.bank("v", j)], 1)

            def find_maxima(u, slot):
                for i in MAXIMA[slot]:
                    h, qt, kc = i // 16, i % 16 // 2, i % 2
                    ps = got(u, "max", i)
                    nc.vector.tensor_reduce(maxima[:, h, qt, kc:kc + 1], ps[:, :], X, ALU.max
                                            ).then_inc(s["shared_free"][u.bank("max", i)], 1)
                    if i % 16 == 15:
                        done(u, "max", i - 1)
                        done(u, "max", i)
                        nc.vector.tensor_reduce(neg_max[:, h, :], maxima[:, h, :, :], X, ALU.max, negate=True
                                                ).then_inc(s["neg_max_ready"], 1)

            def invert(p, n):
                st = p * 2 + n
                dve.wait_ge(s["sum_cols_ready"], st * 64 + 64)
                wait(dve, s["inv_stored"], st * 16)
                nc.vector.reciprocal(inv_cols[:, :, :], sum_cols[:, :, :]).then_inc(s["inverted"], 1)

            def normalise(p, n):
                st = p * 2 + n
                dve.wait_ge(s["inv_sum_ready"], st * 32 + 32)
                dve.wait_ge(s["raw_out_ready"], st + 1)
                nc.vector.tensor_tensor(heads_out[:, :], raw_out[:, :], inv_sum[:, :], ALU.mult
                                        ).then_inc(s["normalised"], 1)

            def normalise_last(u, p, n):
                for c in range(2):
                    ps = got(u, "sum", c)
                    nc.vector.reciprocal(inv_sum[:, C[c]], ps[:, :]).then_inc(s["shared_free"][u.bank("sum", c)], 1)
                    done(u, "sum", c)
                    if c == 0:
                        dve.wait_ge(s["raw_out_ready"], p * 2 + n + 1)
                    nc.vector.tensor_tensor(heads_out[:, C[c]], raw_out[:, C[c]], inv_sum[:, C[c]], ALU.mult
                                            ).then_inc(s["normalised"], 1)

            def add_keys(p, n, kt, h):
                st = p * 2 + n
                dve.wait_ge(s["exp_done"][h], st * 8 + kt + 1)
                dve.wait_ge(s["keys_added"][h], st * 7 + kt - 1)
                if kt == 1:
                    dve.wait_ge(s["normalised"], st - 1)
                a = probs[h][:, 0, :] if kt == 1 else key_sum[n][h][:, :]
                nc.vector.tensor_tensor(key_sum[n][h][:, :], a, probs[h][:, kt % RING, :], ALU.add
                                        ).then_inc(s["keys_added"][h], 1)

            def add_projection(u, n):
                for c in range(2):
                    ps = got(u, "proj", c)
                    y = m.yT[:, n * 1024 + c * BANK:n * 1024 + (c + 1) * BANK]
                    nc.vector.tensor_tensor(y, ps[:, :], y, ALU.add).then_inc(s["shared_free"][u.bank("proj", c)], 1)

            def split_weights(p):
                dve.wait_ge(s["pair_loaded"], p * 64 + 64)
                nc.vector.tensor_copy(w_hi[:, :, :], w_raw[:, :, :]).then_inc(s["w_hi_ready"], 1)
                dve.wait_ge(s["w_hi_ready"], p + 1)
                nc.vector.tensor_tensor(w_lo[:, :, :], w_raw[:, :, :], w_hi[:, :, :].bitcast(F32), ALU.subtract
                                        ).then_inc(s["w_split"], 1)

            def step(p, n, first=False, last=False):
                u = uses_in(p, n, first, last)
                before, after = (p - 1 + n, 1 - n), (p + n, 1 - n)
                for kt in range(8):
                    if kt == 4 and not first:
                        invert(*before)
                    if kt in MAXIMA and not last:
                        find_maxima(u, kt)
                    if kt == 7 and not first:
                        normalise(*before)
                        add_projection(u, before[1])
                    if last and kt > 0:
                        add_keys(p, n, kt, 1)
                    if last:
                        continue
                    if kt == 0:
                        remainders(u, "q", *after)
                    if kt == 1:
                        remainders(u, "k", *after)
                    if kt == 2:
                        values(u, after[1])
                    if kt == 7 and n == 0 and not (isinstance(p, int) and p == PAIRS - 1):
                        split_weights(p + 1)

            split_weights(0)
            remainders(prologue, "q", 0, 0)
            remainders(prologue, "k", 0, 0)
            values(prologue, 0)
            for i in range(16):
                h, qt = i // 8, i % 8
                dve.wait_ge(s["wide_full"], i + 1)
                nc.vector.tensor_reduce(maxima[:, h, qt, 0:1], wide[i % 3][:, :], X, ALU.max).then_inc(s["wide_free"], 1)
                if qt == 7:
                    dve.wait_ge(s["wide_free"], i + 1)
                    nc.vector.tensor_scalar(neg_max[:, h, :], maxima[:, h, :, 0], -1.0, None, ALU.mult
                                            ).then_inc(s["neg_max_ready"], 1)
            dve.wait_ge(s["bias_loaded"], 16)
            nc.vector.memset(m.yT[:, :], 0.0).then_inc(s["yT_clear"], 1)
            dve.wait_ge(s["yT_clear"], 1)
            nc.vector.tensor_scalar(m.yT[:, :], m.yT[:, :], m.b_out[:, 0:1], None, ALU.add)
            step(0, 0, first=True)
            step(0, 1)
            with dve.Fori(1, PAIRS - 1) as p:
                step(p, 0)
                step(p, 1)
            step(PAIRS - 1, 0)
            step(PAIRS - 1, 1, last=True)
            normalise_last(epilogue, PAIRS - 1, 1)
            add_projection(epilogue, 1)

        @block.gpsimd
        def _(pool):
            for b in range(2):
                nc.gpsimd.memset(q_shift[b][0][OTHER[0], :].bitcast(F32), 0.0)
                nc.gpsimd.memset(q_shift[b][1][OTHER[1], :].bitcast(F32), 0.0)
                nc.gpsimd.memset(k_lo[b][0][OTHER[0], :].bitcast(F32), 0.0)
                last = nc.gpsimd.memset(k_lo[b][1][OTHER[1], :].bitcast(F32), 0.0)
            last.then_inc(s["cleared"], 1)
            pool.wait_ge(s["cleared"], 1)
            for b in range(2):
                for h in range(2):
                    r = SHIFT_ROW[h]
                    last = nc.gpsimd.memset(k_lo[b][h][r:r + 1, :].bitcast(F32), 1.0)
            last.then_inc(s["filled"], 1)

            def step(p, n, first=False, heads=(0, 1)):
                st = p * 2 + n
                for kt in range(1, 8):
                    for h in heads:
                        pool.wait_ge(s["exp_done"][h], st * 8 + kt + 1)
                        if kt == 1:
                            if not (first or (isinstance(p, int) and p == 0)):
                                pool.wait_ge(s["normalised"], st - 1)
                            a = probs[h][:, 0, :]
                        else:
                            pool.wait_ge(s["keys_added"][h], st * 7 + kt - 1)
                            a = key_sum[n][h][:, :]
                        nc.gpsimd.tensor_tensor(key_sum[n][h][:, :], a, probs[h][:, kt % RING, :], ALU.add
                                                ).then_inc(s["keys_added"][h], 1)

            step(0, 0, first=True)
            step(0, 1)
            with pool.Fori(1, PAIRS - 1) as p:
                step(p, 0)
                step(p, 1)
            step(PAIRS - 1, 0)
            step(PAIRS - 1, 1, heads=(0,))


class Norms:

    def __init__(self, nc, chain, carrier, var_ready, root_ready, eps, stats, mv, rstd, before):
        self.nc, self.chain, self.var_ready, self.root_ready, self.eps = nc, chain, var_ready, root_ready, eps
        self.carrier = carrier
        self.stats, self.mv, self.rstd, self.done = stats, mv, rstd, before

    def norm(self, src, out):
        nc, dve = self.nc, self.chain.eng
        nc.vector.memset(self.carrier[:, :], 0.0)
        for t, tile in enumerate(src):
            last = nc.vector.bn_stats(self.stats[:, t, :], tile)
        self.chain.link(last)
        nc.vector.memset(self.carrier[:, :], 0.0)
        for t in range(len(src)):
            last = nc.vector.bn_aggr(self.mv[:, t, :], self.stats[:, t, :])
        last.then_inc(self.var_ready, 1)
        self.done = self.done + 1
        dve.wait_ge(self.root_ready, self.done)
        self.chain.link(nc.vector.reciprocal(self.rstd[:, :], self.rstd[:, :]))
        made = []
        for t, tile in enumerate(src):
            made.append(nc.vector.tensor_scalar(out[:, t, :], tile, self.mv[:, t, 0:1], self.rstd[:, t:t + 1],
                                                ALU.subtract, ALU.mult))
        return made[TILES - 1::TILES]

    def root(self, act):
        self.done = self.done + 1
        act.wait_ge(self.var_ready, self.done)
        self.nc.scalar.activation(self.rstd[:, :], self.mv[:, :, 1], ACT.Sqrt, bias=self.eps[:, 0:1]
                                  ).then_inc(self.root_ready, 1)


EXPERTS = 8
GATE_LINKS = 14


def pick_two(nc, ch, t, logits, bias, rank, weights_wanted, weights_ready, value):
    dve = ch.eng
    shape = [P, t.tiles, EXPERTS]

    def wide(a):
        return a[:, :].unsqueeze(2).broadcast_to(shape)

    ranks = rank[:, :].unsqueeze(1).broadcast_to(shape)
    if bias is None:
        ch.link(nc.vector.tensor_copy(t.logit[:, :, :], logits))
    else:
        ch.link(nc.vector.tensor_tensor(t.logit[:, :, :], logits, bias[:, :].unsqueeze(1).broadcast_to(shape), ALU.add))

    def choose(values, best, chosen):
        ch.link(nc.vector.tensor_reduce(best[:, :], values, X, ALU.max))
        ch.link(nc.vector.tensor_tensor(t.score[:, :, :], values, wide(best), ALU.is_equal))
        ch.link(nc.vector.tensor_tensor(t.score[:, :, :], t.score[:, :, :], ranks, ALU.mult))
        ch.link(nc.vector.tensor_reduce(t.first[:, :], t.score[:, :, :], X, ALU.max))
        ch.link(nc.vector.tensor_tensor(chosen[:, :, :], t.score[:, :, :], wide(t.first), ALU.is_equal))

    choose(t.logit[:, :, :], t.best1, t.chosen1)
    ch.link(nc.vector.scalar_tensor_tensor(out=t.rest[:, :, :], in0=t.chosen1[:, :, :], scalar=LEAST,
                                           in1=t.logit[:, :, :], op0=ALU.mult, op1=ALU.add))
    choose(t.rest[:, :, :], t.best2, t.chosen2)
    nc.vector.tensor_tensor(t.gap[:, :], t.best1[:, :], t.best2[:, :], ALU.subtract).then_inc(weights_wanted, 1)
    dve.wait_ge(weights_ready, value)
    ch.link(nc.vector.tensor_tensor(t.chosen1[:, :, :], t.chosen1[:, :, :], wide(t.weight1), ALU.mult))
    ch.link(nc.vector.tensor_tensor(t.chosen2[:, :, :], t.chosen2[:, :, :], wide(t.weight2), ALU.mult))
    return nc.vector.tensor_tensor(t.gates[:, :, :], t.chosen1[:, :, :], t.chosen2[:, :, :], ALU.add)


def weigh_two(nc, act, t, weights_wanted, weights_ready, value):
    act.wait_ge(weights_wanted, value)
    nc.scalar.activation(t.weight1[:, :], t.gap[:, :], ACT.Sigmoid)
    nc.scalar.activation(t.weight2[:, :], t.gap[:, :], ACT.Sigmoid, scale=-1.0).then_inc(weights_ready, 1)


def tiles_of(a):
    return [a[:, t, :] for t in range(a.shape[1])]


def gating_buffers(sb, name, tiles):
    g = Buffers()
    g.tiles = tiles
    g.logit, g.score, g.rest, g.chosen1, g.chosen2, g.gates = (
        sb(f"{name}_{what}", [P, tiles, EXPERTS]) for what in ("logit", "score", "rest", "chosen1", "chosen2", "gates"))
    g.best1, g.best2, g.first, g.gap, g.weight1, g.weight2 = (
        sb(f"{name}_{what}", [P, tiles]) for what in ("best1", "best2", "first", "gap", "weight1", "weight2"))
    return g


M0, H0 = 64, 256
PAIR = 2 * BANK
STEPS0 = EXPERTS
FFN0_ORDER = [
    ("norm_y", 0), ("norm_x", 0), ("turn_x", 0), ("norm_y", 1), ("encode", 0), ("condense", 0),
    ("route", 0), ("gate", 0), ("turn_gates", 0),
    ("norm_x", 1), ("experts", 0, 0), ("turn_x", 1), ("experts", 0, 1), ("encode", 1), ("experts", 0, 2),
    ("condense", 1), ("experts", 0, 3), ("route", 1), ("experts", 0, 4), ("gate", 1), ("turn_gates", 1),
    ("experts", 0, 5), ("experts", 0, 6), ("experts", 0, 7),
    ("experts", 1, 0), ("spread", 0), ("experts", 1, 1), ("decode", 0), ("experts", 1, 2), ("experts", 1, 3),
    ("norm", 0), ("experts", 1, 4), ("affine", 0), ("experts", 1, 5), ("experts", 1, 6), ("norm_again", 0),
    ("experts", 1, 7),
    ("spread", 1), ("decode", 1), ("norm_x_again", 0), ("turn_x_again", 0), ("norm", 1), ("attend", 0), ("affine", 1),
    ("norm_again", 1), ("norm_x_again", 1), ("turn_x_again", 1), ("attend", 1)]


def ffn0_weights(nc, m, sb):
    w = m.ffn0 = Buffers()
    w.enc_raw, w.s2c = sb("enc_raw", [P, H0]), sb("s2c", [P, 2, M0])
    w.r1_raw, w.e1_raw = sb("r1_raw", [P, M0]), sb("e1_raw", [P, EXPERTS, P])
    w.r2, w.e2 = sb("r2", [M0, EXPERTS]), sb("e2", [P, EXPERTS, M0])
    w.e2_b = sb("e2_b", [P, EXPERTS // 2])
    w.c2s, w.dec = sb("c2s", [P, H0]), sb("dec", [P, 2, P])
    w.enc_b, w.c2s_b = sb("enc_b", [P, 2]), sb("c2s_b", [P, 2])
    w.s2c_b, w.r1_b = sb("s2c_b", [M0, 1]), sb("r1_b", [M0, 1])
    w.e1_b, w.r2_b = sb("e1_b", [P, EXPERTS]), sb("r2_b", [P, EXPERTS])
    w.dec_b, w.ln_g, w.ln_b = sb("dec_b", [P, P]), sb("ln_g", [P, P]), sb("ln_b", [P, P])
    w.qkv_raw = sb("qkv_raw", [P, 3, P])
    w.q_b, w.kv_b = sb("q_b", [P, 1]), sb("kv_b", [P, 2 * P])


FFN0_LOADS = 24


def load_ffn0_weights(sp, m, s):
    w = m.ffn0

    def load(dst, src):
        sp.dma_start(dst, src).then_inc(s["f0_loaded"], 16)

    load(w.enc_raw[:, :], m.inputs["enc_W"])
    load(w.s2c[:, :, :], m.inputs["s2c_W"].rearrange("(c p) n -> p c n", p=P))
    for half in range(2):
        rows = slice(half * M0, (half + 1) * M0)
        load(w.r1_raw[rows, :], m.inputs["rW1"])
        load(w.e1_raw[rows, :, :], m.inputs["We1"].rearrange("e m h -> m e h"))
        load(w.c2s[rows, :], m.inputs["c2s_W"])
    load(w.r2[:, :], m.inputs["rW2"])
    load(w.e2[:, :, :], m.inputs["We2"].rearrange("e h m -> h e m"))
    load(w.e2_b[:, :], m.inputs["be2"].rearrange("(e two) m -> (two m) e", two=2))
    load(w.dec[:, :, :], m.inputs["dec_W"].rearrange("(c p) n -> p c n", p=P))
    load(w.qkv_raw[:, :, :], m.inputs["w_qkv1"].rearrange("(c p) d -> p c d", p=P))
    load(w.enc_b[:, :], m.inputs["enc_b"].rearrange("(c p) -> p c", p=P))
    load(w.c2s_b[:, :], m.inputs["c2s_b"].rearrange("(c p) -> p c", p=P))
    load(w.s2c_b[:, :], m.inputs["s2c_b"].unsqueeze(1))
    load(w.r1_b[:, :], m.inputs["rb1"].unsqueeze(1))
    load(w.e1_b[:, :], m.inputs["be1"].rearrange("e p -> p e"))
    load(w.r2_b[:, :], m.inputs["rb2"].partition_broadcast(P))
    load(w.dec_b[:, :], m.inputs["dec_b"].partition_broadcast(P))
    load(w.ln_g[:, :], m.inputs["ln_g"].partition_broadcast(P))
    load(w.ln_b[:, :], m.inputs["ln_b"].partition_broadcast(P))
    load(w.q_b[:, :], m.inputs["b_qkv1"][0:P].unsqueeze(1))
    load(w.kv_b[:, :], m.inputs["b_qkv1"][P:3 * P].partition_broadcast(P))


def ffn0(nc, m, s):
    with ExitStack() as ctx:
        def sb(name, shape, dt=F32):
            return ctx.enter_context(nc.sbuf_tensor(name, shape, dt))

        w = m.ffn0
        enc_hi, enc_lo = sb("enc_hi", [P, H0], F32R), sb("enc_lo", [P, H0], F32R)
        r1_hi, r1_lo = sb("r1_hi", [P, M0], F32R), sb("r1_lo", [P, M0], F32R)
        e1_hi, e1_lo = sb("e1_hi", [P, EXPERTS, P], F32R), sb("e1_lo", [P, EXPERTS, P], F32R)
        qkv_T = sb("qkv_T", [P, 3, P])

        post = sb("post", [P, 2 * TILES, P])
        xn = sb("xn", [P, 2 * TILES, P])
        xT_hi, xT_lo = m.xT_hi, m.xT_lo
        spikes = sb("spikes", [P, 2, PAIR])
        router = sb("router", [M0, PAIR])
        gates_T = sb("gates_T", [EXPERTS, PAIR])
        decoded = [sb("decoded", [P, 2 * TILES, P]),
                   m.yT[:, PAIR:2 * PAIR].rearrange("p (t d) -> p t d", t=2 * TILES)]
        xT2 = spikes[:, 0, :]
        stats, mv, rstd = sb("stats0", [P, 2 * TILES, 6]), sb("mv0", [P, 2 * TILES, 2]), sb("rstd0", [P, 2 * TILES])
        cont = [sb(f"cont{p}", [P, PAIR], F32R) for p in range(2)]
        g = [gating_buffers(sb, f"g0_{p}", 2 * TILES) for p in range(2)]
        mixed = [sb(f"mixed0_{p}", [P, PAIR]) for p in range(2)]
        gate_rows = [sb(f"gate_rows{p}", [P, EXPERTS // 2, PAIR]) for p in range(2)]
        gates_dram = nc.dram_tensor("gates", [2, EXPERTS, PAIR], F32, kind="Internal").ap()
        hidden = [[sb(f"hidden0_{c}{j}", [P, BANK]) for j in range(2)] for c in range(2)]
        part = [m.yT[:, c * BANK:(c + 1) * BANK] for c in range(2)]

        def pb(name):
            return ctx.enter_context(nc.psum_tensor(name, [P, BANK], F32))

        turned = [pb(f"turned0_{c}") for c in range(2)]
        narrow = [pb(f"narrow0_{c}") for c in range(2)]
        hid = [pb(f"hid0_{c}") for c in range(2)]
        eout = [pb(f"eout0_{c}") for c in range(2)]
        turned_t = [a[:, :].rearrange("p (t d) -> p t d", t=TILES) for a in turned]
        logits = turned[0][:, 0:2 * TILES * EXPERTS].rearrange("p (t e) -> p t e", t=2 * TILES)
        TURNED_Y = [turned_t, [a[:, :].rearrange("p (t d) -> p t d", t=TILES) for a in eout]]
        WIDE_FRONT = [narrow, turned]
        WIDE_BACK = [turned, narrow]
        COLS = [slice(0, BANK), slice(BANK, PAIR)]
        ROWS = [slice(0, TILES), slice(TILES, 2 * TILES)]
        HALF = [slice(0, M0), slice(M0, P)]

        block = ctx.enter_context(nc.Block())

        @block.sync
        def _(sp):
            for p in range(2):
                sp.wait_ge(s["f0_gates_T"], p * 2 + 2)
                sp.dma_start(gates_dram[p], gates_T[:, :]).then_inc(s["f0_gates_stored"], 16)
                sp.wait_ge(s["f0_gates_stored"], p * 16 + 16)
                for e in range(EXPERTS):
                    sp.dma_start(gate_rows[p][HALF[e % 2], e // 2, :], gates_dram[p, e].partition_broadcast(M0)
                                 ).then_inc(s["f0_rows"][p * 4 + e // 2], 16)
            load_ffn1_weights(sp, m, s)
            for e in range(EXPERTS):
                sp.dma_start(m.w1_raw[:, e, :], m.inputs["W1"][e]).then_inc(s["w1_loaded"], 16)
                sp.dma_start(m.w2[:, e, :, :], m.inputs["W2"][e].rearrange("(c p) d -> p c d", p=P)
                             ).then_inc(s["w1_loaded"], 16)

        @block.gpsimd
        def _(pool):
            nc.gpsimd.memset(e1_lo[M0:P, :, :].bitcast(F32), 0.0)
            nc.gpsimd.memset(r1_lo[M0:P, :].bitcast(F32), 0.0).then_inc(s["f0_split"], 1)
            pool.wait_ge(s["f0_split"], 1)
            pool.wait_ge(s["f0_w_hi"], 1)
            for n, (lo, raw, hi) in enumerate(((enc_lo[:, :], w.enc_raw[:, :], enc_hi[:, :]),
                                               (r1_lo[0:M0, :], w.r1_raw[0:M0, :], r1_hi[0:M0, :]),
                                               (e1_lo[0:M0, :, :], w.e1_raw[0:M0, :, :], e1_hi[0:M0, :, :]))):
                nc.gpsimd.tensor_tensor(lo, raw, hi.bitcast(F32), ALU.subtract).then_inc(s["f0_split"], 1)
                if n < 2:
                    pool.wait_ge(s["f0_split"], n + 2)

        @block.tensor
        def _(pe):
            def turn(out, src):
                for t in range(TILES):
                    last = nc.tensor.transpose(out[:, t, :], src(t), m.ident[:, :])
                return last

            def front(piece, p):
                if piece == "norm_y":
                    for c in range(2):
                        tok = p * PAIR + c * BANK
                        turn(TURNED_Y[p][c], lambda t: m.yT[:, tok + t * P:tok + (t + 1) * P]
                             ).then_inc(s["f0_y_turned"], 1)
                if piece == "turn_x":
                    wait(pe, s["f0_gates_T"], p * 2)
                    for c in range(2):
                        pe.wait_ge(s["f0_xn"], p * 2 + c + 1)
                        turn(turned_t[c], lambda t: xn[:, c * TILES + t, :]).then_inc(s["f0_x_turned"], 1)
                if piece == "encode":
                    for c in range(2):
                        pe.wait_ge(s["f0_xT_lo"], p * 2 + c + 1)
                        if c == 1:
                            pe.wait_ge(s["f0_xT_hi"], p * 2 + 2)
                        pe.wait_ge(s["f0_split"], 4)
                        for j in range(2):
                            cols, out = slice(j * P, (j + 1) * P), WIDE_FRONT[c][j][:, :]
                            nc.tensor.matmul(out, enc_hi[:, cols], xT_hi[:, COLS[c]], start=True, stop=False)
                            nc.tensor.matmul(out, enc_hi[:, cols], xT_lo[:, COLS[c]], start=False, stop=False)
                            nc.tensor.matmul(out, enc_lo[:, cols], xT_hi[:, COLS[c]], start=False, stop=True
                                             ).then_inc(s["f0_enc"], 1)
                if piece == "condense":
                    for c in range(2):
                        for j in range(2):
                            pe.wait_ge(s["f0_spikes"], p * 4 + 2 * c + 2)
                            last = nc.tensor.matmul(narrow[c][0:M0, :], w.s2c[:, j, :], spikes[:, j, COLS[c]],
                                                    start=j == 0, stop=j == 1)
                        last.then_inc(s["f0_cont"], 1)
                if piece == "route":
                    for c in range(2):
                        pe.wait_ge(s["f0_cont_lo"], p * 2 + c + 1)
                        nc.tensor.matmul(narrow[c][0:M0, :], r1_hi[:, :], cont[p][:, COLS[c]], start=True, stop=False)
                        nc.tensor.matmul(narrow[c][0:M0, :], r1_lo[:, :], cont[p][:, COLS[c]], start=False, stop=True
                                         ).then_inc(s["f0_router"], 1)
                if piece == "gate":
                    for c in range(2):
                        pe.wait_ge(s["f0_tanh"], p * 2 + c + 1)
                        for t in range(TILES):
                            j = c * TILES + t
                            last = nc.tensor.matmul(logits[:, j, :], router[:, j * P:(j + 1) * P], w.r2[:, :],
                                                    start=True, stop=True)
                    last.then_inc(s["f0_logits"], 1)
                if piece == "turn_gates":
                    pe.wait_ge(s["f0_gates"], p + 1)
                    for c in range(2):
                        for t in range(TILES):
                            last = nc.tensor.transpose(turned[c][0:EXPERTS, t * P:(t + 1) * P],
                                                       g[p].gates[:, c * TILES + t, :], m.ident[:, :])
                        last.then_inc(s["f0_gates_turned"], 1)

            def back(piece, p):
                if piece == "spread":
                    pe.wait_ge(s["f0_gates_T"], 4)
                    wait(pe, s["f0_dec_sum"], p * 2)
                    for c in range(2):
                        pe.wait_ge(s["f0_mixed"], p * 2 + c + 1)
                        for j in range(2):
                            nc.tensor.matmul(WIDE_BACK[c][j][:, :], w.c2s[:, j * P:(j + 1) * P], mixed[p][:, COLS[c]],
                                             start=True, stop=True).then_inc(s["f0_enc2"], 1)
                if piece == "decode":
                    for c in range(2):
                        pe.wait_ge(s["f0_spikes2"], p * 4 + 2 * c + 2)
                        for t in range(TILES):
                            tok = c * BANK + t * P
                            for j in range(2):
                                last = nc.tensor.matmul(turned_t[c][:, t, :], spikes[:, j, tok:tok + P],
                                                        w.dec[:, j, :], start=j == 0, stop=j == 1)
                        last.then_inc(s["f0_dec"], 1)
                if piece == "turn_x_again":
                    pe.wait_ge(s["f0_dec_sum"], 4)
                    wait(pe, s["f0_kv_read"], p * 4)
                    for c in range(2):
                        pe.wait_ge(s["f0_xn2"], p * 2 + c + 1)
                        turn(turned_t[c], lambda t: xn[:, c * TILES + t, :]).then_inc(s["f0_x2_turned"], 1)
                if piece == "attend":
                    for c in range(2):
                        pe.wait_ge(s["f0_xT2"], p * 2 + c + 1)
                        nc.tensor.matmul(narrow[c][:, :], qkv_T[:, 0, :], xT2[:, COLS[c]], start=True, stop=True
                                         ).then_inc(s["f0_q"], 1)
                    for c in range(2):
                        if c == 1:
                            pe.wait_ge(s["f0_qT"], p * 2 + 2)
                        for t in range(TILES):
                            tok = c * BANK + t * P
                            last = nc.tensor.matmul(WIDE_BACK[c][t // 2][:, (t % 2) * 256:(t % 2) * 256 + 256],
                                                    xT2[:, tok:tok + P],
                                                    qkv_T[:, 1:3, :].rearrange("p c d -> p (c d)"),
                                                    start=True, stop=True)
                            if t % 2:
                                last.then_inc(s["f0_kv"], 1)

            def expert_hidden(p, k):
                c = k % 2
                for j in range(2):
                    e = k // 2 * 2 + j
                    wait(pe, s["f0_hidden"], (p * STEPS0 + k - 1) * 2 + j + 1)
                    nc.tensor.matmul(hid[j][:, :], e1_hi[:, e, :], cont[p][:, COLS[c]], start=True, stop=False)
                    nc.tensor.matmul(hid[j][:, :], e1_lo[:, e, :], cont[p][:, COLS[c]], start=False, stop=True
                                     ).then_inc(s["f0_hidden_sum"], 1)

            def expert_out(p, k):
                c = k % 2
                pe.wait_ge(s["f0_hidden"], (p * STEPS0 + k) * 2 + 2)
                wait(pe, s["f0_part"], p * STEPS0 + k - 1)
                for j in range(2):
                    last = nc.tensor.matmul(eout[c][HALF[j], :], w.e2[:, k // 2 * 2 + j, :], hidden[c][j][:, :],
                                            start=True, stop=True)
                last.then_inc(s["f0_eout"], 1)

            def experts(p, k):
                if k == 0:
                    expert_hidden(p, 0)
                if k + 1 < STEPS0:
                    expert_hidden(p, k + 1)
                expert_out(p, k)

            pe.wait_ge(s["f0_loaded"], 16 * FFN0_LOADS)
            for c in range(3):
                last = nc.tensor.transpose(hid[0][:, c * P:(c + 1) * P], w.qkv_raw[:, c, :], m.ident[:, :])
            last.then_inc(s["qkv_turned"], 1)
            pe.wait_ge(s["qkv_T_ready"], 1)
            for piece, p, *k in FFN0_ORDER:
                if piece == "experts":
                    experts(p, *k)
                front(piece, p)
                back(piece, p)

        @block.scalar
        def _(act):
            norms = Norms(nc, None, m.carrier, s["f0_var"], s["f0_root"], m.eps, stats, mv, rstd, 0)

            def front(piece, p):
                if piece in ("norm_y", "norm_x"):
                    norms.root(act)
                if piece == "turn_x":
                    for c in range(2):
                        act.wait_ge(s["f0_x_turned"], p * 2 + c + 1)
                        nc.scalar.copy(xT_hi[:, COLS[c]], turned[c][:, :]).then_inc(s["f0_xT_hi"], 1)
                if piece == "encode":
                    for c in range(2):
                        for j in range(2):
                            act.wait_ge(s["f0_enc"], p * 4 + 2 * c + j + 1)
                            nc.scalar.activation(spikes[:, j, COLS[c]], WIDE_FRONT[c][j][:, :], ACT.Sigmoid,
                                                 bias=w.enc_b[:, j:j + 1]).then_inc(s["f0_spikes"], 1)
                if piece == "condense":
                    for c in range(2):
                        act.wait_ge(s["f0_cont"], p * 2 + c + 1)
                        nc.scalar.activation(cont[p][0:M0, COLS[c]], narrow[c][0:M0, :], ACT.Identity,
                                             bias=w.s2c_b[:, 0:1]).then_inc(s["f0_cont_hi"], 1)
                if piece == "route":
                    for c in range(2):
                        act.wait_ge(s["f0_router"], p * 2 + c + 1)
                        nc.scalar.activation(router[:, COLS[c]], narrow[c][0:M0, :], ACT.Tanh, bias=w.r1_b[:, 0:1]
                                             ).then_inc(s["f0_tanh"], 1)
                if piece == "gate":
                    weigh_two(nc, act, g[p], s["f0_gap"], s["f0_weights"], p + 1)
                if piece == "turn_gates":
                    wait(act, s["f0_gates_stored"], p * 16)
                    for c in range(2):
                        act.wait_ge(s["f0_gates_turned"], p * 2 + c + 1)
                        nc.scalar.copy(gates_T[:, COLS[c]], turned[c][0:EXPERTS, :]).then_inc(s["f0_gates_T"], 1)

            def back(piece, p):
                if piece == "spread":
                    for c in range(2):
                        for j in range(2):
                            act.wait_ge(s["f0_enc2"], p * 4 + 2 * c + j + 1)
                            nc.scalar.activation(spikes[:, j, COLS[c]], WIDE_BACK[c][j][:, :], ACT.Sigmoid,
                                                 bias=w.c2s_b[:, j:j + 1]).then_inc(s["f0_spikes2"], 1)
                if piece == "decode":
                    for c in range(2):
                        act.wait_ge(s["f0_dec_sum"], p * 2 + c + 1)
                        nc.scalar.activation(decoded[p][:, ROWS[c], :], decoded[p][:, ROWS[c], :], ACT.Sigmoid
                                             ).then_inc(s["f0_decoded"], 1)
                if piece in ("norm", "norm_again", "norm_x_again"):
                    norms.root(act)
                if piece == "turn_x_again":
                    for c in range(2):
                        act.wait_ge(s["f0_x2_turned"], p * 2 + c + 1)
                        nc.scalar.copy(xT2[:, COLS[c]], turned[c][:, :]).then_inc(s["f0_xT2"], 1)
                if piece == "attend":
                    for c in range(2):
                        act.wait_ge(s["f0_q"], p * 2 + c + 1)
                        tok = p * PAIR + c * BANK
                        nc.scalar.activation(m.qT[:, tok:tok + BANK], narrow[c][:, :], ACT.Identity,
                                             bias=w.q_b[:, 0:1]).then_inc(s["f0_qT"], 1)

            def relu(p, k):
                c = k % 2
                for j in range(2):
                    e = k // 2 * 2 + j
                    act.wait_ge(s["f0_hidden_sum"], (p * STEPS0 + k) * 2 + j + 1)
                    wait(act, s["f0_eout"], p * STEPS0 + k - 1)
                    nc.scalar.activation(hidden[c][j][:, :], hid[j][:, :], ACT.Relu, bias=w.e1_b[:, e:e + 1]
                                         ).then_inc(s["f0_hidden"], 1)

            def experts(p, k):
                if k == 0:
                    relu(p, 0)
                if k + 1 < STEPS0:
                    relu(p, k + 1)

            act.wait_ge(s["qkv_turned"], 1)
            nc.scalar.copy(qkv_T[:, :, :], hid[0][:, 0:3 * P].rearrange("p (c d) -> p c d", c=3)
                           ).then_inc(s["qkv_T_ready"], 1)
            nc.scalar.copy(enc_hi[:, :], w.enc_raw[:, :])
            nc.scalar.copy(r1_hi[:, :], w.r1_raw[:, :])
            nc.scalar.copy(e1_hi[:, :, :], w.e1_raw[:, :, :]).then_inc(s["f0_w_hi"], 1)
            for piece, p, *k in FFN0_ORDER:
                if piece == "experts":
                    experts(p, *k)
                front(piece, p)
                back(piece, p)

        @block.vector
        def _(dve):
            ch = Chain(dve, s["f0_dve"])
            norms = Norms(nc, ch, m.carrier, s["f0_var"], s["f0_root"], m.eps, stats, mv, rstd, 0)

            def x_of(p):
                return m.x[:, p * 2 * TILES:(p + 1) * 2 * TILES, :]

            def over_rows(row):
                return row[:, :].unsqueeze(1).broadcast_to([P, 2 * TILES, P])

            def front(piece, p):
                if piece == "norm_y":
                    dve.wait_ge(s["f0_y_turned"], p * 2 + 2)
                    ch.link(norms.norm([tile for c in range(2) for tile in tiles_of(TURNED_Y[p][c])], post)[-1])
                if piece == "norm_x":
                    ch.link(nc.vector.tensor_tensor(x_of(p), x_of(p), post[:, :, :], ALU.add))
                    for last in norms.norm(tiles_of(x_of(p)), xn):
                        last.then_inc(s["f0_xn"], 1)
                if piece == "turn_x":
                    for c in range(2):
                        dve.wait_ge(s["f0_xT_hi"], p * 2 + c + 1)
                        nc.vector.tensor_tensor(xT_lo[:, COLS[c]], turned[c][:, :], xT_hi[:, COLS[c]].bitcast(F32),
                                                ALU.subtract).then_inc(s["f0_xT_lo"], 1)
                if piece == "condense":
                    for c in range(2):
                        dve.wait_ge(s["f0_cont_hi"], p * 2 + c + 1)
                        nc.vector.scalar_tensor_tensor(out=cont[p][M0:P, COLS[c]], in0=narrow[c][0:M0, :],
                                                       scalar=w.s2c_b[:, 0:1],
                                                       in1=cont[p][0:M0, COLS[c]].bitcast(F32),
                                                       op0=ALU.add, op1=ALU.subtract).then_inc(s["f0_cont_lo"], 1)
                if piece == "gate":
                    dve.wait_ge(s["f0_logits"], p + 1)
                    pick_two(nc, ch, g[p], logits, w.r2_b, m.rank, s["f0_gap"], s["f0_weights"], p + 1
                             ).then_inc(s["f0_gates"], 1)
                    dve.wait_ge(s["f0_gates"], p + 1)

            def back(piece, p):
                if piece == "decode":
                    for c in range(2):
                        dve.wait_ge(s["f0_dec"], p * 2 + c + 1)
                        nc.vector.tensor_tensor(decoded[p][:, ROWS[c], :], turned_t[c],
                                                w.dec_b[:, :].unsqueeze(1).broadcast_to([P, TILES, P]), ALU.add
                                                ).then_inc(s["f0_dec_sum"], 1)
                if piece == "norm":
                    dve.wait_ge(s["f0_decoded"], p * 2 + 2)
                    ch.link(norms.norm(tiles_of(decoded[p]), post)[-1])
                if piece == "affine":
                    ch.link(nc.vector.tensor_tensor(post[:, :, :], post[:, :, :], over_rows(w.ln_g), ALU.mult))
                    ch.link(nc.vector.tensor_tensor(post[:, :, :], post[:, :, :], over_rows(w.ln_b), ALU.add))
                if piece == "norm_again":
                    ch.link(norms.norm(tiles_of(post), decoded[p])[-1])
                if piece == "norm_x_again":
                    ch.link(nc.vector.tensor_tensor(x_of(p), x_of(p), decoded[p][:, :, :], ALU.add))
                    for last in norms.norm(tiles_of(x_of(p)), xn):
                        last.then_inc(s["f0_xn2"], 1)
                if piece == "attend":
                    for c in range(2):
                        for j in range(2):
                            dve.wait_ge(s["f0_kv"], p * 4 + 2 * c + j + 1)
                            tile = p * 2 * TILES + 4 * c + 2 * j
                            nc.vector.tensor_tensor(m.kv[:, tile:tile + 2, :],
                                                    WIDE_BACK[c][j][:, :].rearrange("p (t d) -> p t d", t=2),
                                                    w.kv_b[:, :].unsqueeze(1).broadcast_to([P, 2, 2 * P]), ALU.add
                                                    ).then_inc(s["f0_kv_read"], 1)

            def weigh(p, k):
                c, pair = k % 2, k // 2
                dve.wait_ge(s["f0_eout"], p * STEPS0 + k + 1)
                dve.wait_ge(s["f0_rows"][p * 4 + pair], 32)
                to = part[c][:, :] if pair else mixed[p][:, COLS[c]]
                nc.vector.scalar_tensor_tensor(out=to, in0=eout[c][:, :], scalar=w.e2_b[:, pair:pair + 1],
                                               in1=gate_rows[p][:, pair, COLS[c]], op0=ALU.add, op1=ALU.mult
                                               ).then_inc(s["f0_part"], 1)
                if pair:
                    dve.wait_ge(s["f0_part"], p * STEPS0 + k + 1)
                    ins = nc.vector.tensor_tensor(mixed[p][:, COLS[c]], mixed[p][:, COLS[c]], part[c][:, :], ALU.add)
                    if pair < EXPERTS // 2 - 1:
                        ch.link(ins)
                    else:
                        ins.then_inc(s["f0_mixed"], 1)

            for e in range(EXPERTS):
                last = nc.vector.memset(m.rank[:, e:e + 1], float(EXPERTS - e))
            last.then_inc(s["rank_ready"], 1)
            dve.wait_ge(s["rank_ready"], 1)
            dve.wait_ge(s["f0_loaded"], 16 * FFN0_LOADS)
            for piece, p, *k in FFN0_ORDER:
                if piece == "experts":
                    weigh(p, *k)
                front(piece, p)
                back(piece, p)


DH1 = 16
HEADS1 = 8


def linear_attention(nc, m, s):
    with ExitStack() as ctx:
        w_raw = m.ffn1.wo
        w_ordered = ctx.enter_context(nc.sbuf_tensor("wo_ordered", [P, P], F32))
        w_T = ctx.enter_context(nc.sbuf_tensor("wo_T", [P, P], F32))
        same_head = ctx.enter_context(nc.sbuf_tensor("same_head", [P, HEADS1], F32))
        vk = ctx.enter_context(nc.sbuf_tensor("vk", [P, 2, P], F32))
        turned = ctx.enter_context(nc.psum_tensor("wo_turned", [P, P], F32))
        vk_sum = [ctx.enter_context(nc.psum_tensor(f"vk_sum{b}", [P, P], F32)) for b in range(2)]
        mix = [ctx.enter_context(nc.psum_tensor(f"mix{b}", [P, P], F32)) for b in range(2)]
        block = ctx.enter_context(nc.Block())

        @block.tensor
        def _(pe):
            for b in range(2):
                for t in range(8):
                    kv = m.kv[:, b * 8 + t, :]
                    last = nc.tensor.matmul(vk_sum[b][:, :], kv[:, P:2 * P], kv[:, 0:P], start=t == 0, stop=t == 7)
                last.then_inc(s["vk_summed"], 1)
            pe.wait_ge(s["wo_ordered"], 1)
            nc.tensor.transpose(turned[:, :], w_ordered[:, :], m.ident[:, :]).then_inc(s["wo_turned"], 1)
            pe.wait_ge(s["wo_ready"], 1)
            for b in range(2):
                pe.wait_ge(s["vk_masked"], b + 1)
                nc.tensor.matmul(mix[b][:, :], vk[:, b, :], w_T[:, :], start=True, stop=True).then_inc(s["mixed1"], 1)

        @block.scalar
        def _(act):
            act.wait_ge(s["wo_turned"], 1)
            nc.scalar.copy(w_T[:, :], turned[:, :]).then_inc(s["wo_ready"], 1)
            act.wait_ge(s["mixed1"], 2)
            for c in range(2):
                nc.scalar.copy(m.mix[:, 2 + c, :], mix[1][:, :])

        @block.vector
        def _(dve):
            dve.wait_ge(s["f1_loaded"], 16 * FFN1_LOADS)
            nc.vector.tensor_copy(w_ordered[:, :].rearrange("p (d h) -> p d h", h=HEADS1),
                                  w_raw[:, :].rearrange("p (h d) -> p d h", h=HEADS1)).then_inc(s["wo_ordered"], 1)
            nc.vector.tensor_reduce(same_head[:, :], m.ident[:, :].rearrange("p (d h) -> p h d", h=HEADS1), X, ALU.add
                                    ).then_inc(s["same_head"], 1)
            dve.wait_ge(s["same_head"], 1)
            for b in range(2):
                dve.wait_ge(s["vk_summed"], b + 1)
                nc.vector.tensor_tensor(vk[:, b, :].rearrange("p (d h) -> p d h", h=HEADS1),
                                        vk_sum[b][:, :].rearrange("p (d h) -> p d h", h=HEADS1),
                                        same_head[:, :].unsqueeze(1).broadcast_to([P, DH1, HEADS1]), ALU.mult
                                        ).then_inc(s["vk_masked"], 1)
            dve.wait_ge(s["mixed1"], 1)
            for c in range(2):
                nc.vector.tensor_copy(m.mix[:, c, :], mix[0][:, :])


H1 = 512
HC = H1 // P
NORMS1 = 2
FRONT_LINKS = NORMS1 * 2 + 3
EXPERT_LINKS = EXPERTS - 1
TAIL_LINKS = 3


FFN1_LOADS = 5


def ffn1_weights(m, sb):
    w = m.ffn1 = Buffers()
    w.b1, w.b2 = sb("b1", [P, EXPERTS, HC]), sb("b2", [EXPERTS, P])
    w.wr = sb("wr", [P, EXPERTS])
    w.bo, w.wo = m.b_v, m.w_v


def load_ffn1_weights(sp, m, s):
    w = m.ffn1
    for dst, src in ((w.wo[:, :], m.inputs["w_o1"]), (w.bo[:, :], m.inputs["b_o1"].partition_broadcast(P)),
                     (w.wr[:, :], m.inputs["Wr"]), (w.b2[:, :], m.inputs["b2"]),
                     (w.b1[:, :, :], m.inputs["b1"].rearrange("e (c p) -> p e c", p=P))):
        sp.dma_start(dst, src).then_inc(s["f1_loaded"], 16)


def ffn1(nc, m, s):
    with ExitStack() as ctx:
        def sb(name, shape, dt=F32):
            return ctx.enter_context(nc.sbuf_tensor(name, shape, dt))

        w1_hi, w1_lo = sb("w1_hi", [P, EXPERTS, H1], F32R), sb("w1_lo", [P, EXPERTS, H1], F32R)
        b1, b2, wr, bo = m.ffn1.b1, m.ffn1.b2, m.ffn1.wr, m.ffn1.bo
        qT = sb("qT_chunk", [P, BANK])
        post = sb("post1", [P, TILES, P])
        xn = sb("xn1", [P, TILES, P])
        xT = sb("xT1", [P, BANK])
        hidden = [sb(f"hidden1_{b}", [P, BANK]) for b in range(HC)]
        part = sb("part1", [P, TILES, P])
        mixed = sb("mixed1", [P, TILES, P])
        final = sb("final", [P, TILES, P])
        gates_T = sb("gates_T1", [EXPERTS, BANK])
        stats, mv, rstd = sb("stats1", [P, TILES, 6]), sb("mv1", [P, TILES, 2]), sb("rstd1", [P, TILES])
        g = gating_buffers(sb, "g1", TILES)

        def pb(name, shape):
            return ctx.enter_context(nc.psum_tensor(name, shape, F32))

        turned = pb("turned1", [P, BANK])
        small = pb("small1", [P, BANK])
        hid = [pb(f"hid1_{b}", [P, BANK]) for b in range(4)]
        eout = [pb(f"eout1_{b}", [P, BANK]) for b in range(2)]
        turned_t = turned[:, :].rearrange("p (t d) -> p t d", t=TILES)
        eout_t = [e[:, :].rearrange("p (t d) -> p t d", t=TILES) for e in eout]
        logits = small[:, 0:TILES * EXPERTS].rearrange("p (t e) -> p t e", t=TILES)
        CHUNKS = 4
        STEPS = EXPERTS * HC
        block = ctx.enter_context(nc.Block())

        def chunk_cols(a, i):
            return a[:, bass.ts(i, BANK)]

        @block.sync
        def _(sp):
            with sp.Fori(0, CHUNKS) as i:
                sp.wait_ge(s["f1_x_out"], i + 1)
                sp.dma_start(m.out_tiles[:, bass.ts(i, TILES), :], m.x[:, bass.ts(i, TILES), :]).then_inc(s["stored"], 16)
            sp.wait_ge(s["stored"], 16 * CHUNKS)

        @block.gpsimd
        def _(pool):
            for e in range(EXPERTS):
                pool.wait_ge(s["w1_hi_ready"], e + 1)
                nc.gpsimd.tensor_tensor(w1_lo[:, e, :], m.w1_raw[:, e, :], w1_hi[:, e, :].bitcast(F32), ALU.subtract
                                        ).then_inc(s["w1_split"], 1)

        @block.tensor
        def _(pe):
            def attended(i):
                first = isinstance(i, int) and i == 0
                if not first:
                    pe.wait_ge(s["f1_qT"], i)
                q = m.qT if first else qT
                for t in range(TILES):
                    last = nc.tensor.matmul(turned_t[:, t, :], q[:, t * P:(t + 1) * P],
                                            m.mix[:, bass.ds(i, 1), :].rearrange("p a d -> p (a d)"),
                                            start=True, stop=True)
                last.then_inc(s["f1_attended"], 1)

            def turn_x(i):
                pe.wait_ge(s["f1_xn"], i + 1)
                for t in range(TILES):
                    last = nc.tensor.transpose(turned_t[:, t, :], xn[:, t, :], m.ident[:, :])
                last.then_inc(s["f1_x_turned"], 1)

            def route(i):
                pe.wait_ge(s["f1_xT"], i + 1)
                for t in range(TILES):
                    last = nc.tensor.matmul(logits[:, t, :], xT[:, t * P:(t + 1) * P], wr[:, :], start=True, stop=True)
                last.then_inc(s["f1_logits"], 1)

            def turn_gates(i):
                pe.wait_ge(s["f1_gates"], i + 1)
                for t in range(TILES):
                    last = nc.tensor.transpose(small[0:EXPERTS, t * P:(t + 1) * P], g.gates[:, t, :], m.ident[:, :])
                last.then_inc(s["f1_gates_turned"], 1)

            def bias(i):
                pe.wait_ge(s["f1_gates_T"], i + 1)
                for t in range(TILES):
                    last = nc.tensor.matmul(turned_t[:, t, :], gates_T[:, t * P:(t + 1) * P], b2[:, :],
                                            start=True, stop=True)
                last.then_inc(s["f1_bias"], 1)

            def expert_hidden(i, k):
                e, c = k // HC, k % HC
                if k >= 4 or not (isinstance(i, int) and i == 0):
                    pe.wait_ge(s["f1_hidden"], i * STEPS + (k - 3))
                cols = slice(c * P, (c + 1) * P)
                nc.tensor.matmul(hid[c][:, :], w1_hi[:, e, cols], chunk_cols(m.xT_hi, i), start=True, stop=False)
                nc.tensor.matmul(hid[c][:, :], w1_hi[:, e, cols], chunk_cols(m.xT_lo, i), start=False, stop=False)
                nc.tensor.matmul(hid[c][:, :], w1_lo[:, e, cols], chunk_cols(m.xT_hi, i), start=False, stop=True
                                 ).then_inc(s["f1_hidden_sum"], 1)

            def expert_out(i, k):
                e, c = k // HC, k % HC
                pe.wait_ge(s["f1_hidden"], i * STEPS + (k + 1))
                if c == 0 and (e >= 2 or not (isinstance(i, int) and i == 0)):
                    pe.wait_ge(s["f1_part"], i * EXPERTS + (e - 1))
                for t in range(TILES):
                    last = nc.tensor.matmul(eout_t[e % 2][:, t, :], hidden[c][:, t * P:(t + 1) * P],
                                            m.w2[:, e, c, :], start=c == 0 and t == 0, stop=c == HC - 1,
                                            skip_group_check=True)
                last.then_inc(s["f1_eout"], 1)

            def experts(i, last=False):
                pe.wait_ge(s["f1_xT_lo"], i + 1)
                for k in range(STEPS):
                    e, c = k // HC, k % HC
                    if isinstance(i, int) and i == 0 and c == 0:
                        pe.wait_ge(s["w1_split"], e + 1)
                    if isinstance(i, int) and (i, k) == (0, 1):
                        route(0)
                    if not last:
                        if (e, c) == (3, 2):
                            pe.wait_ge(s["f1_biased"], i + 1)
                            attended(i + 1)
                        if (e, c) == (6, 0):
                            turn_x(i + 1)
                        if (e, c) == (7, 0):
                            route(i + 1)
                    expert_hidden(i, k)
                    if k == 9:
                        turn_gates(i)
                    if k == 11:
                        bias(i)
                    if k >= 2:
                        expert_out(i, k - 2)
                for k in (STEPS - 2, STEPS - 1):
                    expert_out(i, k)

            pe.wait_ge(s["f1_loaded"], 16 * FFN1_LOADS)
            attended(0)
            turn_x(0)
            experts(0)
            with pe.Fori(1, CHUNKS - 1) as i:
                experts(i)
            experts(CHUNKS - 1, last=True)

        @block.scalar
        def _(act):
            def norms_of(i):
                return Norms(nc, None, m.carrier, s["f1_var"], s["f1_root"], m.eps, stats, mv, rstd, i)

            def take_q(i):
                act.wait_ge(s["f1_attended"], i)
                nc.scalar.copy(qT[:, :], chunk_cols(m.qT, i)).then_inc(s["f1_qT"], 1)

            def take_x(i):
                act.wait_ge(s["f1_x_turned"], i + 1)
                nc.scalar.copy(chunk_cols(m.xT_hi, i), turned[:, :]).then_inc(s["f1_xT_hi"], 1)

            def take_gates(i):
                act.wait_ge(s["f1_gates_turned"], i + 1)
                nc.scalar.copy(gates_T[:, :], small[0:EXPERTS, :]).then_inc(s["f1_gates_T"], 1)

            def experts(i, first=False, last=False):
                norms = norms_of(NORMS1 if first else i * (NORMS1 + 1) + (NORMS1 - 1))
                for k in range(STEPS):
                    e, c = k // HC, k % HC
                    act.wait_ge(s["f1_hidden_sum"], i * STEPS + (k + 1))
                    if k >= HC or not first:
                        act.wait_ge(s["f1_eout"], i * STEPS + (k - HC + 1))
                    nc.scalar.activation(hidden[c][:, :], hid[c][:, :], ACT.Gelu, bias=b1[:, e, c:c + 1]
                                         ).then_inc(s["f1_hidden"], 1)
                    if k == 2 and not first:
                        norms.root(act)
                    if k == 6:
                        weigh_two(nc, act, g, s["f1_gap"], s["f1_weights"], i + 1)
                    if k == 9:
                        take_gates(i)
                    if last:
                        continue
                    if (e, c) == (2, 3):
                        take_q(i + 1)
                    if (e, c) in ((4, 0), (5, 0)):
                        norms.root(act)
                    if (e, c) == (6, 0):
                        take_x(i + 1)

            norms = norms_of(0)
            act.wait_ge(s["w1_loaded"], 32 * EXPERTS)
            for e in range(EXPERTS):
                if e == 6:
                    norms.root(act)
                nc.scalar.copy(w1_hi[:, e, :], m.w1_raw[:, e, :]).then_inc(s["w1_hi_ready"], 1)
            norms.root(act)
            take_x(0)
            act.wait_ge(s["f1_loaded"], 16 * FFN1_LOADS)
            experts(0, first=True)
            with act.Fori(1, CHUNKS - 1) as i:
                experts(i)
            experts(CHUNKS - 1, last=True)
            norms_of(CHUNKS * (NORMS1 + 1) - 1).root(act)

        @block.vector
        def _(dve):
            def norms_of(ch, before):
                return Norms(nc, ch, m.carrier, s["f1_var"], s["f1_root"], m.eps, stats, mv, rstd, before)

            def x_of(i):
                return m.x[:, bass.ts(i, TILES), :]

            def x_tiles(i):
                return [m.x[:, bass.ds(i * TILES + t, 1), :].rearrange("p a d -> p (a d)") for t in range(TILES)]

            def add_attention(i, ch, norms):
                dve.wait_ge(s["f1_attended"], i + 1)
                ch.link(nc.vector.tensor_tensor(post[:, :, :], turned_t,
                                                bo[:, :].unsqueeze(1).broadcast_to([P, TILES, P]), ALU.add))
                ch.link(norms.norm(tiles_of(post), xn)[-1])
                ch.link(nc.vector.tensor_tensor(x_of(i), x_of(i), xn[:, :, :], ALU.add))

            def normalise(i, norms):
                norms.norm(x_tiles(i), xn)[-1].then_inc(s["f1_xn"], 1)

            def split_x(i):
                dve.wait_ge(s["f1_x_turned"], i + 1)
                dve.wait_ge(s["f1_xT_hi"], i + 1)
                nc.vector.tensor_tensor(chunk_cols(m.xT_lo, i), turned[:, :], chunk_cols(m.xT_hi, i).bitcast(F32),
                                        ALU.subtract).then_inc(s["f1_xT_lo"], 1)
                nc.vector.tensor_copy(xT[:, :], turned[:, :]).then_inc(s["f1_xT"], 1)

            def find_gates(i):
                ch = Chain(dve, s["f1_gating"], i * GATE_LINKS)
                dve.wait_ge(s["f1_logits"], i + 1)
                pick_two(nc, ch, g, logits, None, m.rank, s["f1_gap"], s["f1_weights"], i + 1).then_inc(s["f1_gates"], 1)
                dve.wait_ge(s["f1_gates"], i + 1)
                assert ch.n == GATE_LINKS, (ch.n, GATE_LINKS)

            def tail(i, before):
                ch = Chain(dve, s["f1_tail"], i * TAIL_LINKS)
                norms = norms_of(ch, before)
                ch.link(norms.norm(tiles_of(mixed), final)[-1])
                nc.vector.tensor_tensor(x_of(i), x_of(i), final[:, :, :], ALU.add).then_inc(s["f1_x_out"], 1)
                assert ch.n == TAIL_LINKS, (ch.n, TAIL_LINKS)

            def experts(i, first=False, last=False):
                norms_before = NORMS1 if first else i * (NORMS1 + 1) + (NORMS1 - 1)
                if not first:
                    tail(i - 1, norms_before)
                    norms_before = norms_before + 1
                find_gates(i)
                ch = Chain(dve, s["f1_dve"], i * EXPERT_LINKS)
                front = None if last else Chain(dve, s["f1_front"], (i + 1) * FRONT_LINKS)
                norms = norms_of(front, norms_before)
                for e in range(EXPERTS):
                    gate = g.gates[:, :, e:e + 1].broadcast_to([P, TILES, P])
                    dve.wait_ge(s["f1_eout"], i * STEPS + (e + 1) * HC)
                    nc.vector.tensor_tensor(part[:, :, :], eout_t[e % 2], gate, ALU.mult).then_inc(s["f1_part"], 1)
                    dve.wait_ge(s["f1_part"], i * EXPERTS + (e + 1))
                    if e == 0:
                        dve.wait_ge(s["f1_bias"], i + 1)
                        nc.vector.tensor_tensor(mixed[:, :, :], turned_t, part[:, :, :], ALU.add
                                                ).then_inc(s["f1_biased"], 1)
                        dve.wait_ge(s["f1_biased"], i + 1)
                    else:
                        ch.link(nc.vector.tensor_tensor(mixed[:, :, :], mixed[:, :, :], part[:, :, :], ALU.add))
                    if last:
                        continue
                    if e == 2:
                        add_attention(i + 1, front, norms)
                    if e == 3:
                        normalise(i + 1, norms)
                        assert front.n == FRONT_LINKS, (front.n, FRONT_LINKS)
                    if e == 5:
                        split_x(i + 1)
                assert ch.n == EXPERT_LINKS, (ch.n, EXPERT_LINKS)

            dve.wait_ge(s["f1_loaded"], 16 * FFN1_LOADS)
            front = Chain(dve, s["f1_front"])
            norms = norms_of(front, 0)
            add_attention(0, front, norms)
            normalise(0, norms)
            split_x(0)
            experts(0, first=True)
            with dve.Fori(1, CHUNKS - 1) as i:
                experts(i)
            experts(CHUNKS - 1, last=True)
            tail(CHUNKS - 1, CHUNKS * (NORMS1 + 1) - 1)


INPUTS = ["L0_attn_data", "L0_attn_W_qkv", "L0_attn_b_qkv", "L0_attn_W_out", "L0_attn_b_out",
          "L0_ffn_enc_W", "L0_ffn_enc_b", "L0_ffn_s2c_W", "L0_ffn_s2c_b", "L0_ffn_rW1", "L0_ffn_rb1", "L0_ffn_rW2",
          "L0_ffn_rb2", "L0_ffn_We1", "L0_ffn_be1", "L0_ffn_We2", "L0_ffn_be2", "L0_ffn_c2s_W", "L0_ffn_c2s_b",
          "L0_ffn_dec_W", "L0_ffn_dec_b", "L0_ffn_ln_g", "L0_ffn_ln_b",
          "L1_attn_w_qkv", "L1_attn_b_qkv", "L1_attn_w_o", "L1_attn_b_o",
          "L1_ffn_Wr", "L1_ffn_W1", "L1_ffn_b1", "L1_ffn_W2", "L1_ffn_b2"]
SHORT = ["data", "W_qkv", "b_qkv", "W_out", "b_out_row", "enc_W", "enc_b", "s2c_W", "s2c_b", "rW1", "rb1", "rW2", "rb2",
         "We1", "be1", "We2", "be2", "c2s_W", "c2s_b", "dec_W", "dec_b", "ln_g", "ln_b",
         "w_qkv1", "b_qkv1", "w_o1", "b_o1", "Wr", "W1", "b1", "W2", "b2"]


SEMAPHORES = """
bias_loaded cleared em_dve em_hi em_sqrt em_turned em_var em_xn eps_ready f0_cont f0_cont_hi f0_cont_lo f0_dec
f0_dec_sum f0_decoded f0_dve f0_enc f0_enc2 f0_eout f0_gap f0_gates f0_gates_T f0_gates_stored f0_gates_turned
f0_hidden f0_hidden_sum f0_kv f0_kv_read f0_loaded f0_logits f0_mixed f0_part f0_q f0_qT f0_root f0_router
f0_spikes f0_spikes2 f0_split f0_tanh f0_var f0_w_hi f0_weights f0_x2_turned f0_xT2 f0_xT_hi f0_xT_lo
f0_x_turned f0_xn f0_xn2 f0_y_turned f1_attended f1_bias f1_biased f1_dve f1_eout f1_front f1_gap f1_gates
f1_gates_T f1_gates_turned f1_gating f1_hidden f1_hidden_sum f1_loaded f1_logits f1_part f1_qT f1_root f1_tail
f1_var f1_weights f1_xT f1_xT_hi f1_xT_lo f1_x_out f1_x_turned f1_xn filled ident0 ident_ready inv_stored
inv_sum_ready inverted leading_copied leading_ready mixed1 neg_max_ready normalised pair_loaded qkv_T_ready
qkv_turned rank_ready raw_out_ready same_head stored sum_cols_ready vk_masked vk_summed w1_hi_ready w1_loaded
w1_split w_hi_ready w_out_loaded w_split weighed wide_free wide_full wo_ordered wo_ready wo_turned yT_clear
""".split()
SEMAPHORE_LISTS = {"x_loaded": 4, "shared_free": 2, "shared_full": 2,
                   "exp_done": 2, "scores_ready": 2, "keys_added": 2, "f0_rows": 8}


def build(nc, inputs, out):
    m = Buffers()
    m.inputs = inputs
    m.out_tiles = out.rearrange("n (t p) d -> p (n t) d", p=P)
    with ExitStack() as ctx:
        def sb(name, shape, dt=F32):
            return ctx.enter_context(nc.sbuf_tensor(name, shape, dt))

        ctx.enter_context(nc.allow_non_contiguous_dma(reason="biases as columns"))
        s = {name: ctx.enter_context(nc.semaphore(name)) for name in SEMAPHORES}
        for name, count in SEMAPHORE_LISTS.items():
            s[name] = [ctx.enter_context(nc.semaphore(f"{name}{i}")) for i in range(count)]
        m.x = sb("x", [P, 16, P])
        m.xT = sb("xT", [P, 2048])
        m.xT_hi = sb("xT_hi", [P, 2048], F32R)
        m.xT_lo = sb("xT_lo", [P, 2048], F32R)
        m.yT = sb("yT", [P, 2048])
        m.qT = m.xT
        m.ident, m.ident_bf = sb("ident", [P, P]), sb("ident_bf", [P, P], BF16)
        m.ones, m.eps, m.rank = sb("ones", [P, P]), sb("eps", [P, 1]), sb("rank", [P, EXPERTS])
        m.b_out, m.carrier = sb("b_out", [P, 1]), sb("carrier", [P, 1])
        m.w_raw, m.b_qk = sb("w_raw", [P, 2, P]), sb("b_qk", [P, 2])
        m.w_v, m.b_v = sb("w_v", [P, P]), sb("b_v", [P, P])
        ffn0_weights(nc, m, sb)
        embed(nc, m, s)
        attention(nc, m, s)
        m.kv = sb("kv", [P, 16, 2 * P])
        m.mix = sb("mix", [P, 4, P])
        m.w1_raw = sb("w1_raw", [P, EXPERTS, H1])
        m.w2 = sb("w2", [P, EXPERTS, HC, P])
        ffn1_weights(m, sb)
        ffn0(nc, m, s)
        linear_attention(nc, m, s)
        ffn1(nc, m, s)


def kernel(**inputs):
    import numpy as _np
    import concourse.bacc as _bacc
    from concourse.bass_utils import run_bass_kernel_spmd as _run

    nc = _bacc.Bacc("TRN2", target_bir_lowering=False, num_devices=1)
    arrays, args = {}, {}
    for name, short in zip(INPUTS, SHORT):
        a = _np.ascontiguousarray(inputs[name])
        arrays[f"in_{name}_dram"] = a
        args[short] = nc.dram_tensor(f"in_{name}_dram", a.shape, mybir.dt.from_np(a.dtype), kind="ExternalInput").ap()
    out = nc.dram_tensor("out_dram", (2, 1024, P), F32, kind="ExternalOutput").ap()
    build(nc, args, out)
    r = _run(nc, [arrays], core_ids=[0])
    return r.results[0]["out_dram"]
```
